# Optimizing a Trainium2 kernel written in Bass

```python
import numpy as np
import jax
import jax.numpy as jnp

def _softmax(x, axis=-1):
    return jax.nn.softmax(x, axis=axis)

def _gelu(x):
    return jax.nn.gelu(x, approximate=True)

def _silu(x):
    return jax.nn.silu(x)

def _sigmoid(x):
    return jax.nn.sigmoid(x)

def _layernorm(x, axis=-1, eps=1e-05):
    m = jnp.mean(x, axis=axis, keepdims=True)
    v = jnp.var(x, axis=axis, keepdims=True)
    return (x - m) / jnp.sqrt(v + eps)

def _scatter_add(tgt, idx, src, axis=0):
    return tgt.at[idx].add(src)

def _segment_sum(src, seg, n):
    return jax.ops.segment_sum(src, seg, n)
kernel_name = 'mk_adaln_d2_jaxref_r8_97fc39'

def setup_inputs(seed: int=0):
    np.random.seed(seed)
    _w = jnp.asarray

    def _L0_attn_setup():
        import jax, jax.numpy as jnp
        import numpy as np
        DIM = 128
        HEADS = 16
        HIDDEN = 512
        EPS_ATTN = 1e-06
        EPS_LN = 1e-05

        def layer_norm(x, g, b):
            mu = jnp.mean(x, axis=-1, keepdims=True)
            var = jnp.var(x, axis=-1, keepdims=True)
            return (x - mu) * jax.lax.rsqrt(var + EPS_LN) * g + b
        key = jax.random.key(seed)
        ks = jax.random.split(key, 8)
        s = 0.02
        return {'x': jax.random.normal(ks[0], (4, 512, DIM), jnp.float32), 'norm1_g': jnp.ones((DIM,), jnp.float32), 'norm1_b': jnp.zeros((DIM,), jnp.float32), 'qkv_w': jax.random.normal(ks[1], (3 * DIM, DIM), jnp.float32) * s, 'proj_w': jax.random.normal(ks[2], (DIM, DIM), jnp.float32) * s, 'proj_b': jnp.zeros((DIM,), jnp.float32), 'norm2_g': jnp.ones((DIM,), jnp.float32), 'norm2_b': jnp.zeros((DIM,), jnp.float32), 'fc1_w': jax.random.normal(ks[3], (HIDDEN, DIM), jnp.float32) * s, 'fc1_b': jnp.zeros((HIDDEN,), jnp.float32), 'fc2_w': jax.random.normal(ks[4], (DIM, HIDDEN), jnp.float32) * s, 'fc2_b': jnp.zeros((DIM,), jnp.float32)}
    _L0_attn_in = _L0_attn_setup()

    def _L0_ffn_setup():
        import jax, jax.numpy as jnp
        import numpy as np
        H_DIM, E_DIM = (128, 64)
        N_SHARED, N_ROUTED, TOP_K = (2, 16, 4)
        B, S = (4, 256)
        key = jax.random.key(seed)
        ks = jax.random.split(key, 6)
        sc = 1.0 / np.sqrt(H_DIM)
        ec = 1.0 / np.sqrt(E_DIM)
        return {'x': jax.random.normal(ks[0], (B, S, H_DIM), dtype=jnp.float32), 'shared_up': jax.random.uniform(ks[1], (N_SHARED, E_DIM, H_DIM), jnp.float32, -sc, sc), 'shared_down': jax.random.uniform(ks[2], (N_SHARED, H_DIM, E_DIM), jnp.float32, -ec, ec), 'routed_up': jax.random.uniform(ks[3], (N_ROUTED, E_DIM, H_DIM), jnp.float32, -sc, sc), 'routed_down': jax.random.uniform(ks[4], (N_ROUTED, H_DIM, E_DIM), jnp.float32, -ec, ec), 'router_w': jax.random.uniform(ks[5], (N_ROUTED, H_DIM), jnp.float32, -sc, sc)}
    _L0_ffn_in = _L0_ffn_setup()
    _L0_c = _w((lambda *s: np.random.randn(*s).astype(np.float32) * 0.05)(4, 128))
    _L0_wmod = _w((lambda *s: np.random.randn(*s).astype(np.float32) * 0.05)(128, 6 * 128) * 128 ** (-0.5))

    def _L1_attn_setup():
        import jax, jax.numpy as jnp
        import numpy as np
        DIM = 128
        DIM_HEAD = 64
        N_HEADS = 16
        INNER = DIM_HEAD * N_HEADS
        LN_EPS = 1e-05

        def layer_norm(x, gamma, beta):
            mu = jnp.mean(x, axis=-1, keepdims=True)
            var = jnp.var(x, axis=-1, keepdims=True)
            return (x - mu) * jax.lax.rsqrt(var + LN_EPS) * gamma + beta

        def alibi_bias(seq, n_heads):
            n_sequence = jnp.arange(n_heads, 0, -1).astype(jnp.float32)
            head_scalars = 2.0 ** (-8.0 / n_sequence)
            idx = jnp.arange(seq)
            dist = -jnp.abs(idx[:, None] - idx[None, :]).astype(jnp.float32)
            return head_scalars[:, None, None] * dist
        key = jax.random.key(seed)
        ks = jax.random.split(key, 6)
        B, S = (2, 256)
        scale = 0.02
        return {'x': jax.random.normal(ks[0], (B, S, DIM), dtype=jnp.float32), 'ln_gamma': jnp.ones((DIM,), dtype=jnp.float32), 'ln_beta': jnp.zeros((DIM,), dtype=jnp.float32), 'Wq': jax.random.normal(ks[1], (DIM, INNER), dtype=jnp.float32) * scale, 'Wk': jax.random.normal(ks[2], (DIM, INNER), dtype=jnp.float32) * scale, 'Wv': jax.random.normal(ks[3], (DIM, INNER), dtype=jnp.float32) * scale, 'Wo': jax.random.normal(ks[4], (INNER, DIM), dtype=jnp.float32) * scale}
    _L1_attn_in = _L1_attn_setup()

    def _L1_ffn_setup():
        import jax, jax.numpy as jnp
        import numpy as np
        B, S, D, F, E, NS, K = (2, 128, 128, 512, 8, 8, 2)
        FS = F // NS
        key = jax.random.key(seed)
        ks = jax.random.split(key, 8)
        scale = 0.02
        return {'hidden_states': jax.random.normal(ks[0], (B, S, D), jnp.float32), 'gate_W': jax.random.normal(ks[1], (E, D), jnp.float32) * scale, 'w1_e': jax.random.normal(ks[2], (E, D, F), jnp.float32) * scale, 'w3_e': jax.random.normal(ks[3], (E, D, F), jnp.float32) * scale, 'w2_e': jax.random.normal(ks[4], (E, F, D), jnp.float32) * scale, 'w1_s': jax.random.normal(ks[5], (NS, D, FS), jnp.float32) * scale, 'w3_s': jax.random.normal(ks[6], (NS, D, FS), jnp.float32) * scale, 'w2_s': jax.random.normal(ks[7], (NS, FS, D), jnp.float32) * scale}
    _L1_ffn_in = _L1_ffn_setup()
    _L1_c = _w((lambda *s: np.random.randn(*s).astype(np.float32) * 0.05)(4, 128))
    _L1_wmod = _w((lambda *s: np.random.randn(*s).astype(np.float32) * 0.05)(128, 6 * 128) * 128 ** (-0.5))
    _d = {'L0_attn_x': _L0_attn_in['x'], 'L0_attn_norm1_g': _L0_attn_in['norm1_g'], 'L0_attn_norm1_b': _L0_attn_in['norm1_b'], 'L0_attn_qkv_w': _L0_attn_in['qkv_w'], 'L0_attn_proj_w': _L0_attn_in['proj_w'], 'L0_attn_proj_b': _L0_attn_in['proj_b'], 'L0_attn_norm2_g': _L0_attn_in['norm2_g'], 'L0_attn_norm2_b': _L0_attn_in['norm2_b'], 'L0_attn_fc1_w': _L0_attn_in['fc1_w'], 'L0_attn_fc1_b': _L0_attn_in['fc1_b'], 'L0_attn_fc2_w': _L0_attn_in['fc2_w'], 'L0_attn_fc2_b': _L0_attn_in['fc2_b'], 'L0_ffn_shared_up': _L0_ffn_in['shared_up'], 'L0_ffn_shared_down': _L0_ffn_in['shared_down'], 'L0_ffn_routed_up': _L0_ffn_in['routed_up'], 'L0_ffn_routed_down': _L0_ffn_in['routed_down'], 'L0_ffn_router_w': _L0_ffn_in['router_w'], 'L0_c': _L0_c, 'L0_wmod': _L0_wmod, 'L1_attn_ln_gamma': _L1_attn_in['ln_gamma'], 'L1_attn_ln_beta': _L1_attn_in['ln_beta'], 'L1_attn_Wq': _L1_attn_in['Wq'], 'L1_attn_Wk': _L1_attn_in['Wk'], 'L1_attn_Wv': _L1_attn_in['Wv'], 'L1_attn_Wo': _L1_attn_in['Wo'], 'L1_ffn_gate_W': _L1_ffn_in['gate_W'], 'L1_ffn_w1_e': _L1_ffn_in['w1_e'], 'L1_ffn_w3_e': _L1_ffn_in['w3_e'], 'L1_ffn_w2_e': _L1_ffn_in['w2_e'], 'L1_ffn_w1_s': _L1_ffn_in['w1_s'], 'L1_ffn_w3_s': _L1_ffn_in['w3_s'], 'L1_ffn_w2_s': _L1_ffn_in['w2_s'], 'L1_c': _L1_c, 'L1_wmod': _L1_wmod}
    _x0 = _d['L0_attn_x']
    _d['L0_attn_x'] = jax.random.normal(jax.random.fold_in(jax.random.key(seed), 1), (4, 1024, 128), dtype=_x0.dtype)
    del _x0
    return _d

def reference(L0_attn_x, L0_attn_norm1_g, L0_attn_norm1_b, L0_attn_qkv_w, L0_attn_proj_w, L0_attn_proj_b, L0_attn_norm2_g, L0_attn_norm2_b, L0_attn_fc1_w, L0_attn_fc1_b, L0_attn_fc2_w, L0_attn_fc2_b, L0_ffn_shared_up, L0_ffn_shared_down, L0_ffn_routed_up, L0_ffn_routed_down, L0_ffn_router_w, L0_c, L0_wmod, L1_attn_ln_gamma, L1_attn_ln_beta, L1_attn_Wq, L1_attn_Wk, L1_attn_Wv, L1_attn_Wo, L1_ffn_gate_W, L1_ffn_w1_e, L1_ffn_w3_e, L1_ffn_w2_e, L1_ffn_w1_s, L1_ffn_w3_s, L1_ffn_w2_s, L1_c, L1_wmod):

    def _L0_attn_ref(x, norm1_g, norm1_b, qkv_w, proj_w, proj_b, norm2_g, norm2_b, fc1_w, fc1_b, fc2_w, fc2_b):
        import jax, jax.numpy as jnp
        import numpy as np
        DIM = 128
        HEADS = 16
        HIDDEN = 512
        EPS_ATTN = 1e-06
        EPS_LN = 1e-05

        def layer_norm(x, g, b):
            mu = jnp.mean(x, axis=-1, keepdims=True)
            var = jnp.var(x, axis=-1, keepdims=True)
            return (x - mu) * jax.lax.rsqrt(var + EPS_LN) * g + b
        B, N, C = x.shape
        H = HEADS
        d = C // H
        h = layer_norm(x, norm1_g, norm1_b)
        qkv = jnp.einsum('bnc,oc->bno', h, qkv_w)
        qkv = qkv.reshape(B, N, 3, H, d)
        q = jnp.transpose(qkv[:, :, 0], (0, 2, 1, 3))
        k = jnp.transpose(qkv[:, :, 1], (0, 2, 1, 3))
        v = jnp.transpose(qkv[:, :, 2], (0, 2, 1, 3))
        q = jax.nn.elu(q) + 1.0
        k = jax.nn.elu(k) + 1.0
        kv = jnp.einsum('bhnd,bhne->bhde', k, v)
        ksum = jnp.sum(k, axis=2)
        z = 1.0 / (jnp.einsum('bhnd,bhd->bhn', q, ksum) + EPS_ATTN)
        attn_out = jnp.einsum('bhnd,bhde->bhne', q, kv) * z[..., None]
        attn_out = jnp.transpose(attn_out, (0, 2, 1, 3)).reshape(B, N, C)
        attn_out = jnp.einsum('bnc,oc->bno', attn_out, proj_w) + proj_b
        x = x + attn_out
        h = layer_norm(x, norm2_g, norm2_b)
        h = jax.nn.gelu(jnp.einsum('bnc,hc->bnh', h, fc1_w) + fc1_b, approximate=False)
        h = jnp.einsum('bnh,ch->bnc', h, fc2_w) + fc2_b
        return x + h

    def _L0_ffn_ref(x, shared_up, shared_down, routed_up, routed_down, router_w):
        import jax, jax.numpy as jnp
        import numpy as np
        H_DIM, E_DIM = (128, 64)
        N_SHARED, N_ROUTED, TOP_K = (2, 16, 4)
        B, S = (4, 256)
        b, s, h = x.shape
        xt = x.reshape(-1, h)
        up_s = jnp.einsum('th,seh->tse', xt, shared_up)
        shared = jnp.einsum('tse,she->th', jax.nn.gelu(up_s, approximate=False), shared_down)
        probs = jax.nn.softmax(xt @ router_w.T, axis=-1)
        topk_p, topk_i = jax.lax.top_k(probs, TOP_K)
        gate = jnp.zeros_like(probs).at[jnp.arange(xt.shape[0])[:, None], topk_i].add(topk_p)
        up_r = jnp.einsum('th,reh->tre', xt, routed_up)
        act = jax.nn.gelu(up_r, approximate=False) * gate[:, :, None]
        routed = jnp.einsum('tre,rhe->th', act, routed_down)
        return (shared + routed).reshape(b, s, h)

    def _L1_attn_ref(x, ln_gamma, ln_beta, Wq, Wk, Wv, Wo):
        import jax, jax.numpy as jnp
        import numpy as np
        DIM = 128
        DIM_HEAD = 64
        N_HEADS = 16
        INNER = DIM_HEAD * N_HEADS
        LN_EPS = 1e-05

        def layer_norm(x, gamma, beta):
            mu = jnp.mean(x, axis=-1, keepdims=True)
            var = jnp.var(x, axis=-1, keepdims=True)
            return (x - mu) * jax.lax.rsqrt(var + LN_EPS) * gamma + beta

        def alibi_bias(seq, n_heads):
            n_sequence = jnp.arange(n_heads, 0, -1).astype(jnp.float32)
            head_scalars = 2.0 ** (-8.0 / n_sequence)
            idx = jnp.arange(seq)
            dist = -jnp.abs(idx[:, None] - idx[None, :]).astype(jnp.float32)
            return head_scalars[:, None, None] * dist
        B, S, _ = x.shape
        xn = layer_norm(x, ln_gamma, ln_beta)

        def heads(t):
            return t.reshape(B, S, N_HEADS, DIM_HEAD).transpose(0, 2, 1, 3)
        q = heads(xn @ Wq)
        k = heads(xn @ Wk)
        v = heads(xn @ Wv)
        att = jnp.einsum('bhid,bhjd->bhij', q, k) / DIM_HEAD ** 0.5
        att = att + alibi_bias(S, N_HEADS)[None]
        p = jax.nn.softmax(att, axis=-1)
        out = jnp.einsum('bhij,bhjd->bhid', p, v)
        out = out.transpose(0, 2, 1, 3).reshape(B, S, INNER)
        return out @ Wo

    def _L1_ffn_ref(hidden_states, gate_W, w1_e, w3_e, w2_e, w1_s, w3_s, w2_s):
        import jax, jax.numpy as jnp
        import numpy as np
        B, S, D, F, E, NS, K = (2, 128, 128, 512, 8, 8, 2)
        FS = F // NS
        b, s, d = hidden_states.shape
        e = gate_W.shape[0]
        flat = hidden_states.reshape(-1, d)
        T = flat.shape[0]
        logits = (flat @ gate_W.T).astype(jnp.float32)
        probs = jax.nn.softmax(logits, axis=-1)
        top_v, top_i = jax.lax.top_k(probs, K)
        gates = jnp.zeros((T, e), probs.dtype).at[jnp.arange(T)[:, None], top_i].set(top_v)
        g = jax.nn.silu(jnp.einsum('td,edf->etf', flat, w1_e))
        u = jnp.einsum('td,edf->etf', flat, w3_e)
        out_e = jnp.einsum('etf,efd->etd', g * u, w2_e)
        routed = jnp.einsum('te,etd->td', gates, out_e).reshape(b, s, d)
        gs = jax.nn.silu(jnp.einsum('bsd,ndf->nbsf', hidden_states, w1_s))
        us = jnp.einsum('bsd,ndf->nbsf', hidden_states, w3_s)
        shared = jnp.einsum('nbsf,nfd->bsd', gs * us, w2_s) / w1_s.shape[0]
        alpha = 0.5
        return alpha * shared + (1.0 - alpha) * routed
    x = L0_attn_x
    mod = (_silu(L0_c) @ L0_wmod).reshape(L0_c.shape[0], 6, 1, -1)
    sa, ca, ga, sb, cb, gb = (mod[:, 0], mod[:, 1], mod[:, 2], mod[:, 3], mod[:, 4], mod[:, 5])
    ga = (2 * (ga >= 0) - 1) * jnp.maximum(jnp.abs(ga), 0.25)
    gb = (2 * (gb >= 0) - 1) * jnp.maximum(jnp.abs(gb), 0.25)
    h = _layernorm(x, axis=-1) * (1 + ca) + sa
    x = x + ga * _L0_attn_ref(h, L0_attn_norm1_g, L0_attn_norm1_b, L0_attn_qkv_w, L0_attn_proj_w, L0_attn_proj_b, L0_attn_norm2_g, L0_attn_norm2_b, L0_attn_fc1_w, L0_attn_fc1_b, L0_attn_fc2_w, L0_attn_fc2_b)
    h = _layernorm(x, axis=-1) * (1 + cb) + sb
    x = x + gb * _L0_ffn_ref(h, L0_ffn_shared_up, L0_ffn_shared_down, L0_ffn_routed_up, L0_ffn_routed_down, L0_ffn_router_w)
    mod = (_silu(L1_c) @ L1_wmod).reshape(L1_c.shape[0], 6, 1, -1)
    sa, ca, ga, sb, cb, gb = (mod[:, 0], mod[:, 1], mod[:, 2], mod[:, 3], mod[:, 4], mod[:, 5])
    ga = (2 * (ga >= 0) - 1) * jnp.maximum(jnp.abs(ga), 0.25)
    gb = (2 * (gb >= 0) - 1) * jnp.maximum(jnp.abs(gb), 0.25)
    h = _layernorm(x, axis=-1) * (1 + ca) + sa
    x = x + ga * _L1_attn_ref(h, L1_attn_ln_gamma, L1_attn_ln_beta, L1_attn_Wq, L1_attn_Wk, L1_attn_Wv, L1_attn_Wo)
    h = _layernorm(x, axis=-1) * (1 + cb) + sb
    x = x + gb * _L1_ffn_ref(h, L1_ffn_gate_W, L1_ffn_w1_e, L1_ffn_w3_e, L1_ffn_w2_e, L1_ffn_w1_s, L1_ffn_w3_s, L1_ffn_w2_s)
    return x

_drawn_inputs = setup_inputs


def setup_inputs(seed=0):
    import zlib

    import numpy as np

    out = dict(_drawn_inputs(seed))
    spreads = {'L0_attn_norm1_g': (1.0, 0.6),
     'L0_attn_norm1_b': (0.0, 0.8),
     'L0_attn_proj_b': (0.0, 0.299),
     'L0_attn_norm2_g': (1.0, 0.6),
     'L0_attn_norm2_b': (0.0, 0.8),
     'L0_attn_fc1_b': (0.0, 0.8),
     'L0_attn_fc2_b': (0.0, 0.308),
     'L1_attn_ln_gamma': (1.0, 0.6),
     'L1_attn_ln_beta': (0.0, 0.8)}
    factors = {'L0_attn_qkv_w': 8.0,
     'L0_attn_proj_w': 8.0,
     'L0_attn_fc1_w': 3.933,
     'L0_attn_fc2_w': 3.657,
     'L0_ffn_routed_up': 5.299,
     'L0_ffn_routed_down': 4.992,
     'L0_ffn_router_w': 5.578,
     'L1_attn_Wq': 8.0,
     'L1_attn_Wk': 8.0,
     'L1_attn_Wv': 4.389,
     'L1_attn_Wo': 4.34,
     'L1_ffn_gate_W': 8.0,
     'L1_ffn_w1_e': 8.0,
     'L1_ffn_w3_e': 8.0,
     'L1_ffn_w2_e': 8.0,
     'L1_ffn_w1_s': 8.0,
     'L1_ffn_w3_s': 8.0,
     'L1_ffn_w2_s': 8.0,
     'L1_c': 4.556,
     'L1_wmod': 4.39}
    for name, (base, spread) in spreads.items():
        noise = np.random.default_rng([zlib.crc32(name.encode()), seed]).standard_normal(out[name].shape)
        drawn = base * np.exp(spread * noise) if base else spread * noise
        out[name] = jnp.asarray(drawn.astype(out[name].dtype))
    for name, factor in factors.items():
        out[name] = (out[name] * factor).astype(out[name].dtype)
    return out
```

```python
from contextlib import ExitStack

import numpy as np

import concourse.bass as bass
from concourse import mybir

F32 = mybir.dt.float32
F32R = mybir.dt.float32r
BF16 = mybir.dt.bfloat16
ACT = mybir.ActivationFunctionType
ALU = mybir.AluOpType
AX = mybir.AxisListType

B, N, D = 4, 1024, 128
T = N // 128
HALF = 512
NHALF = N // HALF
TPH = T // NHALF
EPS_LN = 1e-5
EPS_ATTN = 1e-6
H0, DH0 = 16, 8
HID = 512
FC = HID // 128
E0, K0, SH0 = 16, 4, 2
CH0 = (E0 + SH0) // 2
H1, DH1 = 16, 64
PAIRS = H1 // 2
E1, K1N, F1 = 8, 2, 512
EX1 = E1 + 1
FCH = F1 // 128
UNITS = FCH * NHALF
WBUF = 3
RING = 4
MODS = 6
GW = 16
NAUX = 32
MROW = 96
KEXACT = MROW + 2
ST_AT, EXP_AT, PV_AT, COPIED_AT, NORM_AT, W3_AT, UNIT_AT = 1, 1, RING, 1, 1, 1, 2

C_IDENT, C_DIST, C_MASK, C_SLOPE = 0, 128, 256, 384
C_SELB = C_SLOPE + 3 * H1
C_SELD = C_SELB + (CH0 - 1) * 128
C_AUXQ = C_SELD + (EX1 + 1) * 128
C_END = C_AUXQ + N


def split12(x):
    x = x.astype(np.float32)
    c = (x * np.float32(4097)).astype(np.float32)
    hi = (c - (c - x)).astype(np.float32)
    return hi, (x - hi).astype(np.float32)


def cut8(x):
    return (x.astype(np.float32).view(np.uint32) & np.uint32(0xFFFF0000)).view(np.float32)


def constants():
    c = np.zeros((128, C_END), np.float32)
    i = np.arange(128)
    c[:, C_IDENT:C_IDENT + 128] = np.eye(128)
    c[:, C_DIST:C_DIST + 128] = -np.abs(i[:, None] - i[None, :])
    c[:, C_MASK:C_MASK + 128] = (i[:, None] // DH0) == (i[None, :] // DH0)
    slope = (np.float32(2.0) ** (np.float32(-8.0) / np.arange(H1, 0, -1).astype(np.float32))).astype(np.float32)
    s8 = slope * np.float32(DH1 ** 0.5)
    a = cut8(s8)
    m = cut8(s8 - a)
    for h in range(H1):
        c[:, C_SLOPE + 3 * h:C_SLOPE + 3 * h + 3] = [a[h], m[h], s8[h] - a[h] - m[h]]
    for k in range(CH0 - 1):
        for part in range(3):
            c[part * GW + 2 * k, C_SELB + 128 * k:C_SELB + 128 * k + 64] = 1
            c[part * GW + 2 * k + 1, C_SELB + 128 * k + 64:C_SELB + 128 * k + 128] = 1
    for e in range(EX1):
        for part in range(3):
            c[part * GW + e, C_SELD + 128 * e:C_SELD + 128 * e + 128] = 1
    for t in range(T):
        cols = slice(C_AUXQ + 128 * t, C_AUXQ + 128 * t + 128)
        c[64 + t, cols] = 1
        c[64 + T + t, cols] = 1
        c[64 + 2 * T + t, cols] = i
        c[64 + 3 * T + t, cols] = i
    aux = np.zeros((H1, NAUX, N), np.float32)
    j = np.arange(N)
    for t in range(T):
        d = t - j // 128
        base = (-np.sign(d) * (128 * d - j % 128)).astype(np.float32)
        for h in range(H1):
            aux[h, t], aux[h, T + t] = split12(s8[h] * base)
            aux[h, 2 * T + t], aux[h, 3 * T + t] = split12(-s8[h] * np.sign(d).astype(np.float32))
    return c, aux


LN_TAGS = ["a0", "a1", "a2", "b0", "c0", "c1", "d0"]
TR_TAGS = ["a1", "a2", "b0", "c1", "d0"]
BATCH_SEMS = (
    ["ln_moments", "ln_eps", "ln_rstd", "ln_norm", "modulated", "turned", "hT_dve", "hT_act",
     "x_in", "mod_in", "vec_copied", "x_out"]
    + ["q0_mm", "k0_mm", "q0_min", "k0_min", "q0_exp", "k0_exp", "q0_done", "k0_done", "v0_copied",
       "kv_mm", "ks_mm", "kv_masked", "ks_masked", "num_mm", "den_mm", "den_eps", "den_inv", "o0_done",
       "proj_mm", "x1_sum", "x1_done", "x1_bias", "fc1_mm", "fc1_act", "fc2_mm", "y0", "y0_scaled", "xa_done"]
    + [f"{t}_{n}" for t in ("rb", "rd") for n in ("mm", "sub", "exp", "steps", "lo", "turned", "rows")]
    + ["up_mm", "bcb_mm", "up_act", "up_gated", "downb_mm", "downb_end", "yb_scaled", "xb_done"]
    + ["o1_mm", "o1_scaled", "xc_done"]
    + ["w1_in0", "w1_in1", "w1_in2", "bcd_mm", "hg_done", "w1_mm", "w3_mm", "silu_done", "gu_done",
       "downd_mm", "downd_end", "yd_scaled", "xd_done"]
    + ["wh_in0", "wh_in1", "aux_in0", "aux_in1", "v_mm", "v_in", "qk_mm", "q_hi", "k_hi", "k_aux",
       "k_dup", "k_lo", "q_dup", "q_lo", "max_mm", "max_red", "m_hi", "m_mid", "m_row", "m_in",
       "st_mm", "exp_done", "pv_done", "o_copied", "s_copied", "s_inv", "o_norm"]
)


def network(nc, a):
    ctx = ExitStack()
    with ctx:
        def sb(name, shape, dt=F32):
            return ctx.enter_context(nc.sbuf_tensor(name, shape, dt))

        S = {n: ctx.enter_context(nc.semaphore(n)) for n in BATCH_SEMS}
        first, last = S[BATCH_SEMS[0]].num, S[BATCH_SEMS[-1]].num
        assert last - first == len(BATCH_SEMS) - 1
        G = {n: ctx.enter_context(nc.semaphore(n)) for n in
             ("weights_in", "consts_in", "c_silu", "mod_mm", "modT_mm", "mod_abs", "mod_sgn",
              "mod_pm", "mod_one", "mod_out", "modT_copied", "set_done", "pool_set", "batch_ended", "batch_open", "passed")}

        wqkv0 = sb("wqkv0", [128, 3 * D])
        wproj = sb("wproj", [128, D])
        wfc1 = sb("wfc1", [128, HID])
        wfc2 = sb("wfc2", [128, FC, D])
        wup = sb("wup", [128, CH0, 128])
        wdown = sb("wdown", [128, CH0, D])
        wrout = sb("wrout", [128, E0])
        wgate = sb("wgate", [128, E1])
        wo = sb("wo", [128, PAIRS, D])
        vecs = sb("vecs", [128, 4 + FC + 2])
        biasb = sb("biasb", [128, 2, D])
        identf = sb("identf", [128, 128])
        identb = sb("identb", [128, 128], BF16)
        distb = sb("distb", [128, 128], BF16)
        mask = sb("mask", [128, 128])
        diagb = sb("diagb", [128, 3 * H1, 128], BF16)
        selb = sb("selb", [128, CH0 - 1, 128], BF16)
        seld = sb("seld", [128, EX1 + 1, 128], BF16)
        zerob = sb("zerob", [128, HALF], BF16)
        onecol = sb("onecol", [128, 1])
        halfneg = sb("halfneg", [128, T])
        modT = sb("modT", [128, 2 * MODS, B])
        modv = sb("modv", [128, 2 * MODS])
        modb = sb("modb", [128, 2 * MODS, D])
        x = sb("x", [128, T, D])
        xn = sb("xn", [128, T, D])
        h = sb("h", [128, T, D])
        hT = sb("hT", [128, N])
        A = sb("A", [128, 8, N])
        cT = sb("cT", [128, 2, B])
        cs = sb("cs", [128, 2, B])
        stats = sb("stats", [128, T, 6])
        mv = sb("mv", [128, T, 2])
        veps = sb("veps", [128, T])
        rstd = sb("rstd", [128, T])
        small = sb("small", [128, 2, 128])
        rmax = sb("rmax", [128, 3, T])
        rlog = sb("rlog", [128, T, GW])
        rexp = sb("rexp", [128, T, GW])
        prob = sb("prob", [128, 2, T, GW + 8])
        top8 = sb("top8", [128, T, 8])
        hit = sb("hit", [128, T, GW + 8])
        gate = sb("gate", [128, 3, T, GW])
        gparts = sb("gparts", [128, T, 3 * GW], BF16)
        grows = sb("grows", [128, N], BF16)
        whead = [sb(f"whead{s}", [128, 3 * DH1]) for s in range(2)]
        auxin = sb("auxin", [96, N])
        Ka = [sb(f"Ka{s}", [128, N], F32R) for s in range(2)]
        Kb = [sb(f"Kb{s}", [128, N], F32R) for s in range(2)]
        Qa = [sb(f"Qa{s}", [128, N], F32R) for s in range(2)]
        Qb = [sb(f"Qb{s}", [128, N], F32R) for s in range(2)]
        V = [sb(f"V{s}", [128, T, 128]) for s in range(2)]
        pt = sb("pt", [128, RING, N])
        opair = sb("opair", [128, N])
        spair = sb("spair", [128, N])
        mneg = sb("mneg", [128, T])
        mparts = sb("mparts", [128, T, 2], BF16)
        wex = [sb(f"wex{i}", [128, 3 * F1]) for i in range(WBUF)]

        P = ctx.enter_context(nc.psum_tensor("P", [128, 8, HALF], F32))

        def banks(i, n=2, rows=slice(0, 128)):
            return P[rows, i:i + n, :].rearrange("p a b -> p (a b)")

        def tiles(i):
            return P[:, i:i + 2, :].rearrange("p a (t d) -> p (a t) d", d=D)

        def half(t, i):
            return t[:, i * HALF:(i + 1) * HALF]

        def tok(t):
            return t.rearrange("p (t d) -> p t d", d=D)

        def over(v, shape):
            return v.unsqueeze(1).to_broadcast(shape)

        def col(v, n):
            return v.unsqueeze(2).to_broadcast([128, T, n])

        def bank_t(i, t):
            return P[:, i + t // TPH, (t % TPH) * D:(t % TPH + 1) * D]

        def end_batch(e, b):
            e.drain().then_inc(G["batch_ended"], 1)
            v = e.snap(b + 1)
            e.wait_ge(G["batch_open"], v)
            e.sem_inc(G["passed"], 1)

        block = ctx.enter_context(nc.Block())
        NLOAD = 13
        NSET, NPOOL = 2, 8

        @block.sync
        def _(sp):
            sp.dma_start(A[:, 0:5, :].rearrange("p a b -> p (a b)")[:, 0:C_END], a["consts"]).then_inc(G["consts_in"], 16)
            for dst, src in ((wqkv0[:, :], a["wqkv0"]), (wproj[:, :], a["wproj"]), (wfc1[:, :], a["wfc1"]),
                             (wfc2[:, :, :], a["wfc2"]), (wup[:, :, :], a["wup"]), (wdown[:, :, :], a["wdown"]),
                             (wrout[:, :], a["wrout"]), (wgate[:, :], a["wgate"]), (wo[:, :, :], a["wo"]),
                             (vecs[:, :], a["vecs"]),
                             (biasb[:, :, :], a["biases"].partition_broadcast(128)),
                             (modb[:, :, :].rearrange("p a b -> p (a b)"), a["wmod"]),
                             (cT[:, :, :], a["cT"])):
                sp.dma_start(dst, src).then_inc(G["weights_in"], 16)

            sp.wait_ge(G["mod_one"], 1)
            sp.dma_start(a["modrows"], A[0:B, 6:8, :].rearrange("p a b -> p (a b)")[:, 0:2 * MODS * D]).then_inc(G["mod_out"], 16)
            sp.wait_ge(G["mod_out"], 16)
            sp.wait_ge(G["modT_copied"], 2)
            sp.wait_ge(G["set_done"], NSET)
            sp.wait_ge(G["pool_set"], NPOOL)

            with sp.Fori(0, B) as b:
                sp.dma_start(x[:, :, :], a["x"][b]).then_inc(S["x_in"], 16)
                sp.dma_start(modb[:, :, :], a["modrows"].rearrange("b (m d) -> b m d", d=D)[b].partition_broadcast(128)).then_inc(S["mod_in"], 16)

                def load_head(g, s):
                    sp.dma_start(whead[s][:, :], a["whead"][g]).then_inc(S[f"wh_in{s}"], 16)

                def load_aux(g, s):
                    sp.dma_start(auxin[64:96, :], a["aux"][g]).then_inc(S[f"aux_in{s}"], 16)

                load_head(0, 0)
                load_head(1, 1)
                load_aux(0, 0)
                for e in range(WBUF):
                    sp.dma_start(wex[e][:, :], a["wex"][e]).then_inc(S[f"w1_in{e}"], 16)
                with sp.Fori(0, PAIRS - 1) as p:
                    va, vb = sp.snap(2 * p + 1), sp.snap(2 * p + 2)
                    sp.wait_ge(S["k_aux"], va)
                    sp.sem_inc(G["passed"], 1)
                    load_aux(2 * p + 1, 1)
                    sp.wait_ge(S["qk_mm"], va)
                    sp.sem_inc(G["passed"], 1)
                    load_head(2 * p + 2, 0)
                    sp.wait_ge(S["k_aux"], vb)
                    sp.sem_inc(G["passed"], 1)
                    load_aux(2 * p + 2, 0)
                    sp.wait_ge(S["qk_mm"], vb)
                    sp.sem_inc(G["passed"], 1)
                    load_head(2 * p + 3, 1)
                sp.wait_ge(S["k_aux"], H1 - 1)
                load_aux(H1 - 1, 1)

                with sp.Fori(1, EX1 // WBUF) as r:
                    vs = [sp.snap((r * WBUF - WBUF + i + 1) * UNITS + UNIT_AT) for i in range(WBUF)]
                    for i in range(WBUF):
                        sp.wait_ge(S["downd_mm"], vs[i])
                        sp.sem_inc(G["passed"], 1)
                        sp.dma_start(wex[i][:, :], a["wex"][r * WBUF + i]).then_inc(S[f"w1_in{i}"], 16)

                sp.wait_ge(S["xd_done"], 1)
                sp.dma_start(a["out"][b], x[:, :, :]).then_inc(S["x_out"], 16)
                v = sp.snap(b * 4 + 4)
                sp.wait_ge(S["x_out"], 16)
                sp.sem_inc(G["passed"], 1)
                sp.wait_ge(G["batch_ended"], v)
                sp.sem_inc(G["passed"], 1)
                sp.sem_clear(range(first, last + 1))
                sp.drain().then_inc(G["batch_open"], 1)

        @block.gpsimd
        def _(pool):
            pool.memset(halfneg[:, :], -0.5).then_inc(G["pool_set"], 1)
            pool.memset(zerob[:, :], 0.0).then_inc(G["pool_set"], 1)
            pool.memset(onecol[:, :], 1.0).then_inc(G["pool_set"], 1)
            pool.memset(grows[:, :], 0.0).then_inc(G["pool_set"], 1)
            pool.memset(prob[:, :, :, :], -1.0).then_inc(G["pool_set"], 1)
            pool.memset(V[0][:, :, DH1:2 * DH1], 1.0).then_inc(G["pool_set"], 1)
            pool.memset(V[1][:, :, 0:DH1], 1.0).then_inc(G["pool_set"], 1)
            pool.memset(gate[:, :, :, :], 0.0).then_inc(G["pool_set"], 1)
            pool.wait_ge(G["pool_set"], NPOOL)
            with pool.Fori(0, B) as b:
                for tag in LN_TAGS:
                    pool.wait_ge(S["ln_eps"], LN_TAGS.index(tag) + 1)
                    pool.tensor_tensor(rstd[:, :], veps[:, :], halfneg[:, :], ALU.pow).then_inc(S["ln_rstd"], 1)
                end_batch(pool, b)

        @block.vector
        def _(dve):
            tens = [128, T, D]
            cst = A[:, 0:5, :].rearrange("p a b -> p (a b)")

            dve.wait_ge(G["consts_in"], 16)
            dve.tensor_copy(identf[:, :], cst[:, C_IDENT:C_IDENT + 128])
            dve.tensor_copy(identb[:, :], cst[:, C_IDENT:C_IDENT + 128])
            dve.tensor_copy(distb[:, :], cst[:, C_DIST:C_DIST + 128])
            dve.tensor_copy(mask[:, :], cst[:, C_MASK:C_MASK + 128])
            dve.tensor_copy(selb[:, :, :].rearrange("p a b -> p (a b)"), cst[:, C_SELB:C_SELD])
            dve.tensor_copy(seld[:, :, :].rearrange("p a b -> p (a b)"), cst[:, C_SELD:C_AUXQ])
            dve.tensor_tensor(diagb[:, :, :], over(cst[:, C_IDENT:C_IDENT + 128], [128, 3 * H1, 128]),
                              cst[:, C_SLOPE:C_SLOPE + 3 * H1].unsqueeze(2).to_broadcast([128, 3 * H1, 128]), ALU.mult)
            for s in range(2):
                dve.tensor_copy(Qa[s][64:96, :], cst[64:96, C_AUXQ:C_END])
                dve.tensor_scalar(Ka[s][96:128, :], cst[96:128, C_AUXQ:C_END], 0.0, 1.0, ALU.mult, ALU.add)\
                    .then_inc(G["set_done"], 1)

            rows = A[0:B, 6:8, :].rearrange("p a b -> p (a b)")[:, 0:2 * MODS * D]
            dve.wait_ge(G["mod_mm"], 1)
            dve.tensor_copy(rows, P[0:B, 0:3, :].rearrange("p a b -> p (a b)")).then_inc(G["mod_abs"], 1)
            dve.wait_ge(G["mod_abs"], 1)
            r3 = rows.rearrange("p (m d) -> p m d", d=D)
            gs = r3[:, 2::3, :]
            tmp = A[0:B, 0, 0:4 * D].rearrange("p (m d) -> p m d", d=D)
            sg = A[0:B, 1, 0:4 * D].rearrange("p (m d) -> p m d", d=D)
            dve.wait_ge(G["set_done"], NSET)
            dve.wait_ge(G["pool_set"], NPOOL)
            dve.scalar_tensor_tensor(tmp, gs, -1.0, gs, ALU.mult, ALU.max).then_inc(G["mod_abs"], 1)
            dve.tensor_scalar(sg, gs, 0.0, 2.0, ALU.is_ge, ALU.mult).then_inc(G["mod_abs"], 1)
            dve.wait_ge(G["mod_abs"], 3)
            dve.tensor_scalar(tmp, tmp, 0.25, None, ALU.max).then_inc(G["mod_sgn"], 1)
            dve.tensor_scalar(sg, sg, -1.0, None, ALU.add).then_inc(G["mod_sgn"], 1)
            dve.wait_ge(G["mod_sgn"], 2)
            dve.tensor_tensor(gs, tmp, sg, ALU.mult)
            dve.tensor_scalar(r3[:, 1::3, :], r3[:, 1::3, :], 1.0, None, ALU.add).then_inc(G["mod_one"], 1)
            dve.wait_ge(G["modT_mm"], 1)
            dve.tensor_copy(modT[:, :, :], P[:, 3, 0:2 * MODS * B].rearrange("p (m b) -> p m b", b=B)).then_inc(G["modT_copied"], 1)
            dve.wait_ge(G["modT_copied"], 1)
            dve.tensor_scalar(modT[:, 1::3, :], modT[:, 1::3, :], 1.0, None, ALU.add).then_inc(G["modT_copied"], 1)
            dve.wait_ge(G["modT_copied"], 2)

            def norm(tag, src, dst):
                nth = LN_TAGS.index(tag)
                for t in range(T):
                    dve.bn_stats(stats[:, t, :], src[:, t, :]).then_inc(S["ln_moments"], 1)
                dve.wait_ge(S["ln_moments"], (2 * nth + 1) * T)
                for t in range(T):
                    dve.bn_aggr(mv[:, t, :], stats[:, t, :]).then_inc(S["ln_moments"], 1)
                dve.wait_ge(S["ln_moments"], (2 * nth + 2) * T)
                dve.tensor_scalar(veps[:, :], mv[:, :, 1], EPS_LN, None, ALU.add).then_inc(S["ln_eps"], 1)
                dve.wait_ge(S["ln_rstd"], nth + 1)
                for t in range(T):
                    dve.tensor_scalar(dst[:, t, :], src[:, t, :], mv[:, t, 0:1], rstd[:, t:t + 1],
                                      ALU.subtract, ALU.mult).then_inc(S["ln_norm"], 1)

            def modulate(tag, m):
                dve.wait_ge(S["ln_norm"], (LN_TAGS.index(tag) + 1) * T)
                dve.tensor_tensor(h[:, :, :], xn[:, :, :], over(modb[:, m + 1, :], tens), ALU.mult).then_inc(S["modulated"], 1)
                dve.wait_ge(S["modulated"], m // 3 + 1)
                dve.tensor_tensor(h[:, :, :], h[:, :, :], over(modb[:, m, :], tens), ALU.add).then_inc(S["modulated"], 1)
                dve.wait_ge(S["modulated"], m // 3 + 2)

            def hT_half(tag, bank, scale, bias):
                dve.wait_ge(S["turned"], NHALF * TR_TAGS.index(tag) + 1)
                dve.tensor_scalar(half(hT, 0), P[:, bank, :], scale, bias, ALU.mult, ALU.add).then_inc(S["hT_dve"], 1)

            def router(tag, n, k, bank, bank2, table, factor):
                logits = P[:, bank, 0:T * n].rearrange("p (t e) -> p t e", e=n)
                dve.wait_ge(S[f"{tag}_mm"], 1)
                dve.tensor_reduce(rmax[:, 0, :], logits, AX.X, ALU.max).then_inc(S[f"{tag}_steps"], 1)
                dve.wait_ge(S[f"{tag}_steps"], 1)
                dve.tensor_tensor(rlog[:, :, 0:n], logits, col(rmax[:, 0, :], n), ALU.subtract).then_inc(S[f"{tag}_sub"], 1)
                dve.wait_ge(S[f"{tag}_exp"], 1)
                dve.tensor_reduce(rmax[:, 1, :], rexp[:, :, 0:n], AX.X, ALU.add).then_inc(S[f"{tag}_steps"], 1)
                dve.wait_ge(S[f"{tag}_steps"], 2)
                dve.reciprocal(rmax[:, 2, :], rmax[:, 1, :]).then_inc(S[f"{tag}_steps"], 1)
                dve.wait_ge(S[f"{tag}_steps"], 3)
                pr = prob[:, table, :, 0:n + 8]
                dve.scalar_tensor_tensor(pr[:, :, 0:n], rexp[:, :, 0:n], factor, col(rmax[:, 2, :], n),
                                         ALU.mult, ALU.mult).then_inc(S[f"{tag}_steps"], 1)
                dve.wait_ge(S[f"{tag}_steps"], 4)
                for t in range(T):
                    dve.max(top8[:, t, :], pr[:, t, :]).then_inc(S[f"{tag}_steps"], 1)
                dve.wait_ge(S[f"{tag}_steps"], 4 + T)
                dve.memset(top8[:, :, k:8], -1.0).then_inc(S[f"{tag}_steps"], 1)
                dve.wait_ge(S[f"{tag}_steps"], 5 + T)
                for t in range(T):
                    dve.match_replace(hit[:, t, 0:n + 8], top8[:, t, :], pr[:, t, :], -5.0).then_inc(S[f"{tag}_steps"], 1)
                dve.wait_ge(S[f"{tag}_steps"], 5 + 2 * T)
                dve.scalar_tensor_tensor(gate[:, 0, :, 0:n], hit[:, :, 0:n], -2.0, pr[:, :, 0:n],
                                         ALU.is_lt, ALU.mult).then_inc(S[f"{tag}_steps"], 1)
                dve.wait_ge(S[f"{tag}_steps"], 6 + 2 * T)
                g, r1, r2 = (gate[:, i, :, :] for i in range(3))
                hi, mid, lo = (gparts[:, :, i * GW:(i + 1) * GW] for i in range(3))
                dve.tensor_copy(hi, g).then_inc(S[f"{tag}_steps"], 1)
                dve.wait_ge(S[f"{tag}_steps"], 7 + 2 * T)
                dve.tensor_tensor(r1, g, hi, ALU.subtract).then_inc(S[f"{tag}_steps"], 1)
                dve.wait_ge(S[f"{tag}_steps"], 8 + 2 * T)
                dve.tensor_copy(mid, r1).then_inc(S[f"{tag}_steps"], 1)
                dve.wait_ge(S[f"{tag}_steps"], 9 + 2 * T)
                dve.tensor_tensor(lo, r1, mid, ALU.subtract).then_inc(S[f"{tag}_lo"], 1)
                dve.wait_ge(S[f"{tag}_turned"], 1)
                dve.tensor_copy(grows[0:3 * GW, :], P[0:3 * GW, bank2, :].bitcast(BF16)).then_inc(S[f"{tag}_rows"], 1)

            with dve.Fori(0, B) as b:
                dve.tensor_copy(modv[:, :], modT[:, :, b]).then_inc(S["vec_copied"], 1)

                dve.wait_ge(S["x_in"], 16)
                norm("a0", x, xn)
                dve.wait_ge(S["mod_in"], 16)
                modulate("a0", 0)
                norm("a1", h, xn)
                dve.wait_ge(S["vec_copied"], 1)
                hT_half("a1", 0, vecs[:, 0:1], vecs[:, 1:2])
                dve.wait_ge(S["q0_mm"], 2)
                dve.tensor_scalar(A[:, 0, :], banks(0), 0.0, None, ALU.min).then_inc(S["q0_min"], 1)
                kpsum = P[:, 2:6, :].rearrange("p a (t c) -> p (a t) c", c=2 * D)
                dve.wait_ge(S["k0_mm"], T)
                dve.tensor_scalar(tok(A[:, 2, :]), kpsum[:, :, 0:D], 0.0, None, ALU.min).then_inc(S["k0_min"], 1)
                dve.wait_ge(S["q0_exp"], 1)
                dve.scalar_tensor_tensor(A[:, 0, :], banks(0), 0.0, A[:, 1, :], ALU.max, ALU.add).then_inc(S["q0_done"], 1)
                dve.wait_ge(S["k0_exp"], 1)
                dve.scalar_tensor_tensor(tok(A[:, 2, :]), kpsum[:, :, 0:D], 0.0, tok(A[:, 3, :]), ALU.max, ALU.add).then_inc(S["k0_done"], 1)
                dve.tensor_copy(tok(A[:, 4, :]), kpsum[:, :, D:2 * D]).then_inc(S["v0_copied"], 1)
                dve.wait_ge(S["kv_mm"], 1)
                dve.tensor_tensor(small[:, 0, :], P[:, 6, 0:D], mask[:, :], ALU.mult).then_inc(S["kv_masked"], 1)
                dve.wait_ge(S["ks_mm"], 1)
                dve.tensor_scalar(small[:, 1, :], mask[:, :], P[:, 7, 0:1], None, ALU.mult).then_inc(S["ks_masked"], 1)
                dve.wait_ge(S["den_mm"], 2)
                dve.tensor_scalar(A[:, 1, :], banks(2), EPS_ATTN, None, ALU.add).then_inc(S["den_eps"], 1)
                dve.wait_ge(S["den_eps"], 1)
                dve.reciprocal(A[:, 3, :], A[:, 1, :]).then_inc(S["den_inv"], 1)
                dve.wait_ge(S["den_inv"], 1)
                dve.wait_ge(S["num_mm"], 2)
                dve.tensor_tensor(A[:, 5, :], banks(0), A[:, 3, :], ALU.mult).then_inc(S["o0_done"], 1)
                dve.wait_ge(S["proj_mm"], T)
                dve.tensor_tensor(tok(A[:, 6, :]), tiles(4), h[:, :, :], ALU.add).then_inc(S["x1_sum"], 1)
                dve.wait_ge(S["x1_sum"], 1)
                dve.tensor_tensor(tok(A[:, 6, :]), tok(A[:, 6, :]), over(biasb[:, 0, :], tens), ALU.add).then_inc(S["x1_done"], 1)
                dve.wait_ge(S["x1_done"], 1)
                norm("a2", tok(A[:, 6, :]), xn)
                hT_half("a2", 0, vecs[:, 2:3], vecs[:, 3:4])
                dve.tensor_tensor(tok(A[:, 7, :]), tok(A[:, 6, :]), over(biasb[:, 1, :], tens), ALU.add).then_inc(S["x1_bias"], 1)
                dve.wait_ge(S["x1_bias"], 1)
                dve.wait_ge(S["fc2_mm"], T)
                dve.tensor_tensor(tok(A[:, 6, :]), tiles(4), tok(A[:, 7, :]), ALU.add).then_inc(S["y0"], 1)
                dve.wait_ge(S["y0"], 1)
                dve.tensor_tensor(tok(A[:, 6, :]), tok(A[:, 6, :]), over(modb[:, 2, :], tens), ALU.mult).then_inc(S["y0_scaled"], 1)
                dve.wait_ge(S["y0_scaled"], 1)
                dve.tensor_tensor(x[:, :, :], x[:, :, :], tok(A[:, 6, :]), ALU.add).then_inc(S["xa_done"], 1)
                dve.wait_ge(S["xa_done"], 1)

                norm("b0", x, xn)
                hT_half("b0", 6, modv[:, 4:5], modv[:, 3:4])
                router("rb", E0, K0, 7, 7, 0, 1.0)
                for u in range(NHALF, CH0 * NHALF):
                    dve.wait_ge(S["up_act"], u + 1)
                    dve.wait_ge(S["bcb_mm"], u - NHALF + 1)
                    if u - NHALF >= 4:
                        dve.wait_ge(S["downb_mm"], u - 4 + 1)
                    ga_ = A[:, 2 + (u % 4) // 2, (u % 2) * HALF:(u % 2 + 1) * HALF]
                    ac_ = A[:, (u % 4) // 2, (u % 2) * HALF:(u % 2 + 1) * HALF]
                    dve.tensor_tensor(ga_, P[:, 5 + u % 2, :], ac_, ALU.mult).then_inc(S["up_gated"], 1)
                dve.wait_ge(S["downb_end"], NHALF)
                dve.tensor_tensor(tok(A[:, 4, :]), tiles(0), over(modb[:, 5, :], tens), ALU.mult).then_inc(S["yb_scaled"], 1)
                dve.wait_ge(S["yb_scaled"], 1)
                dve.tensor_tensor(x[:, :, :], x[:, :, :], tok(A[:, 4, :]), ALU.add).then_inc(S["xb_done"], 1)
                dve.wait_ge(S["xb_done"], 1)

                norm("c0", x, xn)
                modulate("c0", MODS)
                norm("c1", h, xn)
                hT_half("c1", 6, vecs[:, 4 + FC:5 + FC], vecs[:, 5 + FC:6 + FC])

                def prep(s, n):
                    dve.wait_ge(S["st_mm"], T * (n - 1) + ST_AT if not (isinstance(n, int) and n == 0) else ST_AT)
                    dve.wait_ge(S["q_hi"], n + 1)
                    dve.tensor_tensor(Qb[s][0:64, :], banks(6, 2, slice(0, 64)), Qa[s][0:64, :].bitcast(F32), ALU.subtract).then_inc(S["q_lo"], 1)
                    dve.wait_ge(S["k_hi"], n + 1)
                    dve.tensor_tensor(Kb[s][64:128, :], banks(6, 2, slice(64, 128)), Ka[s][0:64, :].bitcast(F32), ALU.subtract).then_inc(S["k_lo"], 1)
                    dve.tensor_copy(Qb[s][64:128, :], Qa[s][0:64, :].bitcast(F32)).then_inc(S["q_dup"], 1)
                    dve.tensor_copy(Kb[s][0:64, :], Ka[s][0:64, :].bitcast(F32)).then_inc(S["k_dup"], 1)
                    for t in range(T):
                        dve.wait_ge(S["max_mm"], n * T + t + 1)
                        dve.tensor_reduce(mneg[:, t:t + 1], banks(6), AX.X, ALU.max, negate=True).then_inc(S["max_red"], 1)
                    dve.wait_ge(S["max_red"], n * T + T)
                    dve.tensor_copy(mparts[:, :, 0], mneg[:, :]).then_inc(S["m_hi"], 1)
                    dve.wait_ge(S["m_hi"], n + 1)
                    dve.tensor_tensor(mparts[:, :, 1], mneg[:, :], mparts[:, :, 0], ALU.subtract).then_inc(S["m_mid"], 1)

                def sums(s, p):
                    dve.wait_ge(S["pv_done"], (2 * p + s + 1) * T + PV_AT)
                    dve.wait_ge(S["o_norm"], p + NORM_AT)
                    dve.tensor_copy(spair[64 * s:64 * s + 64, :], banks(4, 2, slice(64 - 64 * s, 128 - 64 * s))).then_inc(S["s_copied"], 1)

                def pair(p, is_last):
                    prep(1, 2 * p + 1)
                    sums(0, p)
                    if not is_last:
                        prep(0, 2 * p + 2)
                    sums(1, p)
                    dve.wait_ge(S["s_copied"], 2 * p + 2 + COPIED_AT)
                    dve.reciprocal(spair[:, :], spair[:, :]).then_inc(S["s_inv"], 1)
                    dve.wait_ge(S["s_inv"], p + 1)
                    dve.wait_ge(S["o_copied"], 2 * p + 2 + COPIED_AT)
                    dve.tensor_tensor(A[:, p, :], opair[:, :], spair[:, :], ALU.mult).then_inc(S["o_norm"], 1)

                dve.sem_inc(S["s_copied"], COPIED_AT)
                dve.sem_inc(S["o_norm"], NORM_AT)
                prep(0, 0)
                with dve.Fori(0, PAIRS - 1) as p:
                    pair(p, False)
                pair(PAIRS - 1, True)

                dve.wait_ge(S["o1_mm"], T)
                dve.tensor_tensor(h[:, :, :], tiles(0), over(modb[:, MODS + 2, :], tens), ALU.mult).then_inc(S["o1_scaled"], 1)
                dve.wait_ge(S["o1_scaled"], 1)
                dve.tensor_tensor(x[:, :, :], x[:, :, :], h[:, :, :], ALU.add).then_inc(S["xc_done"], 1)
                dve.wait_ge(S["xc_done"], 1)

                norm("d0", x, xn)
                hT_half("d0", 6, modv[:, MODS + 4:MODS + 5], modv[:, MODS + 3:MODS + 4])
                dve.memset(gate[:, 0, :, E1:E1 + 1], 0.5 / E1)
                router("rd", E1, K1N, 2, 3, 1, 0.5)

                dve.sem_inc(S["gu_done"], UNIT_AT)
                with dve.Fori(0, EX1) as n:
                    dve.wait_ge(S["w3_mm"], n * UNITS + W3_AT)
                    for i in range(NHALF):
                        dve.wait_ge(S["bcd_mm"], n * NHALF + i + 1)
                        dve.tensor_tensor(half(A[:, 0, :], i), P[:, 6 + i, :], half(hT, i), ALU.mult).then_inc(S["hg_done"], 1)
                    for u in range(UNITS):
                        i = u % 2
                        dve.wait_ge(S["w3_mm"], n * UNITS + u + 1 + W3_AT)
                        dve.wait_ge(S["silu_done"], n * UNITS + u + 1 + UNIT_AT)
                        dve.wait_ge(S["downd_mm"], n * UNITS + u - 1 + UNIT_AT)
                        dve.tensor_tensor(half(A[:, 2, :], i), P[:, 4 + i, :], half(A[:, 1, :], i), ALU.mult).then_inc(S["gu_done"], 1)
                dve.wait_ge(S["downd_end"], NHALF)
                dve.tensor_tensor(h[:, :, :], tiles(0), over(modb[:, MODS + 5, :], tens), ALU.mult).then_inc(S["yd_scaled"], 1)
                dve.wait_ge(S["yd_scaled"], 1)
                dve.tensor_tensor(x[:, :, :], x[:, :, :], h[:, :, :], ALU.add).then_inc(S["xd_done"], 1)
                end_batch(dve, b)

        @block.scalar
        def _(act):
            act.wait_ge(G["weights_in"], 16 * NLOAD)
            act.activation(cs[:, :, :], cT[:, :, :], ACT.Silu).then_inc(G["c_silu"], 1)

            def hT_half(tag, bank, scale, bias):
                act.wait_ge(S["vec_copied"], 1)
                act.wait_ge(S["turned"], NHALF * TR_TAGS.index(tag) + 2)
                act.activation(half(hT, 1), P[:, bank + 1, :], ACT.Identity, bias=bias, scale=scale).then_inc(S["hT_act"], 1)

            act.wait_ge(G["set_done"], NSET)
            act.wait_ge(G["pool_set"], NPOOL)
            with act.Fori(0, B) as b:
                hT_half("a1", 0, vecs[:, 0:1], vecs[:, 1:2])
                act.wait_ge(S["q0_min"], 1)
                act.activation(A[:, 1, :], A[:, 0, :], ACT.Exp).then_inc(S["q0_exp"], 1)
                act.wait_ge(S["k0_min"], 1)
                act.activation(A[:, 3, :], A[:, 2, :], ACT.Exp).then_inc(S["k0_exp"], 1)
                hT_half("a2", 0, vecs[:, 2:3], vecs[:, 3:4])
                for u in range(FC * NHALF):
                    c, i = u // NHALF, u % NHALF
                    act.wait_ge(S["fc1_mm"], u + 1)
                    act.activation(half(A[:, c, :], i), P[:, 2 + u % 2, :], ACT.Gelu, bias=vecs[:, 4 + c:5 + c]).then_inc(S["fc1_act"], 1)
                hT_half("b0", 6, modv[:, 4:5], modv[:, 3:4])
                act.wait_ge(S["rb_sub"], 1)
                act.activation(rexp[:, :, 0:E0], rlog[:, :, 0:E0], ACT.Exp).then_inc(S["rb_exp"], 1)
                for u in range(CH0 * NHALF):
                    act.wait_ge(S["up_mm"], u + 1)
                    if u >= 4:
                        if u - 4 < NHALF:
                            act.wait_ge(S["downb_mm"], u - 4 + 1)
                        else:
                            act.wait_ge(S["up_gated"], u - 4 - NHALF + 1)
                    act.activation(A[:, (u % 4) // 2, (u % 2) * HALF:(u % 2 + 1) * HALF], P[:, 2 + u % 3, :], ACT.Gelu).then_inc(S["up_act"], 1)
                hT_half("c1", 6, vecs[:, 4 + FC:5 + FC], vecs[:, 5 + FC:6 + FC])

                def values(s, n):
                    act.wait_ge(S["st_mm"], ST_AT if isinstance(n, int) and n == 0 else T * (n - 1) + ST_AT)
                    act.wait_ge(S[f"aux_in{s}"], 8 * (n - s) + 16)
                    act.activation(Ka[s][64:96, :], auxin[64:96, :], ACT.Copy).then_inc(S["k_aux"], 1)
                    act.wait_ge(S["v_mm"], n + 1)
                    act.wait_ge(S["pv_done"], PV_AT if isinstance(n, int) and n == 0 else T * (n - 1) + PV_AT)
                    act.activation(V[s][:, :, 64 * s:64 * s + 64], P[:, 6, :].rearrange("p (t d) -> p t d", d=DH1), ACT.Copy).then_inc(S["v_in"], 1)

                def high_parts(s, n):
                    act.wait_ge(S["qk_mm"], n + 1)
                    act.activation(Qa[s][0:64, :], banks(6, 2, slice(0, 64)), ACT.Copy).then_inc(S["q_hi"], 1)
                    act.activation(Ka[s][0:64, :], banks(6, 2, slice(64, 128)), ACT.Copy).then_inc(S["k_hi"], 1)

                def maxima(s, n):
                    act.wait_ge(S["m_row"], n + 1)
                    act.activation(Qa[s][MROW:MROW + 2, :], banks(6, 2, slice(0, 2)), ACT.Copy).then_inc(S["m_in"], 1)

                def exps(k, j):
                    act.wait_ge(S["st_mm"], k + 1 + ST_AT)
                    act.wait_ge(S["pv_done"], k + 1 - RING + PV_AT)
                    act.activation(pt[:, j % RING, :], banks(2 * (j % 2)), ACT.Exp, scale=DH1 ** -0.5).then_inc(S["exp_done"], 1)

                def outputs(s, p):
                    act.wait_ge(S["pv_done"], (2 * p + s + 1) * T + PV_AT)
                    act.wait_ge(S["o_norm"], p + NORM_AT)
                    act.activation(opair[64 * s:64 * s + 64, :], banks(4, 2, slice(64 * s, 64 * s + 64)), ACT.Copy).then_inc(S["o_copied"], 1)

                def pair(p, is_last):
                    for j in range(2 * T):
                        s, n = j // T, 2 * p + 1 + j // T
                        ahead = not (is_last and s == 1)
                        if ahead and j % T == 0:
                            values(1 - s, n)
                        if ahead and j % T == 1:
                            high_parts(1 - s, n)
                        if ahead and j % T == T - 1:
                            maxima(1 - s, n)
                        if j % T == T - 1:
                            outputs(s, p)
                        if not (is_last and j == 2 * T - 1):
                            exps(2 * T * p + j + 1, j + 1)

                act.sem_inc(S["exp_done"], EXP_AT)
                act.sem_inc(S["o_copied"], COPIED_AT)
                act.wait_ge(S["hT_act"], TR_TAGS.index("c1") + 1)
                values(0, 0)
                high_parts(0, 0)
                maxima(0, 0)
                exps(0, 0)
                with act.Fori(0, PAIRS - 1) as p:
                    pair(p, False)
                pair(PAIRS - 1, True)

                hT_half("d0", 6, modv[:, MODS + 4:MODS + 5], modv[:, MODS + 3:MODS + 4])
                act.wait_ge(S["rd_sub"], 1)
                act.activation(rexp[:, :, 0:E1], rlog[:, :, 0:E1], ACT.Exp).then_inc(S["rd_exp"], 1)
                act.sem_inc(S["silu_done"], UNIT_AT)
                with act.Fori(0, EX1) as n:
                    for u in range(UNITS):
                        i = u % 2
                        act.wait_ge(S["w1_mm"], n * UNITS + u + 1)
                        act.wait_ge(S["gu_done"], n * UNITS + u - 1 + UNIT_AT)
                        act.activation(half(A[:, 1, :], i), P[:, 2 + i, :], ACT.Silu).then_inc(S["silu_done"], 1)
                end_batch(act, b)

        @block.tensor
        def _(pe):
            pe.wait_ge(G["weights_in"], 16 * NLOAD)
            wmod = modb[:, :, :].rearrange("p a b -> p (a b)")
            pe.wait_ge(G["c_silu"], 1)
            for i, l in ((0, 0), (1, 0), (1, 1), (2, 1)):
                lo, hi = max(i * HALF, l * MODS * D), min((i + 1) * HALF, (l + 1) * MODS * D)
                mm = pe.matmul(P[0:B, i, lo - i * HALF:hi - i * HALF], cs[:, l, :], wmod[:, lo:hi], start=True, stop=True)
            mm.then_inc(G["mod_mm"], 1)
            for m in range(2 * MODS):
                mm = pe.matmul(P[:, 3, m * B:(m + 1) * B], wmod[:, m * D:(m + 1) * D], cs[:, m // MODS, :], start=True, stop=True)
            mm.then_inc(G["modT_mm"], 1)
            pe.wait_ge(G["modT_copied"], 2)
            pe.wait_ge(G["mod_one"], 1)
            pe.wait_ge(G["set_done"], NSET)
            pe.wait_ge(G["pool_set"], NPOOL)

            def turn(tag, bank):
                for t in range(T):
                    pe.wait_ge(S["ln_norm"], LN_TAGS.index(tag) * T + t + 1)
                    tr = pe.transpose(bank_t(bank, t), xn[:, t, :], identf[:, :])
                    if t % TPH == TPH - 1:
                        tr.then_inc(S["turned"], 1)
                pe.wait_ge(S["hT_dve"], TR_TAGS.index(tag) + 1)
                pe.wait_ge(S["hT_act"], TR_TAGS.index(tag) + 1)

            def tile(t_, t):
                return t_[:, t * 128:(t + 1) * 128]

            def route(tag, n, w, bank):
                for t in range(T):
                    mm = pe.matmul(P[:, bank, t * n:(t + 1) * n], tile(hT, t), w, start=True, stop=True)
                mm.then_inc(S[f"{tag}_mm"], 1)

            def turn_gates(tag, bank):
                pe.wait_ge(S[f"{tag}_lo"], 1)
                rows = P[0:3 * GW, bank, :].bitcast(BF16)
                for t in range(T):
                    tr = pe.transpose(rows[:, t * 128:(t + 1) * 128], gparts[:, t, :], identb[:, :])
                tr.then_inc(S[f"{tag}_turned"], 1)

            def zero(bank):
                pe.matmul(P[:, bank, :], zerob[:, 0:128], zerob[:, :], start=True, stop=False)

            def close(bank):
                return pe.matmul(P[:, bank, :], zerob[:, 0:128], zerob[:, :], start=False, stop=True)

            with pe.Fori(0, B) as b:
                turn("a1", 0)
                for i in range(NHALF):
                    pe.matmul(P[:, i, :], wqkv0[:, 0:D], half(hT, i), start=True, stop=True).then_inc(S["q0_mm"], 1)
                for t in range(T):
                    pe.matmul(P[:, 2 + t // 2, (t % 2) * 2 * D:(t % 2 + 1) * 2 * D], tile(hT, t), wqkv0[:, D:3 * D],
                              start=True, stop=True).then_inc(S["k0_mm"], 1)
                pe.wait_ge(S["k0_done"], 1)
                for t in range(T):
                    if t == 0:
                        pe.wait_ge(S["v0_copied"], 1)
                    mm = pe.matmul(P[:, 6, 0:D], tile(A[:, 2, :], t), tile(A[:, 4, :], t), start=(t == 0), stop=(t == T - 1))
                mm.then_inc(S["kv_mm"], 1)
                for t in range(T):
                    mm = pe.matmul(P[:, 7, 0:1], tile(A[:, 2, :], t), onecol[:, :], start=(t == 0), stop=(t == T - 1))
                mm.then_inc(S["ks_mm"], 1)
                pe.wait_ge(S["q0_done"], 1)
                pe.wait_ge(S["ks_masked"], 1)
                for i in range(NHALF):
                    pe.matmul(P[:, 2 + i, :], small[:, 1, :], half(A[:, 0, :], i), start=True, stop=True).then_inc(S["den_mm"], 1)
                pe.wait_ge(S["kv_masked"], 1)
                for i in range(NHALF):
                    pe.matmul(P[:, i, :], small[:, 0, :], half(A[:, 0, :], i), start=True, stop=True).then_inc(S["num_mm"], 1)
                pe.wait_ge(S["o0_done"], 1)
                for t in range(T):
                    pe.matmul(bank_t(4, t), tile(A[:, 5, :], t), wproj[:, :], start=True, stop=True).then_inc(S["proj_mm"], 1)
                turn("a2", 0)
                for u in range(FC * NHALF):
                    c, i = u // NHALF, u % NHALF
                    if u >= 2:
                        pe.wait_ge(S["fc1_act"], u - 1)
                    pe.matmul(P[:, 2 + u % 2, :], wfc1[:, c * 128:(c + 1) * 128], half(hT, i), start=True, stop=True).then_inc(S["fc1_mm"], 1)
                pe.wait_ge(S["fc1_act"], FC * NHALF)
                for t in range(T):
                    for c in range(FC):
                        mm = pe.matmul(bank_t(4, t), tile(A[:, c, :], t), wfc2[:, c, :], start=(c == 0), stop=(c == FC - 1))
                    mm.then_inc(S["fc2_mm"], 1)

                turn("b0", 6)
                route("rb", E0, wrout[:, :], 7)
                zero(0)
                zero(1)

                def up(u):
                    if u >= 3:
                        pe.wait_ge(S["up_act"], u - 2)
                    pe.matmul(P[:, 2 + u % 3, :], wup[:, u // NHALF, :], half(hT, u % 2), start=True, stop=True).then_inc(S["up_mm"], 1)

                def spread(u):
                    if u - NHALF >= 2:
                        pe.wait_ge(S["up_gated"], u - NHALF - 1)
                    pe.matmul(P[:, 5 + u % 2, :], selb[:, u // NHALF - 1, :], half(grows, u % 2), start=True, stop=True).then_inc(S["bcb_mm"], 1)

                def down(u):
                    if u < NHALF:
                        pe.wait_ge(S["up_act"], u + 1)
                    else:
                        pe.wait_ge(S["up_gated"], u - NHALF + 1)
                    f = A[:, (0 if u < NHALF else 2) + (u % 4) // 2, (u % 2) * HALF:(u % 2 + 1) * HALF]
                    for t in range(TPH):
                        mm = pe.matmul(bank_t(0, u % 2 * TPH + t), tile(f, t), wdown[:, u // NHALF, :],
                                       start=False, stop=False)
                    mm.then_inc(S["downb_mm"], 1)

                up(0)
                up(1)
                down(0)
                up(2)
                down(1)
                turn_gates("rb", 7)
                pe.wait_ge(S["rb_rows"], 1)
                spread(2)
                for u in range(2, CH0 * NHALF):
                    if u + 1 < CH0 * NHALF:
                        up(u + 1)
                        spread(u + 1)
                    down(u)
                close(0).then_inc(S["downb_end"], 1)
                close(1).then_inc(S["downb_end"], 1)

                turn("c1", 6)

                def project_v(s, n):
                    pe.wait_ge(S[f"wh_in{s}"], 8 * (n - s) + 16)
                    if not isinstance(n, int) or n > 0:
                        pe.wait_ge(S["m_in"], n)
                    for t in range(T):
                        mm = pe.matmul(P[:, 6, t * DH1:(t + 1) * DH1], tile(hT, t), whead[s][:, 2 * DH1:3 * DH1], start=True, stop=True)
                    mm.then_inc(S["v_mm"], 1)

                def project_qk(s, n):
                    pe.wait_ge(S["v_in"], n + 1)
                    for i in range(NHALF):
                        mm = pe.matmul(P[:, 6 + i, :], whead[s][:, 0:2 * DH1], half(hT, i), start=True, stop=True)
                    mm.then_inc(S["qk_mm"], 1)

                def near(out, n, parts, stop):
                    for part in range(parts):
                        mm = pe.matmul(out, distb[:, :], diagb[:, 3 * n + part, :], start=False, stop=(stop and part == parts - 1))
                    return mm

                def max_tile(s, n, t):
                    if t == 0:
                        pe.wait_ge(S["k_aux"], n + 1)
                        pe.wait_ge(S["k_lo"], n + 1)
                    else:
                        pe.wait_ge(S["max_red"], n * T + t)
                    for i in (1 - t // TPH, t // TPH):
                        mine = i == t // TPH
                        mm = pe.matmul(P[:, 6 + i, :], tile(Qa[s][0:MROW, :], t), half(Ka[s][0:MROW, :], i), start=True, stop=not mine)
                    mm = near(P[:, 6 + t // TPH, (t % TPH) * 128:(t % TPH + 1) * 128], n, 1, True)
                    mm.then_inc(S["max_mm"], 1)

                def turn_max(n):
                    pe.wait_ge(S["m_mid"], n + 1)
                    for t in range(T):
                        mm = pe.matmul(P[0:2, 6 + t // TPH, (t % TPH) * 128:(t % TPH + 1) * 128], mparts[:, t, :], identb[:, :], start=True, stop=True)
                    mm.then_inc(S["m_row"], 1)

                def scores(k, j, s, n):
                    if j == 0:
                        pe.wait_ge(S["m_in"], n + 1)
                        pe.wait_ge(S["k_dup"], n + 1)
                    if not isinstance(k, int) or k > 0:
                        pe.wait_ge(S["exp_done"], k - 1 + EXP_AT)
                    bank = 2 * (j % 2)
                    for i in (1 - j // TPH, j // TPH):
                        pe.matmul(P[:, bank + i, :], tile(Ka[s][0:KEXACT, :], j), half(Qa[s][0:KEXACT, :], i), start=True, stop=False)
                        if i == j // TPH:
                            near(P[:, bank + i, (j % TPH) * 128:(j % TPH + 1) * 128], n, 3, False)
                        mm = pe.matmul(P[:, bank + i, :], tile(Kb[s], j), half(Qb[s], i), start=False, stop=True)
                    mm.then_inc(S["st_mm"], 1)

                def weigh(k, j, s, n):
                    pe.wait_ge(S["exp_done"], k + 1 + EXP_AT)
                    if j == 0:
                        pe.wait_ge(S["v_in"], n + 1)
                        pe.wait_ge(S["o_copied"], n + COPIED_AT)
                        pe.wait_ge(S["s_copied"], n + COPIED_AT)
                    for i in range(NHALF):
                        mm = pe.matmul(P[:, 4 + i, :], V[s][:, j, :], half(pt[:, j % RING, :], i), start=(j == 0), stop=(j == T - 1))
                    mm.then_inc(S["pv_done"], 1)

                def pair(p, is_last):
                    for j in range(2 * T):
                        k, s, jj = 2 * T * p + j, j // T, j % T
                        n = 2 * p + s
                        ahead = not (is_last and s == 1)
                        if ahead and jj == 0:
                            project_v(1 - s, n + 1)
                        if ahead and jj == 1:
                            project_qk(1 - s, n + 1)
                        if ahead and 3 <= jj < 7:
                            max_tile(1 - s, n + 1, 2 * (jj - 3))
                        if jj < T - 1:
                            scores(k + 1, jj + 1, s, n)
                        if ahead and 3 <= jj < 7:
                            max_tile(1 - s, n + 1, 2 * (jj - 3) + 1)
                        if ahead and jj == T - 1:
                            turn_max(n + 1)
                        weigh(k, jj, s, n)
                        if ahead and jj == T - 1:
                            scores(k + 1, 0, 1 - s, n + 1)

                pe.sem_inc(S["st_mm"], ST_AT)
                pe.sem_inc(S["pv_done"], PV_AT)
                project_v(0, 0)
                project_qk(0, 0)
                for t in range(T):
                    max_tile(0, 0, t)
                turn_max(0)
                scores(0, 0, 0, 0)
                with pe.Fori(0, PAIRS - 1) as p:
                    pair(p, False)
                pair(PAIRS - 1, True)

                pe.wait_ge(S["o_norm"], PAIRS + NORM_AT)
                for t in range(T):
                    for c in range(PAIRS):
                        mm = pe.matmul(bank_t(0, t), tile(A[:, c, :], t), wo[:, c, :], start=(c == 0), stop=(c == PAIRS - 1))
                    mm.then_inc(S["o1_mm"], 1)

                turn("d0", 6)
                route("rd", E1, wgate[:, :], 2)
                zero(0)
                zero(1)
                turn_gates("rd", 3)
                pe.wait_ge(S["rd_rows"], 1)
                pe.sem_inc(S["w3_mm"], W3_AT)
                pe.sem_inc(S["downd_mm"], UNIT_AT)

                def spread_gate(n):
                    for i in range(NHALF):
                        pe.matmul(P[:, 6 + i, :], seld[:, n, :], half(grows, i), start=True, stop=True).then_inc(S["bcd_mm"], 1)

                def down_unit(n, u, w):
                    c, i = u // NHALF, u % NHALF
                    pe.wait_ge(S["gu_done"], n * UNITS + u + 1 + UNIT_AT)
                    for t in range(TPH):
                        mm = pe.matmul(bank_t(0, i * TPH + t), tile(half(A[:, 2, :], i), t), w[:, 2 * F1 + c * 128:2 * F1 + (c + 1) * 128],
                                       start=False, stop=False)
                    mm.then_inc(S["downd_mm"], 1)

                spread_gate(0)
                with pe.Fori(0, EX1 // WBUF) as r:
                    for q in range(WBUF):
                        n, w = r * WBUF + q, wex[q]
                        pe.wait_ge(S[f"w1_in{q}"], r * 16 + 16)
                        for u in range(UNITS):
                            c, i = u // NHALF, u % NHALF
                            pe.wait_ge(S["silu_done"], n * UNITS + u - 1 + UNIT_AT)
                            pe.matmul(P[:, 2 + i, :], w[:, c * 128:(c + 1) * 128], half(hT, i), start=True, stop=True).then_inc(S["w1_mm"], 1)
                            if u < NHALF:
                                pe.wait_ge(S["hg_done"], n * NHALF + i + 1)
                            pe.wait_ge(S["gu_done"], n * UNITS + u - 1 + UNIT_AT)
                            pe.matmul(P[:, 4 + i, :], w[:, F1 + c * 128:F1 + (c + 1) * 128], half(A[:, 0, :], i), start=True, stop=True).then_inc(S["w3_mm"], 1)
                            if u > 0:
                                down_unit(n, u - 1, w)
                        spread_gate(n + 1)
                        down_unit(n, UNITS - 1, w)
                close(0).then_inc(S["downd_end"], 1)
                close(1).then_inc(S["downd_end"], 1)
                end_batch(pe, b)


def kernel(**inputs):
    import concourse.bacc as bacc
    from concourse.bass_utils import run_bass_kernel_spmd as run

    g = {k: np.asarray(v) for k, v in inputs.items()}
    consts, aux = constants()
    flat = lambda w: np.ascontiguousarray(w)
    per_chunk = lambda w: flat(w.reshape(-1, 128, w.shape[-1]).transpose(1, 0, 2))

    def heads(w):
        return w.reshape(D, H1, DH1).transpose(1, 0, 2)

    shared_w1, shared_w3 = (g[n].transpose(1, 0, 2).reshape(D, F1) for n in ("L1_ffn_w1_s", "L1_ffn_w3_s"))
    w1 = np.concatenate([g["L1_ffn_w1_e"], shared_w1[None]])
    w3 = np.concatenate([g["L1_ffn_w3_e"], shared_w3[None]])
    w2 = np.concatenate([g["L1_ffn_w2_e"], g["L1_ffn_w2_s"].reshape(1, F1, D)])
    w2 = w2.reshape(EX1, FCH, 128, D).transpose(0, 2, 1, 3).reshape(EX1, 128, F1)
    up = np.concatenate([g["L0_ffn_shared_up"], g["L0_ffn_routed_up"]]).reshape(CH0, 128, D)
    down = np.concatenate([g["L0_ffn_shared_down"], g["L0_ffn_routed_down"]]).transpose(0, 2, 1).reshape(CH0, 128, D)
    arrays = {
        "x": flat(g["L0_attn_x"].reshape(B, T, 128, D).transpose(0, 2, 1, 3)),
        "consts": consts, "aux": aux,
        "wqkv0": flat(g["L0_attn_qkv_w"].T), "wproj": flat(g["L0_attn_proj_w"].T),
        "wfc1": flat(g["L0_attn_fc1_w"].T), "wfc2": per_chunk(g["L0_attn_fc2_w"].T),
        "wup": flat(up.transpose(2, 0, 1)), "wdown": flat(down.transpose(1, 0, 2)),
        "wrout": flat(g["L0_ffn_router_w"].T), "wgate": flat(g["L1_ffn_gate_W"].T),
        "wo": per_chunk(g["L1_attn_Wo"]),
        "vecs": flat(np.stack([g["L0_attn_norm1_g"], g["L0_attn_norm1_b"], g["L0_attn_norm2_g"], g["L0_attn_norm2_b"],
                               *g["L0_attn_fc1_b"].reshape(FC, 128), g["L1_attn_ln_gamma"], g["L1_attn_ln_beta"]], axis=1)),
        "biases": flat(np.stack([g["L0_attn_proj_b"], g["L0_attn_fc2_b"]])),
        "wmod": flat(np.concatenate([g["L0_wmod"], g["L1_wmod"]], axis=1)),
        "cT": flat(np.stack([g["L0_c"].T, g["L1_c"].T], axis=1)),
        "whead": flat(np.concatenate([heads(g["L1_attn_Wq"]), heads(g["L1_attn_Wk"]), heads(g["L1_attn_Wv"])], axis=2)),
        "wex": flat(np.concatenate([w1, w3, w2], axis=2)),
    }
    nc = bacc.Bacc("TRN2", target_bir_lowering=False, num_devices=1)
    a = {n: nc.dram_tensor(f"in_{n}", v.shape, F32, kind="ExternalInput").ap() for n, v in arrays.items()}
    a["out"] = nc.dram_tensor("out_x", [B, 128, T, D], F32, kind="ExternalOutput").ap()
    a["modrows"] = nc.dram_tensor("modrows", [B, 2 * MODS * D], F32).ap()
    network(nc, a)
    r = run(nc, [{f"in_{n}": v for n, v in arrays.items()}], core_ids=[0])
    return r.results[0]["out_x"].transpose(0, 2, 1, 3).reshape(B, N, D)
```

```python
from contextlib import ExitStack

import numpy as np

import concourse.bass as bass
from concourse import mybir

F32 = mybir.dt.float32
F32R = mybir.dt.float32r
BF16 = mybir.dt.bfloat16
ACT = mybir.ActivationFunctionType
ALU = mybir.AluOpType
AX = mybir.AxisListType

B, N, D = 4, 1024, 128
T = N // 128
HALF = 512
NHALF = N // HALF
TPH = T // NHALF
EPS_LN = 1e-5
EPS_ATTN = 1e-6
H0, DH0 = 16, 8
HID = 512
FC = HID // 128
E0, K0, SH0 = 16, 4, 2
CH0 = (E0 + SH0) // 2
H1, DH1 = 16, 64
PAIRS = H1 // 2
E1, K1N, F1 = 8, 2, 512
EX1 = E1 + 1
FCH = F1 // 128
UNITS = FCH * NHALF
WBUF = 2
NEXT = 3
RING = 4
NCHUNK = T // 2
MODS = 6
GW = 16
NAUX = 32
MROW = 96
KEXACT = MROW + 2
ST_AT, EXP_AT, PV_AT, COPIED_AT, NORM_AT, UNIT_AT, PLOW_AT = 1, 1, RING, 1, 1, 2, 1

MAX_TILES = [([], []), ([], []), ([], []), ([0], [1]), ([2], [3]), ([4], [5]), ([6], [7]), ([], [])]

C_IDENT, C_DIST, C_MASK, C_SLOPE = 0, 128, 256, 384
C_SELB = C_SLOPE + 3 * H1
C_SELD = C_SELB + (CH0 - 1) * 128
C_AUXQ = C_SELD + (EX1 + 1) * 128
C_END = C_AUXQ + N


def split12(x):
    x = x.astype(np.float32)
    c = (x * np.float32(4097)).astype(np.float32)
    hi = (c - (c - x)).astype(np.float32)
    return hi, (x - hi).astype(np.float32)


def cut8(x):
    return (x.astype(np.float32).view(np.uint32) & np.uint32(0xFFFF0000)).view(np.float32)


def constants():
    c = np.zeros((128, C_END), np.float32)
    i = np.arange(128)
    c[:, C_IDENT:C_IDENT + 128] = np.eye(128)
    c[:, C_DIST:C_DIST + 128] = -np.abs(i[:, None] - i[None, :])
    c[:, C_MASK:C_MASK + 128] = (i[:, None] // DH0) == (i[None, :] // DH0)
    slope = (np.float32(2.0) ** (np.float32(-8.0) / np.arange(H1, 0, -1).astype(np.float32))).astype(np.float32)
    s8 = slope * np.float32(DH1 ** 0.5)
    a = cut8(s8)
    m = cut8(s8 - a)
    for h in range(H1):
        c[:, C_SLOPE + 3 * h:C_SLOPE + 3 * h + 3] = [a[h], m[h], s8[h] - a[h] - m[h]]
    for k in range(CH0 - 1):
        for part in range(3):
            c[part * GW + 2 * k, C_SELB + 128 * k:C_SELB + 128 * k + 64] = 1
            c[part * GW + 2 * k + 1, C_SELB + 128 * k + 64:C_SELB + 128 * k + 128] = 1
    for e in range(EX1):
        for part in range(3):
            c[part * GW + e, C_SELD + 128 * e:C_SELD + 128 * e + 128] = 1
    for t in range(T):
        cols = slice(C_AUXQ + 128 * t, C_AUXQ + 128 * t + 128)
        c[64 + t, cols] = 1
        c[64 + T + t, cols] = 1
        c[64 + 2 * T + t, cols] = i
        c[64 + 3 * T + t, cols] = i
    aux = np.zeros((H1, NAUX, N), np.float32)
    j = np.arange(N)
    for t in range(T):
        d = t - j // 128
        base = (-np.sign(d) * (128 * d - j % 128)).astype(np.float32)
        for h in range(H1):
            aux[h, t], aux[h, T + t] = split12(s8[h] * base)
            aux[h, 2 * T + t], aux[h, 3 * T + t] = split12(-s8[h] * np.sign(d).astype(np.float32))
    return c, aux


LN_TAGS = ["a0", "a1", "a2", "b0", "c0", "c1", "d0"]
TR_TAGS = ["a1", "a2", "b0", "c1", "d0"]
BATCH_SEMS = (
    ["ln_moments", "ln_eps", "ln_rstd", "ln_norm", "modulated", "turned", "hT_dve", "hT_act",
     "x_in", "mod_in", "vec_copied", "x_out"]
    + ["q0_mm", "k0_mm", "q0_min", "k0_min", "q0_exp", "k0_exp", "q0_done", "k0_done", "v0_copied",
       "kv_mm", "ks_mm", "kv_masked", "ks_masked", "num_mm", "den_mm", "den_eps", "den_inv", "o0_done",
       "proj_mm", "x1_sum", "x1_done", "x1_bias", "fc1_mm", "fc1_act", "fc2_mm", "y0", "y0_scaled", "xa_done"]
    + [f"{t}_{n}" for t in ("rb", "rd") for n in ("mm", "sub", "exp", "steps", "lo", "turned", "rows")]
    + ["up_mm", "bcb_mm", "up_act", "up_gated", "downb_mm", "downb_end", "yb_scaled", "xb_done"]
    + ["o1_mm", "o1_scaled", "xc_done"]
    + ["w1_in0", "w1_in1", "gates_in", "silu_gated", "bcd_mm", "w1_mm", "w3_mm", "silu_done", "gu_done",
       "hT_high", "hT_low", "w_high", "w_low", "gu_high", "gu_low", "ydT_copied", "yd_turned",
       "downd_mm", "downd_end", "yd_scaled", "xd_done"]
    + ["wh_in0", "wh_in1", "aux_in0", "aux_in1", "v_mm", "v_high", "v_low", "p_high", "p_low", "qk_mm", "q_hi", "k_hi", "k_aux",
       "k_dup", "k_lo", "q_dup", "q_lo", "max_mm", "max_red", "max_both", "m_hi", "m_mid", "m_row", "m_in",
       "st_mm", "exp_done", "pv_done", "o_copied", "s_copied", "s_inv", "o_norm"]
)


def network(nc, a):
    ctx = ExitStack()
    with ctx:
        def sb(name, shape, dt=F32):
            return ctx.enter_context(nc.sbuf_tensor(name, shape, dt))

        S = {n: ctx.enter_context(nc.semaphore(n)) for n in BATCH_SEMS}
        first, last = S[BATCH_SEMS[0]].num, S[BATCH_SEMS[-1]].num
        assert last - first == len(BATCH_SEMS) - 1
        G = {n: ctx.enter_context(nc.semaphore(n)) for n in
             ("weights_in", "consts_in", "c_silu", "mod_mm", "modT_mm", "mod_abs", "mod_sgn",
              "mod_pm", "mod_one", "mod_out", "modT_copied", "set_done", "pool_set", "batch_ended", "batch_open", "passed")}

        wqkv0 = sb("wqkv0", [128, 3 * D])
        wproj = sb("wproj", [128, D])
        wfc1 = sb("wfc1", [128, HID])
        wfc2 = sb("wfc2", [128, FC, D])
        wup = sb("wup", [128, CH0, 128])
        wdown = sb("wdown", [128, CH0, D])
        wrout = sb("wrout", [128, E0])
        wgate = sb("wgate", [128, E1])
        wo = sb("wo", [128, PAIRS, D])
        vecs = sb("vecs", [128, 4 + FC + 2])
        biasb = sb("biasb", [128, 2, D])
        identf = sb("identf", [128, 128])
        identb = sb("identb", [128, 128], BF16)
        distb = sb("distb", [128, 128], BF16)
        mask = sb("mask", [128, 128])
        diagb = sb("diagb", [128, 3 * H1, 128], BF16)
        selb = sb("selb", [128, CH0 - 1, 128], BF16)
        seld = sb("seld", [128, EX1 + 1, 128], BF16)
        zerob = sb("zerob", [128, HALF], BF16)
        onecol = sb("onecol", [128, 1])
        halfneg = sb("halfneg", [128, T])
        modT = sb("modT", [128, 2 * MODS, B])
        modv = sb("modv", [128, 2 * MODS])
        modb = sb("modb", [128, 2 * MODS, D])
        x = sb("x", [128, T, D])
        xn = sb("xn", [128, T, D])
        h = sb("h", [128, T, D])
        hT = sb("hT", [128, N])
        A = sb("A", [128, 8, N])
        cT = sb("cT", [128, 2, B])
        cs = sb("cs", [128, 2, B])
        stats = sb("stats", [128, T, 6])
        mv = sb("mv", [128, T, 2])
        veps = sb("veps", [128, T])
        rstd = sb("rstd", [128, T])
        rmax = sb("rmax", [128, 3, T])
        rlog = sb("rlog", [128, T, GW])
        rexp = sb("rexp", [128, T, GW])
        prob = sb("prob", [128, 2, T, GW + 8])
        top8 = sb("top8", [128, T, 8])
        hit = sb("hit", [128, T, GW + 8])
        gate = sb("gate", [128, 3, T, GW])
        gparts = sb("gparts", [128, T, 3 * GW], BF16)
        grows = sb("grows", [128, N], BF16)
        whead = [sb(f"whead{s}", [128, 3 * DH1]) for s in range(2)]
        auxin = sb("auxin", [96, N])
        Ka = [sb(f"Ka{s}", [128, N], F32R) for s in range(2)]
        Kb = [sb(f"Kb{s}", [128, N], F32R) for s in range(2)]
        Qa = [sb(f"Qa{s}", [128, N], F32R) for s in range(2)]
        Qb = [sb(f"Qb{s}", [128, N], F32R) for s in range(2)]
        Vh = [sb(f"Vh{s}", [128, T, 128], F32R) for s in range(2)]
        Vl = [sb(f"Vl{s}", [128, T, 128], F32R) for s in range(2)]
        pfull = sb("pfull", [128, 2, N])
        R = sb("R", [128, RING + 2, N], F32R)
        opair = sb("opair", [128, N])
        spair = sb("spair", [128, N])
        small = opair[:, 0:256].rearrange("p (a b) -> p a b", b=128)
        mhalf = sb("mhalf", [128, NHALF, T])
        mneg = sb("mneg", [128, T])
        mparts = sb("mparts", [128, T, 2], BF16)
        wex = [sb(f"wex{i}", [128, 3 * F1]) for i in range(WBUF)]

        P = ctx.enter_context(nc.psum_tensor("P", [128, 8, HALF], F32))

        phigh = [R[:, i, :] for i in range(RING)]
        plow = [R[:, RING + i, :] for i in range(2)]
        rows_r = R[:, :, :].rearrange("p a b -> p (a b)")
        wh, wl = ([rows_r[:, (2 * j + i) * 3 * F1:(2 * j + i + 1) * 3 * F1] for i in range(WBUF)] for j in range(2))
        hTh, hTl = Kb[0], Qb[0]
        guh, gul = Kb[1], Qb[1]
        gatesb = [opair, spair]
        silu, gsilu, gu = A[:, 0, :], A[:, 1, :], A[:, 2, :]

        def banks(i, n=2, rows=slice(0, 128)):
            return P[rows, i:i + n, :].rearrange("p a b -> p (a b)")

        def tiles(i):
            return P[:, i:i + 2, :].rearrange("p a (t d) -> p (a t) d", d=D)

        def half(t, i):
            return t[:, i * HALF:(i + 1) * HALF]

        def tok(t):
            return t.rearrange("p (t d) -> p t d", d=D)

        def over(v, shape):
            return v.unsqueeze(1).to_broadcast(shape)

        def col(v, n):
            return v.unsqueeze(2).to_broadcast([128, T, n])

        vpsum = P[:, 6, :].rearrange("p (t d) -> p t d", d=DH1)

        def bank_t(i, t):
            return P[:, i + t // TPH, (t % TPH) * D:(t % TPH + 1) * D]

        def end_batch(e, b):
            e.drain().then_inc(G["batch_ended"], 1)
            v = e.snap(b + 1)
            e.wait_ge(G["batch_open"], v)
            e.sem_inc(G["passed"], 1)

        block = ctx.enter_context(nc.Block())
        NLOAD = 13
        NSET, NPOOL = 2, 10

        @block.sync
        def _(sp):
            sp.dma_start(A[:, 0:5, :].rearrange("p a b -> p (a b)")[:, 0:C_END], a["consts"]).then_inc(G["consts_in"], 16)
            for dst, src in ((wqkv0[:, :], a["wqkv0"]), (wproj[:, :], a["wproj"]), (wfc1[:, :], a["wfc1"]),
                             (wfc2[:, :, :], a["wfc2"]), (wup[:, :, :], a["wup"]), (wdown[:, :, :], a["wdown"]),
                             (wrout[:, :], a["wrout"]), (wgate[:, :], a["wgate"]), (wo[:, :, :], a["wo"]),
                             (vecs[:, :], a["vecs"]),
                             (biasb[:, :, :], a["biases"].partition_broadcast(128)),
                             (modb[:, :, :].rearrange("p a b -> p (a b)"), a["wmod"]),
                             (cT[:, :, :], a["cT"])):
                sp.dma_start(dst, src).then_inc(G["weights_in"], 16)

            sp.wait_ge(G["mod_one"], 1)
            sp.dma_start(a["modrows"], A[0:B, 6:8, :].rearrange("p a b -> p (a b)")[:, 0:2 * MODS * D]).then_inc(G["mod_out"], 16)
            sp.wait_ge(G["mod_out"], 16)
            sp.wait_ge(G["modT_copied"], 2)
            sp.wait_ge(G["set_done"], NSET)
            sp.wait_ge(G["pool_set"], NPOOL)

            with sp.Fori(0, B) as b:
                sp.dma_start(x[:, :, :], a["x"][b]).then_inc(S["x_in"], 16)
                sp.dma_start(modb[:, :, :], a["modrows"].rearrange("b (m d) -> b m d", d=D)[b].partition_broadcast(128)).then_inc(S["mod_in"], 16)

                def load_head(g, s):
                    sp.dma_start(whead[s][:, :], a["whead"][g]).then_inc(S[f"wh_in{s}"], 16)

                def load_aux(g, s):
                    sp.dma_start(auxin[64:96, :], a["aux"][g]).then_inc(S[f"aux_in{s}"], 16)

                load_head(0, 0)
                load_head(1, 1)
                load_aux(0, 0)
                for e in range(WBUF):
                    sp.dma_start(wex[e][:, :], a["wex"][e]).then_inc(S[f"w1_in{e}"], 16)
                with sp.Fori(0, PAIRS - 1) as p:
                    va, vb = sp.snap(2 * p + 1), sp.snap(2 * p + 2)
                    sp.wait_ge(S["k_aux"], va)
                    sp.sem_inc(G["passed"], 1)
                    load_aux(2 * p + 1, 1)
                    sp.wait_ge(S["qk_mm"], va)
                    sp.sem_inc(G["passed"], 1)
                    load_head(2 * p + 2, 0)
                    sp.wait_ge(S["k_aux"], vb)
                    sp.sem_inc(G["passed"], 1)
                    load_aux(2 * p + 2, 0)
                    sp.wait_ge(S["qk_mm"], vb)
                    sp.sem_inc(G["passed"], 1)
                    load_head(2 * p + 3, 1)
                sp.wait_ge(S["k_aux"], H1 - 1)
                load_aux(H1 - 1, 1)

                with sp.Fori(0, (EX1 - 1) // WBUF - 1) as r:
                    vs = [sp.snap(3 * (r * WBUF + i + 1)) for i in range(WBUF)]
                    for i in range(WBUF):
                        sp.wait_ge(S["w_low"], vs[i])
                        sp.sem_inc(G["passed"], 1)
                        sp.dma_start(wex[i][:, :], a["wex"][(r + 1) * WBUF + i]).then_inc(S[f"w1_in{i}"], 16)
                for e, src in ((EX1 - 1, EX1 - 1), (EX1, 0)):
                    sp.wait_ge(S["w_low"], 3 * (e - WBUF + 1))
                    sp.dma_start(wex[e % WBUF][:, :], a["wex"][src]).then_inc(S[f"w1_in{e % WBUF}"], 16)

                sp.wait_ge(S["xd_done"], 1)
                sp.dma_start(a["out"][b], x[:, :, :]).then_inc(S["x_out"], 16)
                v = sp.snap(b * 4 + 4)
                for i in range(WBUF):
                    sp.wait_ge(S[f"w1_in{i}"], 16 * (EX1 + 1) // WBUF)
                sp.wait_ge(S["x_out"], 16)
                sp.sem_inc(G["passed"], 1)
                sp.wait_ge(G["batch_ended"], v)
                sp.sem_inc(G["passed"], 1)
                sp.sem_clear(range(first, last + 1))
                sp.drain().then_inc(G["batch_open"], 1)

        @block.gpsimd
        def _(pool):
            pool.memset(halfneg[:, :], -0.5).then_inc(G["pool_set"], 1)
            pool.memset(zerob[:, :], 0.0).then_inc(G["pool_set"], 1)
            pool.memset(onecol[:, :], 1.0).then_inc(G["pool_set"], 1)
            pool.memset(grows[:, :], 0.0).then_inc(G["pool_set"], 1)
            pool.memset(prob[:, :, :, :], -1.0).then_inc(G["pool_set"], 1)
            for s in range(2):
                beside = slice(64 - 64 * s, 128 - 64 * s)
                pool.memset(Vh[s][:, :, beside].bitcast(F32), 1.0).then_inc(G["pool_set"], 1)
                pool.memset(Vl[s][:, :, beside].bitcast(F32), 0.0).then_inc(G["pool_set"], 1)
            pool.memset(gate[:, :, :, :], 0.0).then_inc(G["pool_set"], 1)
            pool.wait_ge(G["pool_set"], NPOOL)
            with pool.Fori(0, B) as b:
                def inverse_root(tag):
                    pool.wait_ge(S["ln_eps"], LN_TAGS.index(tag) + 1)
                    pool.tensor_tensor(rstd[:, :], veps[:, :], halfneg[:, :], ALU.pow).then_inc(S["ln_rstd"], 1)

                for tag in LN_TAGS[:-1]:
                    inverse_root(tag)

                pool.sem_inc(S["p_low"], PLOW_AT)
                with pool.Fori(0, PAIRS) as p:
                    for j in range(2 * T):
                        k = 2 * T * p + j
                        pool.wait_ge(S["p_high"], k + 1)
                        pool.wait_ge(S["pv_done"], k - 1 + PV_AT)
                        pool.tensor_tensor(plow[j % 2], pfull[:, j % 2, :], phigh[j % RING].bitcast(F32), ALU.subtract).then_inc(S["p_low"], 1)

                inverse_root("d0")

                def low_weights(n, q, m):
                    pool.wait_ge(S["w_high"], 3 * n + m + 1)
                    cols = slice(m * F1, (m + 1) * F1)
                    pool.tensor_tensor(wl[q][:, cols], wex[q][:, cols], wh[q][:, cols].bitcast(F32), ALU.subtract).then_inc(S["w_low"], 1)

                def expert(n, q):
                    for u in range(UNITS):
                        i = u % 2
                        pool.wait_ge(S["silu_done"], n * UNITS + u + 1 + UNIT_AT)
                        if u == 0:
                            pool.wait_ge(S["gates_in"], n * NHALF + NHALF)
                        pool.wait_ge(S["gu_done"], n * UNITS + u - 1 + UNIT_AT)
                        pool.tensor_tensor(half(gsilu, i), half(silu, i), half(gatesb[q], i), ALU.mult).then_inc(S["silu_gated"], 1)
                        if NEXT < u <= NEXT + 3:
                            low_weights(n + 1, 1 - q, u - NEXT - 1)

                for m in range(3):
                    low_weights(0, 0, m)
                pool.sem_inc(S["silu_gated"], UNIT_AT)
                expert(0, 0)
                with pool.Fori(0, (EX1 - 1) // 2) as r:
                    expert(2 * r + 1, 1)
                    expert(2 * r + 2, 0)
                end_batch(pool, b)

        @block.vector
        def _(dve):
            tens = [128, T, D]
            cst = A[:, 0:5, :].rearrange("p a b -> p (a b)")

            dve.wait_ge(G["consts_in"], 16)
            dve.tensor_copy(identf[:, :], cst[:, C_IDENT:C_IDENT + 128])
            dve.tensor_copy(identb[:, :], cst[:, C_IDENT:C_IDENT + 128])
            dve.tensor_copy(distb[:, :], cst[:, C_DIST:C_DIST + 128])
            dve.tensor_copy(mask[:, :], cst[:, C_MASK:C_MASK + 128])
            dve.tensor_copy(selb[:, :, :].rearrange("p a b -> p (a b)"), cst[:, C_SELB:C_SELD])
            dve.tensor_copy(seld[:, :, :].rearrange("p a b -> p (a b)"), cst[:, C_SELD:C_AUXQ])
            dve.tensor_tensor(diagb[:, :, :], over(cst[:, C_IDENT:C_IDENT + 128], [128, 3 * H1, 128]),
                              cst[:, C_SLOPE:C_SLOPE + 3 * H1].unsqueeze(2).to_broadcast([128, 3 * H1, 128]), ALU.mult)
            for s in range(2):
                dve.tensor_copy(Qa[s][64:96, :], cst[64:96, C_AUXQ:C_END])
                dve.tensor_scalar(Ka[s][96:128, :], cst[96:128, C_AUXQ:C_END], 0.0, 1.0, ALU.mult, ALU.add)\
                    .then_inc(G["set_done"], 1)

            rows = A[0:B, 6:8, :].rearrange("p a b -> p (a b)")[:, 0:2 * MODS * D]
            dve.wait_ge(G["mod_mm"], 1)
            dve.tensor_copy(rows, P[0:B, 0:3, :].rearrange("p a b -> p (a b)")).then_inc(G["mod_abs"], 1)
            dve.wait_ge(G["mod_abs"], 1)
            r3 = rows.rearrange("p (m d) -> p m d", d=D)
            gs = r3[:, 2::3, :]
            tmp = A[0:B, 0, 0:4 * D].rearrange("p (m d) -> p m d", d=D)
            sg = A[0:B, 1, 0:4 * D].rearrange("p (m d) -> p m d", d=D)
            dve.wait_ge(G["set_done"], NSET)
            dve.wait_ge(G["pool_set"], NPOOL)
            dve.scalar_tensor_tensor(tmp, gs, -1.0, gs, ALU.mult, ALU.max).then_inc(G["mod_abs"], 1)
            dve.tensor_scalar(sg, gs, 0.0, 2.0, ALU.is_ge, ALU.mult).then_inc(G["mod_abs"], 1)
            dve.wait_ge(G["mod_abs"], 3)
            dve.tensor_scalar(tmp, tmp, 0.25, None, ALU.max).then_inc(G["mod_sgn"], 1)
            dve.tensor_scalar(sg, sg, -1.0, None, ALU.add).then_inc(G["mod_sgn"], 1)
            dve.wait_ge(G["mod_sgn"], 2)
            dve.tensor_tensor(gs, tmp, sg, ALU.mult)
            dve.tensor_scalar(r3[:, 1::3, :], r3[:, 1::3, :], 1.0, None, ALU.add).then_inc(G["mod_one"], 1)
            dve.wait_ge(G["modT_mm"], 1)
            dve.tensor_copy(modT[:, :, :], P[:, 3, 0:2 * MODS * B].rearrange("p (m b) -> p m b", b=B)).then_inc(G["modT_copied"], 1)
            dve.wait_ge(G["modT_copied"], 1)
            dve.tensor_scalar(modT[:, 1::3, :], modT[:, 1::3, :], 1.0, None, ALU.add).then_inc(G["modT_copied"], 1)
            dve.wait_ge(G["modT_copied"], 2)

            def norm(tag, src, dst):
                nth = LN_TAGS.index(tag)
                for t in range(T):
                    dve.bn_stats(stats[:, t, :], src[:, t, :]).then_inc(S["ln_moments"], 1)
                dve.wait_ge(S["ln_moments"], (2 * nth + 1) * T)
                for t in range(T):
                    dve.bn_aggr(mv[:, t, :], stats[:, t, :]).then_inc(S["ln_moments"], 1)
                dve.wait_ge(S["ln_moments"], (2 * nth + 2) * T)
                dve.tensor_scalar(veps[:, :], mv[:, :, 1], EPS_LN, None, ALU.add).then_inc(S["ln_eps"], 1)
                dve.wait_ge(S["ln_rstd"], nth + 1)
                for t in range(T):
                    dve.tensor_scalar(dst[:, t, :], src[:, t, :], mv[:, t, 0:1], rstd[:, t:t + 1],
                                      ALU.subtract, ALU.mult).then_inc(S["ln_norm"], 1)

            def modulate(tag, m):
                dve.wait_ge(S["ln_norm"], (LN_TAGS.index(tag) + 1) * T)
                dve.tensor_tensor(h[:, :, :], xn[:, :, :], over(modb[:, m + 1, :], tens), ALU.mult).then_inc(S["modulated"], 1)
                dve.wait_ge(S["modulated"], m // 3 + 1)
                dve.tensor_tensor(h[:, :, :], h[:, :, :], over(modb[:, m, :], tens), ALU.add).then_inc(S["modulated"], 1)
                dve.wait_ge(S["modulated"], m // 3 + 2)

            def hT_half(tag, bank, scale, bias):
                dve.wait_ge(S["turned"], NHALF * TR_TAGS.index(tag) + 1)
                dve.tensor_scalar(half(hT, 0), P[:, bank, :], scale, bias, ALU.mult, ALU.add).then_inc(S["hT_dve"], 1)

            def router(tag, n, k, bank, bank2, table, factor):
                logits = P[:, bank, 0:T * n].rearrange("p (t e) -> p t e", e=n)
                dve.wait_ge(S[f"{tag}_mm"], 1)
                dve.tensor_reduce(rmax[:, 0, :], logits, AX.X, ALU.max).then_inc(S[f"{tag}_steps"], 1)
                dve.wait_ge(S[f"{tag}_steps"], 1)
                dve.tensor_tensor(rlog[:, :, 0:n], logits, col(rmax[:, 0, :], n), ALU.subtract).then_inc(S[f"{tag}_sub"], 1)
                dve.wait_ge(S[f"{tag}_exp"], 1)
                dve.tensor_reduce(rmax[:, 1, :], rexp[:, :, 0:n], AX.X, ALU.add).then_inc(S[f"{tag}_steps"], 1)
                dve.wait_ge(S[f"{tag}_steps"], 2)
                dve.reciprocal(rmax[:, 2, :], rmax[:, 1, :]).then_inc(S[f"{tag}_steps"], 1)
                dve.wait_ge(S[f"{tag}_steps"], 3)
                pr = prob[:, table, :, 0:n + 8]
                dve.scalar_tensor_tensor(pr[:, :, 0:n], rexp[:, :, 0:n], factor, col(rmax[:, 2, :], n),
                                         ALU.mult, ALU.mult).then_inc(S[f"{tag}_steps"], 1)
                dve.wait_ge(S[f"{tag}_steps"], 4)
                for t in range(T):
                    dve.max(top8[:, t, :], pr[:, t, :]).then_inc(S[f"{tag}_steps"], 1)
                dve.wait_ge(S[f"{tag}_steps"], 4 + T)
                dve.memset(top8[:, :, k:8], -1.0).then_inc(S[f"{tag}_steps"], 1)
                dve.wait_ge(S[f"{tag}_steps"], 5 + T)
                for t in range(T):
                    dve.match_replace(hit[:, t, 0:n + 8], top8[:, t, :], pr[:, t, :], -5.0).then_inc(S[f"{tag}_steps"], 1)
                dve.wait_ge(S[f"{tag}_steps"], 5 + 2 * T)
                dve.scalar_tensor_tensor(gate[:, 0, :, 0:n], hit[:, :, 0:n], -2.0, pr[:, :, 0:n],
                                         ALU.is_lt, ALU.mult).then_inc(S[f"{tag}_steps"], 1)
                dve.wait_ge(S[f"{tag}_steps"], 6 + 2 * T)
                g, r1, r2 = (gate[:, i, :, :] for i in range(3))
                hi, mid, lo = (gparts[:, :, i * GW:(i + 1) * GW] for i in range(3))
                dve.tensor_copy(hi, g).then_inc(S[f"{tag}_steps"], 1)
                dve.wait_ge(S[f"{tag}_steps"], 7 + 2 * T)
                dve.tensor_tensor(r1, g, hi, ALU.subtract).then_inc(S[f"{tag}_steps"], 1)
                dve.wait_ge(S[f"{tag}_steps"], 8 + 2 * T)
                dve.tensor_copy(mid, r1).then_inc(S[f"{tag}_steps"], 1)
                dve.wait_ge(S[f"{tag}_steps"], 9 + 2 * T)
                dve.tensor_tensor(lo, r1, mid, ALU.subtract).then_inc(S[f"{tag}_lo"], 1)
                dve.wait_ge(S[f"{tag}_turned"], 1)
                dve.tensor_copy(grows[0:3 * GW, :], P[0:3 * GW, bank2, :].bitcast(BF16)).then_inc(S[f"{tag}_rows"], 1)

            with dve.Fori(0, B) as b:
                dve.tensor_copy(modv[:, :], modT[:, :, b]).then_inc(S["vec_copied"], 1)

                dve.wait_ge(S["x_in"], 16)
                norm("a0", x, xn)
                dve.wait_ge(S["mod_in"], 16)
                modulate("a0", 0)
                norm("a1", h, xn)
                dve.wait_ge(S["vec_copied"], 1)
                hT_half("a1", 0, vecs[:, 0:1], vecs[:, 1:2])
                dve.wait_ge(S["q0_mm"], 2)
                dve.tensor_scalar(A[:, 0, :], banks(0), 0.0, None, ALU.min).then_inc(S["q0_min"], 1)
                kpsum = P[:, 2:6, :].rearrange("p a (t c) -> p (a t) c", c=2 * D)
                dve.wait_ge(S["k0_mm"], T)
                dve.tensor_scalar(tok(A[:, 2, :]), kpsum[:, :, 0:D], 0.0, None, ALU.min).then_inc(S["k0_min"], 1)
                dve.wait_ge(S["q0_exp"], 1)
                dve.scalar_tensor_tensor(A[:, 0, :], banks(0), 0.0, A[:, 1, :], ALU.max, ALU.add).then_inc(S["q0_done"], 1)
                dve.wait_ge(S["k0_exp"], 1)
                dve.scalar_tensor_tensor(tok(A[:, 2, :]), kpsum[:, :, 0:D], 0.0, tok(A[:, 3, :]), ALU.max, ALU.add).then_inc(S["k0_done"], 1)
                dve.tensor_copy(tok(A[:, 4, :]), kpsum[:, :, D:2 * D]).then_inc(S["v0_copied"], 1)
                dve.wait_ge(S["kv_mm"], 1)
                dve.tensor_tensor(small[:, 0, :], P[:, 6, 0:D], mask[:, :], ALU.mult).then_inc(S["kv_masked"], 1)
                dve.wait_ge(S["ks_mm"], 1)
                dve.tensor_scalar(small[:, 1, :], mask[:, :], P[:, 7, 0:1], None, ALU.mult).then_inc(S["ks_masked"], 1)
                dve.wait_ge(S["den_mm"], 2)
                dve.tensor_scalar(A[:, 1, :], banks(2), EPS_ATTN, None, ALU.add).then_inc(S["den_eps"], 1)
                dve.wait_ge(S["den_eps"], 1)
                dve.reciprocal(A[:, 3, :], A[:, 1, :]).then_inc(S["den_inv"], 1)
                dve.wait_ge(S["den_inv"], 1)
                dve.wait_ge(S["num_mm"], 2)
                dve.tensor_tensor(A[:, 5, :], banks(0), A[:, 3, :], ALU.mult).then_inc(S["o0_done"], 1)
                dve.wait_ge(S["proj_mm"], T)
                dve.tensor_tensor(tok(A[:, 6, :]), tiles(4), h[:, :, :], ALU.add).then_inc(S["x1_sum"], 1)
                dve.wait_ge(S["x1_sum"], 1)
                dve.tensor_tensor(tok(A[:, 6, :]), tok(A[:, 6, :]), over(biasb[:, 0, :], tens), ALU.add).then_inc(S["x1_done"], 1)
                dve.wait_ge(S["x1_done"], 1)
                norm("a2", tok(A[:, 6, :]), xn)
                hT_half("a2", 0, vecs[:, 2:3], vecs[:, 3:4])
                dve.tensor_tensor(tok(A[:, 7, :]), tok(A[:, 6, :]), over(biasb[:, 1, :], tens), ALU.add).then_inc(S["x1_bias"], 1)
                dve.wait_ge(S["x1_bias"], 1)
                dve.wait_ge(S["fc2_mm"], T)
                dve.tensor_tensor(tok(A[:, 6, :]), tiles(4), tok(A[:, 7, :]), ALU.add).then_inc(S["y0"], 1)
                dve.wait_ge(S["y0"], 1)
                dve.tensor_tensor(tok(A[:, 6, :]), tok(A[:, 6, :]), over(modb[:, 2, :], tens), ALU.mult).then_inc(S["y0_scaled"], 1)
                dve.wait_ge(S["y0_scaled"], 1)
                dve.tensor_tensor(x[:, :, :], x[:, :, :], tok(A[:, 6, :]), ALU.add).then_inc(S["xa_done"], 1)
                dve.wait_ge(S["xa_done"], 1)

                norm("b0", x, xn)
                hT_half("b0", 6, modv[:, 4:5], modv[:, 3:4])
                router("rb", E0, K0, 7, 7, 0, 1.0)
                for u in range(NHALF, CH0 * NHALF):
                    dve.wait_ge(S["up_act"], u + 1)
                    dve.wait_ge(S["bcb_mm"], u - NHALF + 1)
                    if u - NHALF >= 4:
                        dve.wait_ge(S["downb_mm"], u - 4 + 1)
                    ga_ = A[:, 2 + (u % 4) // 2, (u % 2) * HALF:(u % 2 + 1) * HALF]
                    ac_ = A[:, (u % 4) // 2, (u % 2) * HALF:(u % 2 + 1) * HALF]
                    dve.tensor_tensor(ga_, P[:, 5 + u % 2, :], ac_, ALU.mult).then_inc(S["up_gated"], 1)
                dve.wait_ge(S["downb_end"], NHALF)
                dve.tensor_tensor(tok(A[:, 4, :]), tiles(0), over(modb[:, 5, :], tens), ALU.mult).then_inc(S["yb_scaled"], 1)
                dve.wait_ge(S["yb_scaled"], 1)
                dve.tensor_tensor(x[:, :, :], x[:, :, :], tok(A[:, 4, :]), ALU.add).then_inc(S["xb_done"], 1)
                dve.wait_ge(S["xb_done"], 1)

                norm("c0", x, xn)
                modulate("c0", MODS)
                norm("c1", h, xn)
                hT_half("c1", 6, vecs[:, 4 + FC:5 + FC], vecs[:, 5 + FC:6 + FC])

                def normalise(p, c):
                    if c == 0:
                        dve.wait_ge(S["s_copied"], 2 * p + 2 + COPIED_AT)
                        dve.wait_ge(S["o_copied"], 2 * p + 2 + COPIED_AT)
                    cols = slice(c * N // NCHUNK, (c + 1) * N // NCHUNK)
                    dve.reciprocal(spair[:, cols], spair[:, cols]).then_inc(S["s_inv"], 1)
                    dve.wait_ge(S["s_inv"], p * NCHUNK + c + 1)
                    dve.tensor_tensor(A[:, p, cols], opair[:, cols], spair[:, cols], ALU.mult).then_inc(S["o_norm"], 1)

                def prep(s, n, done=None):
                    dve.wait_ge(S["pv_done"], PV_AT if isinstance(n, int) and n == 0 else T * (n - 1) + PV_AT)
                    dve.wait_ge(S["st_mm"], T * (n - 1) + ST_AT if not (isinstance(n, int) and n == 0) else ST_AT)
                    dve.wait_ge(S["v_high"], n + 1)
                    dve.tensor_tensor(Vl[s][:, :, 64 * s:64 * s + 64], vpsum, Vh[s][:, :, 64 * s:64 * s + 64].bitcast(F32), ALU.subtract).then_inc(S["v_low"], 1)
                    dve.wait_ge(S["q_hi"], n + 1)
                    dve.tensor_tensor(Qb[s][0:64, :], banks(6, 2, slice(0, 64)), Qa[s][0:64, :].bitcast(F32), ALU.subtract).then_inc(S["q_lo"], 1)
                    dve.wait_ge(S["k_hi"], n + 1)
                    dve.tensor_tensor(Kb[s][64:128, :], banks(6, 2, slice(64, 128)), Ka[s][0:64, :].bitcast(F32), ALU.subtract).then_inc(S["k_lo"], 1)
                    dve.tensor_copy(Qb[s][64:128, :], Qa[s][0:64, :].bitcast(F32)).then_inc(S["q_dup"], 1)
                    dve.tensor_copy(Kb[s][0:64, :], Ka[s][0:64, :].bitcast(F32)).then_inc(S["k_dup"], 1)
                    for t in range(T):
                        for i in range(NHALF):
                            dve.wait_ge(S["max_mm"], (n * T + t) * NHALF + i + 1)
                            dve.tensor_reduce(mhalf[:, i, t:t + 1], P[:, 6 + i, :], AX.X, ALU.max, negate=True).then_inc(S["max_red"], 1)
                        if done is not None and t % 2 == 1:
                            normalise(done, t // 2)
                    dve.wait_ge(S["max_red"], (n + 1) * T * NHALF)
                    dve.tensor_tensor(mneg[:, :], mhalf[:, 0, :], mhalf[:, 1, :], ALU.min).then_inc(S["max_both"], 1)
                    dve.wait_ge(S["max_both"], n + 1)
                    dve.tensor_copy(mparts[:, :, 0], mneg[:, :]).then_inc(S["m_hi"], 1)
                    dve.wait_ge(S["m_hi"], n + 1)
                    dve.tensor_tensor(mparts[:, :, 1], mneg[:, :], mparts[:, :, 0], ALU.subtract).then_inc(S["m_mid"], 1)

                def sums(s, p):
                    dve.wait_ge(S["pv_done"], (2 * p + s + 1) * T + PV_AT)
                    dve.wait_ge(S["o_norm"], p * NCHUNK + NORM_AT)
                    dve.tensor_copy(spair[64 * s:64 * s + 64, :], banks(4, 2, slice(64 - 64 * s, 128 - 64 * s))).then_inc(S["s_copied"], 1)

                dve.sem_inc(S["s_copied"], COPIED_AT)
                dve.sem_inc(S["o_norm"], NORM_AT)
                prep(0, 0)
                prep(1, 1)
                sums(0, 0)
                with dve.Fori(0, PAIRS - 1) as p:
                    prep(0, 2 * p + 2)
                    sums(1, p)
                    prep(1, 2 * p + 3, p)
                    sums(0, p + 1)
                sums(1, PAIRS - 1)
                for c in range(NCHUNK):
                    normalise(PAIRS - 1, c)

                dve.wait_ge(S["o1_mm"], T)
                dve.tensor_tensor(h[:, :, :], tiles(0), over(modb[:, MODS + 2, :], tens), ALU.mult).then_inc(S["o1_scaled"], 1)
                dve.wait_ge(S["o1_scaled"], 1)
                dve.tensor_tensor(x[:, :, :], x[:, :, :], h[:, :, :], ALU.add).then_inc(S["xc_done"], 1)
                dve.wait_ge(S["xc_done"], 1)

                norm("d0", x, xn)
                hT_half("d0", 6, modv[:, MODS + 4:MODS + 5], modv[:, MODS + 3:MODS + 4])
                dve.memset(gate[:, 0, :, E1:E1 + 1], 0.5 / E1)
                router("rd", E1, K1N, 2, 3, 1, 0.5)

                def low_unit(c, i):
                    dve.wait_ge(S["gu_high"], c + 1)
                    dve.wait_ge(S["downd_mm"], c - 1 + UNIT_AT)
                    dve.tensor_tensor(half(gul, i), half(gu, i), half(guh, i).bitcast(F32), ALU.subtract).then_inc(S["gu_low"], 1)

                def expert(n):
                    for u in range(UNITS):
                        c, i = n * UNITS + u, u % 2
                        if not (isinstance(c, int) and c == 0):
                            low_unit(c - 1, 1 - i)
                        dve.wait_ge(S["w3_mm"], c + 1)
                        dve.wait_ge(S["silu_gated"], c + 1 + UNIT_AT)
                        dve.wait_ge(S["gu_low"], c - 1 + UNIT_AT)
                        dve.tensor_tensor(half(gu, i), P[:, 4 + i, :], half(gsilu, i), ALU.mult).then_inc(S["gu_done"], 1)

                dve.wait_ge(S["hT_high"], 1)
                dve.tensor_tensor(hTl[:, :], hT[:, :], hTh[:, :].bitcast(F32), ALU.subtract).then_inc(S["hT_low"], 1)
                dve.sem_inc(S["gu_done"], UNIT_AT)
                dve.sem_inc(S["gu_low"], UNIT_AT)
                expert(0)
                with dve.Fori(0, (EX1 - 1) // 2) as r:
                    expert(2 * r + 1)
                    expert(2 * r + 2)
                low_unit(EX1 * UNITS - 1, 1)
                dve.wait_ge(S["downd_end"], NHALF)
                dve.tensor_copy(A[:, 3, :], banks(0)).then_inc(S["ydT_copied"], 1)
                dve.wait_ge(S["yd_turned"], 1)
                dve.tensor_tensor(h[:, :, :], tiles(2), over(modb[:, MODS + 5, :], tens), ALU.mult).then_inc(S["yd_scaled"], 1)
                dve.wait_ge(S["yd_scaled"], 1)
                dve.tensor_tensor(x[:, :, :], x[:, :, :], h[:, :, :], ALU.add).then_inc(S["xd_done"], 1)
                end_batch(dve, b)

        @block.scalar
        def _(act):
            act.wait_ge(G["weights_in"], 16 * NLOAD)
            act.activation(cs[:, :, :], cT[:, :, :], ACT.Silu).then_inc(G["c_silu"], 1)

            def hT_half(tag, bank, scale, bias):
                act.wait_ge(S["vec_copied"], 1)
                act.wait_ge(S["turned"], NHALF * TR_TAGS.index(tag) + 2)
                act.activation(half(hT, 1), P[:, bank + 1, :], ACT.Identity, bias=bias, scale=scale).then_inc(S["hT_act"], 1)

            act.wait_ge(G["set_done"], NSET)
            act.wait_ge(G["pool_set"], NPOOL)
            with act.Fori(0, B) as b:
                hT_half("a1", 0, vecs[:, 0:1], vecs[:, 1:2])
                act.wait_ge(S["q0_min"], 1)
                act.activation(A[:, 1, :], A[:, 0, :], ACT.Exp).then_inc(S["q0_exp"], 1)
                act.wait_ge(S["k0_min"], 1)
                act.activation(A[:, 3, :], A[:, 2, :], ACT.Exp).then_inc(S["k0_exp"], 1)
                hT_half("a2", 0, vecs[:, 2:3], vecs[:, 3:4])
                for u in range(FC * NHALF):
                    c, i = u // NHALF, u % NHALF
                    act.wait_ge(S["fc1_mm"], u + 1)
                    act.activation(half(A[:, c, :], i), P[:, 2 + u % 2, :], ACT.Gelu, bias=vecs[:, 4 + c:5 + c]).then_inc(S["fc1_act"], 1)
                hT_half("b0", 6, modv[:, 4:5], modv[:, 3:4])
                act.wait_ge(S["rb_sub"], 1)
                act.activation(rexp[:, :, 0:E0], rlog[:, :, 0:E0], ACT.Exp).then_inc(S["rb_exp"], 1)
                for u in range(CH0 * NHALF):
                    act.wait_ge(S["up_mm"], u + 1)
                    if u >= 4:
                        if u - 4 < NHALF:
                            act.wait_ge(S["downb_mm"], u - 4 + 1)
                        else:
                            act.wait_ge(S["up_gated"], u - 4 - NHALF + 1)
                    act.activation(A[:, (u % 4) // 2, (u % 2) * HALF:(u % 2 + 1) * HALF], P[:, 2 + u % 3, :], ACT.Gelu).then_inc(S["up_act"], 1)
                hT_half("c1", 6, vecs[:, 4 + FC:5 + FC], vecs[:, 5 + FC:6 + FC])

                def values(s, n):
                    act.wait_ge(S["st_mm"], ST_AT if isinstance(n, int) and n == 0 else T * (n - 1) + ST_AT)
                    act.wait_ge(S["v_mm"], n + 1)
                    act.wait_ge(S["pv_done"], PV_AT if isinstance(n, int) and n == 0 else T * (n - 1) + PV_AT)
                    act.activation(Vh[s][:, :, 64 * s:64 * s + 64], vpsum, ACT.Copy).then_inc(S["v_high"], 1)

                def factors(s, n):
                    act.wait_ge(S[f"aux_in{s}"], 8 * (n - s) + 16)
                    act.activation(Ka[s][64:96, :], auxin[64:96, :], ACT.Copy).then_inc(S["k_aux"], 1)

                def high_parts(s, n):
                    act.wait_ge(S["qk_mm"], n + 1)
                    act.activation(Qa[s][0:64, :], banks(6, 2, slice(0, 64)), ACT.Copy).then_inc(S["q_hi"], 1)
                    act.activation(Ka[s][0:64, :], banks(6, 2, slice(64, 128)), ACT.Copy).then_inc(S["k_hi"], 1)

                def maxima(s, n):
                    act.wait_ge(S["m_row"], n + 1)
                    act.activation(Qa[s][MROW:MROW + 2, :], banks(6, 2, slice(0, 2)), ACT.Copy).then_inc(S["m_in"], 1)

                def exps(k, j, between=None):
                    act.wait_ge(S["st_mm"], k + 1 + ST_AT)
                    act.wait_ge(S["p_low"], k - 1 + PLOW_AT if not (isinstance(k, int) and k == 0) else PLOW_AT)
                    act.activation(pfull[:, j % 2, :], banks(2 * (j % 2)), ACT.Exp, scale=DH1 ** -0.5).then_inc(S["exp_done"], 1)
                    if between:
                        between()
                    act.wait_ge(S["pv_done"], k + 1 - RING + PV_AT)
                    act.wait_ge(S["exp_done"], k + 1 + EXP_AT)
                    act.activation(phigh[j % RING], pfull[:, j % 2, :], ACT.Copy).then_inc(S["p_high"], 1)

                def outputs(s, p):
                    act.wait_ge(S["pv_done"], (2 * p + s + 1) * T + PV_AT)
                    act.wait_ge(S["o_norm"], p * NCHUNK + NORM_AT)
                    act.activation(opair[64 * s:64 * s + 64, :], banks(4, 2, slice(64 * s, 64 * s + 64)), ACT.Copy).then_inc(S["o_copied"], 1)

                def pair(p, is_last):
                    for j in range(2 * T):
                        s, n = j // T, 2 * p + 1 + j // T
                        ahead = not (is_last and s == 1)
                        if ahead and j % T == T - 1:
                            maxima(1 - s, n)
                        if is_last and j == 2 * T - 1:
                            outputs(s, p)
                        elif j % T == T - 1:
                            exps(2 * T * p + j + 1, j + 1, lambda s=s: outputs(s, p))
                        elif j % T == 0 and ahead:
                            exps(2 * T * p + j + 1, j + 1, lambda s=s, n=n: values(1 - s, n))
                        elif j % T == 1 and ahead:
                            exps(2 * T * p + j + 1, j + 1, lambda s=s, n=n: high_parts(1 - s, n))
                        else:
                            exps(2 * T * p + j + 1, j + 1)
                        if ahead and j % T == 1:
                            factors(1 - s, n)

                act.sem_inc(S["exp_done"], EXP_AT)
                act.sem_inc(S["o_copied"], COPIED_AT)
                act.wait_ge(S["hT_act"], TR_TAGS.index("c1") + 1)
                values(0, 0)
                factors(0, 0)
                high_parts(0, 0)
                maxima(0, 0)
                exps(0, 0)
                with act.Fori(0, PAIRS - 1) as p:
                    pair(p, False)
                pair(PAIRS - 1, True)

                hT_half("d0", 6, modv[:, MODS + 4:MODS + 5], modv[:, MODS + 3:MODS + 4])
                act.wait_ge(S["rd_sub"], 1)
                act.activation(rexp[:, :, 0:E1], rlog[:, :, 0:E1], ACT.Exp).then_inc(S["rd_exp"], 1)
                act.wait_ge(S["hT_dve"], len(TR_TAGS))
                act.wait_ge(S["hT_act"], len(TR_TAGS))
                act.activation(hTh[:, :], hT[:, :], ACT.Copy).then_inc(S["hT_high"], 1)

                def high_weights(n, q, m, loads):
                    act.wait_ge(S[f"w1_in{q}"], loads)
                    cols = slice(m * F1, (m + 1) * F1)
                    act.activation(wh[q][:, cols], wex[q][:, cols], ACT.Copy).then_inc(S["w_high"], 1)

                def gates(n, q):
                    for i in range(NHALF):
                        act.wait_ge(S["bcd_mm"], n * NHALF + i + 1)
                        act.activation(half(gatesb[q], i), P[:, 6 + i, :], ACT.Copy).then_inc(S["gates_in"], 1)

                def high_unit(c, i):
                    act.wait_ge(S["gu_done"], c + 1 + UNIT_AT)
                    act.wait_ge(S["downd_mm"], c - 1 + UNIT_AT)
                    act.activation(half(guh, i), half(gu, i), ACT.Copy).then_inc(S["gu_high"], 1)

                def expert(n, q, loads):
                    for u in range(UNITS):
                        c, i = n * UNITS + u, u % 2
                        act.wait_ge(S["w1_mm"], c + 1)
                        act.wait_ge(S["silu_gated"], c - 1 + UNIT_AT)
                        act.activation(half(silu, i), P[:, 2 + i, :], ACT.Silu).then_inc(S["silu_done"], 1)
                        if NEXT <= u < NEXT + 3:
                            high_weights(n + 1, 1 - q, u - NEXT, loads)
                        if not (isinstance(c, int) and c == 0):
                            high_unit(c - 1, 1 - i)
                        if u == UNITS - 2:
                            gates(n + 1, 1 - q)

                for m in range(3):
                    high_weights(0, 0, m, 16)
                gates(0, 0)
                act.sem_inc(S["silu_done"], UNIT_AT)
                expert(0, 0, 16)
                with act.Fori(0, (EX1 - 1) // 2) as r:
                    expert(2 * r + 1, 1, 16 * r + 32)
                    expert(2 * r + 2, 0, 16 * r + 32)
                high_unit(EX1 * UNITS - 1, 1)
                end_batch(act, b)

        @block.tensor
        def _(pe):
            pe.wait_ge(G["weights_in"], 16 * NLOAD)
            wmod = modb[:, :, :].rearrange("p a b -> p (a b)")
            pe.wait_ge(G["c_silu"], 1)
            for i, l in ((0, 0), (1, 0), (1, 1), (2, 1)):
                lo, hi = max(i * HALF, l * MODS * D), min((i + 1) * HALF, (l + 1) * MODS * D)
                mm = pe.matmul(P[0:B, i, lo - i * HALF:hi - i * HALF], cs[:, l, :], wmod[:, lo:hi], start=True, stop=True)
            mm.then_inc(G["mod_mm"], 1)
            for m in range(2 * MODS):
                mm = pe.matmul(P[:, 3, m * B:(m + 1) * B], wmod[:, m * D:(m + 1) * D], cs[:, m // MODS, :], start=True, stop=True)
            mm.then_inc(G["modT_mm"], 1)
            pe.wait_ge(G["modT_copied"], 2)
            pe.wait_ge(G["mod_one"], 1)
            pe.wait_ge(G["set_done"], NSET)
            pe.wait_ge(G["pool_set"], NPOOL)

            def turn(tag, bank):
                for t in range(T):
                    pe.wait_ge(S["ln_norm"], LN_TAGS.index(tag) * T + t + 1)
                    tr = pe.transpose(bank_t(bank, t), xn[:, t, :], identf[:, :])
                    if t % TPH == TPH - 1:
                        tr.then_inc(S["turned"], 1)
                pe.wait_ge(S["hT_dve"], TR_TAGS.index(tag) + 1)
                pe.wait_ge(S["hT_act"], TR_TAGS.index(tag) + 1)

            def tile(t_, t):
                return t_[:, t * 128:(t + 1) * 128]

            def route(tag, n, w, bank):
                for t in range(T):
                    mm = pe.matmul(P[:, bank, t * n:(t + 1) * n], tile(hT, t), w, start=True, stop=True)
                mm.then_inc(S[f"{tag}_mm"], 1)

            def turn_gates(tag, bank):
                pe.wait_ge(S[f"{tag}_lo"], 1)
                rows = P[0:3 * GW, bank, :].bitcast(BF16)
                for t in range(T):
                    tr = pe.transpose(rows[:, t * 128:(t + 1) * 128], gparts[:, t, :], identb[:, :])
                tr.then_inc(S[f"{tag}_turned"], 1)

            def zero(bank):
                pe.matmul(P[:, bank, :], zerob[:, 0:128], zerob[:, :], start=True, stop=False)

            def close(bank):
                return pe.matmul(P[:, bank, :], zerob[:, 0:128], zerob[:, :], start=False, stop=True)

            with pe.Fori(0, B) as b:
                turn("a1", 0)
                for i in range(NHALF):
                    pe.matmul(P[:, i, :], wqkv0[:, 0:D], half(hT, i), start=True, stop=True).then_inc(S["q0_mm"], 1)
                for t in range(T):
                    pe.matmul(P[:, 2 + t // 2, (t % 2) * 2 * D:(t % 2 + 1) * 2 * D], tile(hT, t), wqkv0[:, D:3 * D],
                              start=True, stop=True).then_inc(S["k0_mm"], 1)
                pe.wait_ge(S["k0_done"], 1)
                for t in range(T):
                    if t == 0:
                        pe.wait_ge(S["v0_copied"], 1)
                    mm = pe.matmul(P[:, 6, 0:D], tile(A[:, 2, :], t), tile(A[:, 4, :], t), start=(t == 0), stop=(t == T - 1))
                mm.then_inc(S["kv_mm"], 1)
                for t in range(T):
                    mm = pe.matmul(P[:, 7, 0:1], tile(A[:, 2, :], t), onecol[:, :], start=(t == 0), stop=(t == T - 1))
                mm.then_inc(S["ks_mm"], 1)
                pe.wait_ge(S["q0_done"], 1)
                pe.wait_ge(S["ks_masked"], 1)
                for i in range(NHALF):
                    pe.matmul(P[:, 2 + i, :], small[:, 1, :], half(A[:, 0, :], i), start=True, stop=True).then_inc(S["den_mm"], 1)
                pe.wait_ge(S["kv_masked"], 1)
                for i in range(NHALF):
                    pe.matmul(P[:, i, :], small[:, 0, :], half(A[:, 0, :], i), start=True, stop=True).then_inc(S["num_mm"], 1)
                pe.wait_ge(S["o0_done"], 1)
                for t in range(T):
                    pe.matmul(bank_t(4, t), tile(A[:, 5, :], t), wproj[:, :], start=True, stop=True).then_inc(S["proj_mm"], 1)
                turn("a2", 0)
                for u in range(FC * NHALF):
                    c, i = u // NHALF, u % NHALF
                    if u >= 2:
                        pe.wait_ge(S["fc1_act"], u - 1)
                    pe.matmul(P[:, 2 + u % 2, :], wfc1[:, c * 128:(c + 1) * 128], half(hT, i), start=True, stop=True).then_inc(S["fc1_mm"], 1)
                pe.wait_ge(S["fc1_act"], FC * NHALF)
                for t in range(T):
                    for c in range(FC):
                        mm = pe.matmul(bank_t(4, t), tile(A[:, c, :], t), wfc2[:, c, :], start=(c == 0), stop=(c == FC - 1))
                    mm.then_inc(S["fc2_mm"], 1)

                turn("b0", 6)
                route("rb", E0, wrout[:, :], 7)
                zero(0)
                zero(1)

                def up(u):
                    if u >= 3:
                        pe.wait_ge(S["up_act"], u - 2)
                    pe.matmul(P[:, 2 + u % 3, :], wup[:, u // NHALF, :], half(hT, u % 2), start=True, stop=True).then_inc(S["up_mm"], 1)

                def spread(u):
                    if u - NHALF >= 2:
                        pe.wait_ge(S["up_gated"], u - NHALF - 1)
                    pe.matmul(P[:, 5 + u % 2, :], selb[:, u // NHALF - 1, :], half(grows, u % 2), start=True, stop=True).then_inc(S["bcb_mm"], 1)

                def down(u):
                    if u < NHALF:
                        pe.wait_ge(S["up_act"], u + 1)
                    else:
                        pe.wait_ge(S["up_gated"], u - NHALF + 1)
                    f = A[:, (0 if u < NHALF else 2) + (u % 4) // 2, (u % 2) * HALF:(u % 2 + 1) * HALF]
                    for t in range(TPH):
                        mm = pe.matmul(bank_t(0, u % 2 * TPH + t), tile(f, t), wdown[:, u // NHALF, :],
                                       start=False, stop=False)
                    mm.then_inc(S["downb_mm"], 1)

                up(0)
                up(1)
                down(0)
                up(2)
                down(1)
                turn_gates("rb", 7)
                pe.wait_ge(S["rb_rows"], 1)
                spread(2)
                for u in range(2, CH0 * NHALF):
                    if u + 1 < CH0 * NHALF:
                        up(u + 1)
                        spread(u + 1)
                    down(u)
                close(0).then_inc(S["downb_end"], 1)
                close(1).then_inc(S["downb_end"], 1)

                turn("c1", 6)

                def project_v(s, n):
                    pe.wait_ge(S[f"wh_in{s}"], 8 * (n - s) + 16)
                    if not isinstance(n, int) or n > 0:
                        pe.wait_ge(S["m_in"], n)
                    for t in range(T):
                        mm = pe.matmul(P[:, 6, t * DH1:(t + 1) * DH1], tile(hT, t), whead[s][:, 2 * DH1:3 * DH1], start=True, stop=True)
                    mm.then_inc(S["v_mm"], 1)

                def project_qk(s, n):
                    pe.wait_ge(S["v_low"], n + 1)
                    for i in range(NHALF):
                        mm = pe.matmul(P[:, 6 + i, :], whead[s][:, 0:2 * DH1], half(hT, i), start=True, stop=True)
                    mm.then_inc(S["qk_mm"], 1)

                def near(out, n, parts, stop):
                    for part in range(parts):
                        mm = pe.matmul(out, distb[:, :], diagb[:, 3 * n + part, :], start=False, stop=(stop and part == parts - 1))
                    return mm

                def max_tile(s, n, t):
                    if t == 0:
                        pe.wait_ge(S["k_aux"], n + 1)
                        pe.wait_ge(S["k_lo"], n + 1)
                    for i in range(NHALF):
                        if t > 0:
                            pe.wait_ge(S["max_red"], (n * T + t) * NHALF + i - 1)
                        mine = i == t // TPH
                        mm = pe.matmul(P[:, 6 + i, :], tile(Qa[s][0:MROW, :], t), half(Ka[s][0:MROW, :], i), start=True, stop=not mine)
                        if mine:
                            mm = near(P[:, 6 + i, (t % TPH) * 128:(t % TPH + 1) * 128], n, 1, True)
                        mm.then_inc(S["max_mm"], 1)

                def turn_max(n):
                    pe.wait_ge(S["m_mid"], n + 1)
                    for t in range(T):
                        mm = pe.matmul(P[0:2, 6 + t // TPH, (t % TPH) * 128:(t % TPH + 1) * 128], mparts[:, t, :], identb[:, :], start=True, stop=True)
                    mm.then_inc(S["m_row"], 1)

                def scores(k, j, s, n):
                    if j == 0:
                        pe.wait_ge(S["m_in"], n + 1)
                        pe.wait_ge(S["k_dup"], n + 1)
                    if not isinstance(k, int) or k > 0:
                        pe.wait_ge(S["exp_done"], k - 1 + EXP_AT)
                    bank = 2 * (j % 2)
                    for i in (1 - j // TPH, j // TPH):
                        pe.matmul(P[:, bank + i, :], tile(Ka[s][0:KEXACT, :], j), half(Qa[s][0:KEXACT, :], i), start=True, stop=False)
                        if i == j // TPH:
                            near(P[:, bank + i, (j % TPH) * 128:(j % TPH + 1) * 128], n, 3, False)
                        mm = pe.matmul(P[:, bank + i, :], tile(Kb[s], j), half(Qb[s], i), start=False, stop=True)
                    mm.then_inc(S["st_mm"], 1)

                def weigh_high(k, j, s, n):
                    pe.wait_ge(S["p_high"], k + 1)
                    if j == 0:
                        pe.wait_ge(S["v_low"], n + 1)
                        pe.wait_ge(S["o_copied"], n + COPIED_AT)
                        pe.wait_ge(S["s_copied"], n + COPIED_AT)
                    for v, starts in ((Vh[s], j == 0), (Vl[s], False)):
                        for i in range(NHALF):
                            pe.matmul(P[:, 4 + i, :], v[:, j, :], half(phigh[j % RING], i), start=starts, stop=False)

                def weigh_low(k, j, s):
                    pe.wait_ge(S["p_low"], k + 1 + PLOW_AT)
                    for i in range(NHALF):
                        mm = pe.matmul(P[:, 4 + i, :], Vh[s][:, j, :], half(plow[j % 2], i), start=False, stop=(j == T - 1))
                    mm.then_inc(S["pv_done"], 1)

                def pair(p, is_last):
                    for j in range(2 * T):
                        k, s, jj = 2 * T * p + j, j // T, j % T
                        n = 2 * p + s
                        ahead = not (is_last and s == 1)
                        before, after = MAX_TILES[jj]
                        if ahead:
                            for t in before:
                                max_tile(1 - s, n + 1, t)
                        if jj < T - 1:
                            scores(k + 1, jj + 1, s, n)
                        if ahead and jj == 0:
                            project_v(1 - s, n + 1)
                        if ahead and jj == 1:
                            project_qk(1 - s, n + 1)
                        if ahead:
                            for t in after:
                                max_tile(1 - s, n + 1, t)
                        if ahead and jj == T - 1:
                            turn_max(n + 1)
                        weigh_high(k, jj, s, n)
                        if jj > 0:
                            weigh_low(k - 1, jj - 1, s)
                        if ahead and jj == T - 1:
                            scores(k + 1, 0, 1 - s, n + 1)
                        if jj == T - 1:
                            weigh_low(k, jj, s)

                pe.sem_inc(S["st_mm"], ST_AT)
                pe.sem_inc(S["pv_done"], PV_AT)
                project_v(0, 0)
                project_qk(0, 0)
                for t in range(T):
                    max_tile(0, 0, t)
                turn_max(0)
                scores(0, 0, 0, 0)
                with pe.Fori(0, PAIRS - 1) as p:
                    pair(p, False)
                pair(PAIRS - 1, True)

                pe.wait_ge(S["o_norm"], PAIRS * NCHUNK + NORM_AT)
                for t in range(T):
                    for c in range(PAIRS):
                        mm = pe.matmul(bank_t(0, t), tile(A[:, c, :], t), wo[:, c, :], start=(c == 0), stop=(c == PAIRS - 1))
                    mm.then_inc(S["o1_mm"], 1)

                turn("d0", 6)
                route("rd", E1, wgate[:, :], 2)
                zero(0)
                zero(1)
                turn_gates("rd", 3)
                pe.wait_ge(S["rd_rows"], 1)

                def spread_gate(n):
                    for i in range(NHALF):
                        if not isinstance(n, int) or n > 0:
                            pe.wait_ge(S["gates_in"], n * NHALF - NHALF + i + 1)
                        pe.matmul(P[:, 6 + i, :], seld[:, n, :], half(grows, i), start=True, stop=True).then_inc(S["bcd_mm"], 1)

                def parts(out, q, lo, high, low, starts, stops):
                    cols = slice(lo, lo + 128)
                    pe.matmul(out, wh[q][:, cols], high, start=starts, stop=False)
                    pe.matmul(out, wl[q][:, cols], high, start=False, stop=False)
                    return pe.matmul(out, wh[q][:, cols], low, start=False, stop=stops)

                def down_unit(c, q, u):
                    i = u % 2
                    pe.wait_ge(S["gu_low"], c + 1 + UNIT_AT)
                    parts(P[:, i, :], q, 2 * F1 + u // NHALF * 128, half(guh, i), half(gul, i), False, False).then_inc(S["downd_mm"], 1)

                def expert(n, q):
                    pe.wait_ge(S["w_low"], 3 * n + 3)
                    for u in range(UNITS):
                        c, f, i = n * UNITS + u, u // NHALF * 128, u % 2
                        pe.wait_ge(S["silu_done"], c - 1 + UNIT_AT)
                        parts(P[:, 2 + i, :], q, f, half(hTh, i), half(hTl, i), True, True).then_inc(S["w1_mm"], 1)
                        pe.wait_ge(S["gu_done"], c - 1 + UNIT_AT)
                        parts(P[:, 4 + i, :], q, F1 + f, half(hTh, i), half(hTl, i), True, True).then_inc(S["w3_mm"], 1)
                        if u >= 2:
                            down_unit(c - 2, q, u - 2)
                        elif not isinstance(n, int):
                            down_unit(c - 2, 1 - q, UNITS - 2 + u)
                        if u == NEXT:
                            spread_gate(n + 1)

                pe.sem_inc(S["downd_mm"], UNIT_AT)
                spread_gate(0)
                pe.wait_ge(S["hT_low"], 1)
                expert(0, 0)
                with pe.Fori(0, (EX1 - 1) // 2) as r:
                    expert(2 * r + 1, 1)
                    expert(2 * r + 2, 0)
                down_unit(EX1 * UNITS - 2, 0, UNITS - 2)
                down_unit(EX1 * UNITS - 1, 0, UNITS - 1)
                close(0).then_inc(S["downd_end"], 1)
                close(1).then_inc(S["downd_end"], 1)
                pe.wait_ge(S["ydT_copied"], 1)
                for t in range(T):
                    tr = pe.transpose(bank_t(2, t), tile(A[:, 3, :], t), identf[:, :])
                tr.then_inc(S["yd_turned"], 1)
                end_batch(pe, b)


def kernel(**inputs):
    import concourse.bacc as bacc
    from concourse.bass_utils import run_bass_kernel_spmd as run

    g = {k: np.asarray(v) for k, v in inputs.items()}
    consts, aux = constants()
    flat = lambda w: np.ascontiguousarray(w)
    per_chunk = lambda w: flat(w.reshape(-1, 128, w.shape[-1]).transpose(1, 0, 2))

    def heads(w):
        return w.reshape(D, H1, DH1).transpose(1, 0, 2)

    shared_w1, shared_w3 = (g[n].transpose(1, 0, 2).reshape(D, F1) for n in ("L1_ffn_w1_s", "L1_ffn_w3_s"))
    w1 = np.concatenate([g["L1_ffn_w1_e"], shared_w1[None]])
    w3 = np.concatenate([g["L1_ffn_w3_e"], shared_w3[None]])
    w2 = np.concatenate([g["L1_ffn_w2_e"], g["L1_ffn_w2_s"].reshape(1, F1, D)])
    w2 = w2.reshape(EX1, FCH, 128, D).transpose(0, 2, 1, 3).reshape(EX1, 128, F1)
    up = np.concatenate([g["L0_ffn_shared_up"], g["L0_ffn_routed_up"]]).reshape(CH0, 128, D)
    down = np.concatenate([g["L0_ffn_shared_down"], g["L0_ffn_routed_down"]]).transpose(0, 2, 1).reshape(CH0, 128, D)
    arrays = {
        "x": flat(g["L0_attn_x"].reshape(B, T, 128, D).transpose(0, 2, 1, 3)),
        "consts": consts, "aux": aux,
        "wqkv0": flat(g["L0_attn_qkv_w"].T), "wproj": flat(g["L0_attn_proj_w"].T),
        "wfc1": flat(g["L0_attn_fc1_w"].T), "wfc2": per_chunk(g["L0_attn_fc2_w"].T),
        "wup": flat(up.transpose(2, 0, 1)), "wdown": flat(down.transpose(1, 0, 2)),
        "wrout": flat(g["L0_ffn_router_w"].T), "wgate": flat(g["L1_ffn_gate_W"].T),
        "wo": per_chunk(g["L1_attn_Wo"]),
        "vecs": flat(np.stack([g["L0_attn_norm1_g"], g["L0_attn_norm1_b"], g["L0_attn_norm2_g"], g["L0_attn_norm2_b"],
                               *g["L0_attn_fc1_b"].reshape(FC, 128), g["L1_attn_ln_gamma"], g["L1_attn_ln_beta"]], axis=1)),
        "biases": flat(np.stack([g["L0_attn_proj_b"], g["L0_attn_fc2_b"]])),
        "wmod": flat(np.concatenate([g["L0_wmod"], g["L1_wmod"]], axis=1)),
        "cT": flat(np.stack([g["L0_c"].T, g["L1_c"].T], axis=1)),
        "whead": flat(np.concatenate([heads(g["L1_attn_Wq"]), heads(g["L1_attn_Wk"]), heads(g["L1_attn_Wv"])], axis=2)),
        "wex": flat(np.concatenate([w1, w3, w2], axis=2)),
    }
    nc = bacc.Bacc("TRN2", target_bir_lowering=False, num_devices=1)
    a = {n: nc.dram_tensor(f"in_{n}", v.shape, F32, kind="ExternalInput").ap() for n, v in arrays.items()}
    a["out"] = nc.dram_tensor("out_x", [B, 128, T, D], F32, kind="ExternalOutput").ap()
    a["modrows"] = nc.dram_tensor("modrows", [B, 2 * MODS * D], F32).ap()
    network(nc, a)
    r = run(nc, [{f"in_{n}": v for n, v in arrays.items()}], core_ids=[0])
    return r.results[0]["out_x"].transpose(0, 2, 1, 3).reshape(B, N, D)
```

```python
from contextlib import ExitStack

import numpy as np

import concourse.bass as bass
from concourse import mybir

F32 = mybir.dt.float32
F32R = mybir.dt.float32r
BF16 = mybir.dt.bfloat16
ACT = mybir.ActivationFunctionType
ALU = mybir.AluOpType
AX = mybir.AxisListType

B, N, D = 4, 1024, 128
T = N // 128
HALF = 512
NHALF = N // HALF
TPH = T // NHALF
EPS_LN = 1e-5
EPS_ATTN = 1e-6
H0, DH0 = 16, 8
HID = 512
FC = HID // 128
E0, K0, SH0 = 16, 4, 2
CH0 = (E0 + SH0) // 2
H1, DH1 = 16, 64
PAIRS = H1 // 2
E1, K1N, F1 = 8, 2, 512
EX1 = E1 + 1
FCH = F1 // 128
UNITS = FCH * NHALF
WBUF = 2
NEXT = 1
RING = 4
DHIGH = 1
J_SCALE = 3
NSCALE = 4
NCHUNK = T
MODS = 6
GW = 16
NAUX = 32
MROW = 96
KEXACT = MROW + 2
ST_AT, EXP_AT, PV_AT, COPIED_AT, NORM_AT, UNIT_AT, PLOW_AT = 1, 1, RING, 1, 1, 2, 1

MAX_TILES = [([], []), ([], []), ([], []), ([0], [1]), ([2], [3]), ([4], [5]), ([6], [7]), ([], [])]

C_IDENT, C_DIST, C_MASK, C_SLOPE = 0, 128, 256, 384
C_SELB = C_SLOPE + 3 * H1
C_SELD = C_SELB + (CH0 - 1) * 128
C_AUXQ = C_SELD + (EX1 + 1) * 128
C_END = C_AUXQ + N


def split12(x):
    x = x.astype(np.float32)
    c = (x * np.float32(4097)).astype(np.float32)
    hi = (c - (c - x)).astype(np.float32)
    return hi, (x - hi).astype(np.float32)


def cut8(x):
    return (x.astype(np.float32).view(np.uint32) & np.uint32(0xFFFF0000)).view(np.float32)


def constants():
    c = np.zeros((128, C_END), np.float32)
    i = np.arange(128)
    c[:, C_IDENT:C_IDENT + 128] = np.eye(128)
    c[:, C_DIST:C_DIST + 128] = -np.abs(i[:, None] - i[None, :])
    c[:, C_MASK:C_MASK + 128] = (i[:, None] // DH0) == (i[None, :] // DH0)
    slope = (np.float32(2.0) ** (np.float32(-8.0) / np.arange(H1, 0, -1).astype(np.float32))).astype(np.float32)
    s8 = slope * np.float32(DH1 ** 0.5)
    a = cut8(s8)
    m = cut8(s8 - a)
    for h in range(H1):
        c[:, C_SLOPE + 3 * h:C_SLOPE + 3 * h + 3] = [a[h], m[h], s8[h] - a[h] - m[h]]
    for k in range(CH0 - 1):
        for part in range(3):
            c[part * GW + 2 * k, C_SELB + 128 * k:C_SELB + 128 * k + 64] = 1
            c[part * GW + 2 * k + 1, C_SELB + 128 * k + 64:C_SELB + 128 * k + 128] = 1
    for e in range(EX1):
        for part in range(3):
            c[part * GW + e, C_SELD + 128 * e:C_SELD + 128 * e + 128] = 1
    for t in range(T):
        cols = slice(C_AUXQ + 128 * t, C_AUXQ + 128 * t + 128)
        c[64 + t, cols] = 1
        c[64 + T + t, cols] = 1
        c[64 + 2 * T + t, cols] = i
        c[64 + 3 * T + t, cols] = i
    aux = np.zeros((H1, NAUX, N), np.float32)
    j = np.arange(N)
    for t in range(T):
        d = t - j // 128
        base = (-np.sign(d) * (128 * d - j % 128)).astype(np.float32)
        for h in range(H1):
            aux[h, t], aux[h, T + t] = split12(s8[h] * base)
            aux[h, 2 * T + t], aux[h, 3 * T + t] = split12(-s8[h] * np.sign(d).astype(np.float32))
    return c, aux


LN_TAGS = ["a2", "b0", "c0", "c1", "d0"]
TR_TAGS = ["a1", "a2", "b0", "c1", "d0"]
BATCH_SEMS = (
    ["ln_moments", "ln_eps", "ln_rstd", "ln_norm", "modulated", "turned", "hT_dve", "hT_act",
     "x_in", "mod_in", "vec_copied", "next_in", "next_mod",
      "f_moments", "f_eps", "f_rstd", "f_h", "f_xn", "wfc2_scaled", "wdown_scaled", "wo_scaled"]
    + ["q0_mm", "k0_mm", "q0_min", "k0_min", "q0_exp", "k0_exp", "q0_done", "k0_done", "v0_copied",
       "kv_mm", "ks_mm", "kv_masked", "ks_masked", "num_mm", "den_mm", "den_eps", "den_inv", "o0_tok", "o0_turned", "o0_done", "o0_done_a",
       "proj_mm", "h_bias", "x1_done", "x1_bias", "fc1_mm", "fc1_act", "fc2_mm", "x1_scaled", "x_ready", "xa_done"]
    + [f"{t}_{n}" for t in ("rb", "rd") for n in ("mm", "sub", "exp", "steps", "lo", "turned", "rows")]
    + ["up_mm", "bcb_mm", "up_act", "up_gated", "downb_mm", "downb_end", "xb_done"]
    + ["o1_mm", "xc_done"]
    + ["w1_in0", "w1_in1", "gates_in", "silu_gated", "bcd_mm", "w1_mm", "w3_mm", "silu_done", "gu_done",
       "hT_high", "hT_low", "w_high", "w_low", "gu_high", "gu_low", "ydT_copied", "yd_turned",
       "downd_mm", "downd_end", "xd_done"]
    + ["wh_in0", "wh_in1", "aux_in0", "aux_in1", "v_mm", "v_high", "v_low", "p_high", "p_high_v", "p_low", "qk_mm", "q_hi", "k_hi", "k_aux",
       "k_dup", "k_lo", "q_dup", "q_lo", "max_mm", "max_red", "max_both", "m_hi", "m_mid", "m_row", "m_in",
       "st_mm", "exp_done", "pv_done", "o_copied", "s_copied", "s_inv", "o_norm"]
)


def network(nc, a):
    ctx = ExitStack()
    with ctx:
        def sb(name, shape, dt=F32):
            return ctx.enter_context(nc.sbuf_tensor(name, shape, dt))

        S = {n: ctx.enter_context(nc.semaphore(n)) for n in BATCH_SEMS}
        first, last = S[BATCH_SEMS[0]].num, S[BATCH_SEMS[-1]].num
        assert last - first == len(BATCH_SEMS) - 1
        G = {n: ctx.enter_context(nc.semaphore(n)) for n in
             ("weights_in", "modw_in", "consts_in", "c_silu", "mod_mm", "modT_mm", "mod_abs", "mod_sgn",
              "mod_pm", "mod_one", "mod_out", "modT_copied", "set_done", "pool_set", "batch_ended", "batch_open", "x_out", "passed")}

        wqkv0 = sb("wqkv0", [128, 3 * D])
        wproj = sb("wproj", [128, D])
        wfc1 = sb("wfc1", [128, HID])
        wfc2 = sb("wfc2", [128, FC, D])
        wup = sb("wup", [128, CH0, 128])
        wdown = sb("wdown", [128, CH0, D])
        wrout = sb("wrout", [128, E0])
        wgate = sb("wgate", [128, E1])
        wo = sb("wo", [128, PAIRS, D])
        vecs = sb("vecs", [128, 4 + FC + 2])
        biasb = sb("biasb", [128, 2, D])
        identf = sb("identf", [128, 128])
        identb = sb("identb", [128, 128], BF16)
        distb = sb("distb", [128, 128], BF16)
        mask = sb("mask", [128, 128])
        diagb = sb("diagb", [128, 3 * H1, 128], BF16)
        selb = sb("selb", [128, CH0 - 1, 128], BF16)
        seld = sb("seld", [128, EX1 + 1, 128], BF16)
        zerob = sb("zerob", [128, HALF], BF16)
        onecol = sb("onecol", [128, 1])
        halfneg = sb("halfneg", [128, T])
        modT = sb("modT", [128, 2 * MODS, B])
        modv = sb("modv", [128, 2 * MODS])
        modb = sb("modb", [128, 2 * MODS, D])
        x = sb("x", [128, T, D])
        xn = sb("xn", [128, T, D])
        h = sb("h", [128, T, D])
        hT = sb("hT", [128, N])
        A = sb("A", [128, 8, N])
        cT = sb("cT", [128, 2, B])
        cs = sb("cs", [128, 2, B])
        stats = sb("stats", [128, T, 6])
        mv = sb("mv", [128, T, 2])
        veps = sb("veps", [128, T])
        rstd = sb("rstd", [128, T])
        rmax = sb("rmax", [128, 3, T])
        rlog = sb("rlog", [128, T, GW])
        rexp = sb("rexp", [128, T, GW])
        prob = sb("prob", [128, 2, T, GW + 8])
        top8 = sb("top8", [128, T, 8])
        hit = sb("hit", [128, T, GW + 8])
        gate = sb("gate", [128, 3, T, GW])
        gparts = sb("gparts", [128, T, 3 * GW], BF16)
        grows = sb("grows", [128, N], BF16)
        whead = [sb(f"whead{s}", [128, 3 * DH1]) for s in range(2)]
        auxin = sb("auxin", [96, N])
        Ka = [sb(f"Ka{s}", [128, N], F32R) for s in range(2)]
        Kb = [sb(f"Kb{s}", [128, N], F32R) for s in range(2)]
        Qa = [sb(f"Qa{s}", [128, N], F32R) for s in range(2)]
        Qb = [sb(f"Qb{s}", [128, N], F32R) for s in range(2)]
        Vh = [sb(f"Vh{s}", [128, T, 128], F32R) for s in range(2)]
        Vl = [sb(f"Vl{s}", [128, T, 128], F32R) for s in range(2)]
        pfull = sb("pfull", [128, 2, N])
        R = sb("R", [128, RING + 2, N], F32R)
        opair = sb("opair", [128, N])
        spair = sb("spair", [128, N])
        small = opair[:, 0:256].rearrange("p (a b) -> p a b", b=128)
        mhalf = sb("mhalf", [128, NHALF, T])
        mneg = sb("mneg", [128, T])
        mparts = sb("mparts", [128, T, 2], BF16)
        wex = [sb(f"wex{i}", [128, 3 * F1]) for i in range(WBUF)]

        P = ctx.enter_context(nc.psum_tensor("P", [128, 8, HALF], F32))

        def tok_(t):
            return t.rearrange("p (t d) -> p t d", d=D)

        phigh = [R[:, i, :] for i in range(RING)]
        plow = [R[:, RING + i, :] for i in range(2)]
        rows_r = R[:, :, :].rearrange("p a b -> p (a b)")
        wh, wl = ([rows_r[:, (2 * j + i) * 3 * F1:(2 * j + i + 1) * 3 * F1] for i in range(WBUF)] for j in range(2))
        hTh, hTl = Kb[0], Qb[0]
        guh, gul = Kb[1], Qb[1]
        gatesb = [opair, spair]
        xnext, modnext = tok_(A[:, 5, :]), A[:, 6, 0:2 * D].rearrange("p (m d) -> p m d", d=D)
        pflat = pfull[:, :, :].rearrange("p a b -> p (a b)")
        wfc2s = pflat[:, 0:FC * D].rearrange("p (c d) -> p c d", d=D)
        wdowns = pflat[:, FC * D:(FC + CH0) * D].rearrange("p (c d) -> p c d", d=D)
        wos = xn
        silu, gsilu, gu = A[:, 0, :], A[:, 1, :], A[:, 2, :]

        def banks(i, n=2, rows=slice(0, 128)):
            return P[rows, i:i + n, :].rearrange("p a b -> p (a b)")

        def tiles(i):
            return P[:, i:i + 2, :].rearrange("p a (t d) -> p (a t) d", d=D)

        def half(t, i):
            return t[:, i * HALF:(i + 1) * HALF]

        def tok(t):
            return t.rearrange("p (t d) -> p t d", d=D)

        def over(v, shape):
            return v.unsqueeze(1).to_broadcast(shape)

        def col(v, n):
            return v.unsqueeze(2).to_broadcast([128, T, n])

        vpsum = P[:, 6, :].rearrange("p (t d) -> p t d", d=DH1)

        def wait_high(e, n, j):
            if j < DHIGH:
                e.wait_ge(S["p_high_v"], n * DHIGH + j + 1)
            else:
                e.wait_ge(S["p_high"], n * (T - DHIGH) + j - DHIGH + 1)

        def bank_t(i, t):
            return P[:, i + t // TPH, (t % TPH) * D:(t % TPH + 1) * D]

        def end_batch(e, b):
            e.drain().then_inc(G["batch_ended"], 1)
            v = e.snap(b + 2) if not isinstance(b, int) else b + 2
            e.wait_ge(G["batch_open"], v)
            e.sem_inc(G["passed"], 1)

        block = ctx.enter_context(nc.Block())
        NLOAD = 11
        NSET, NPOOL = 2, 10

        @block.sync
        def _(sp):
            sp.dma_start(cT[:, :, :], a["cT"]).then_inc(G["modw_in"], 16)
            sp.dma_start(modb[:, :, :].rearrange("p a b -> p (a b)"), a["wmod"]).then_inc(G["modw_in"], 16)

            def load_rows(b):
                sp.dma_start(A[:, 5, :].rearrange("p (t d) -> p t d", d=D), a["x"][b]).then_inc(S["next_in"], 16)

            def load_mods(b):
                sp.dma_start(modnext, a["modrows"].rearrange("b (m d) -> b m d", d=D)[b, 0:2].partition_broadcast(128)).then_inc(S["next_mod"], 16)

            load_rows(0)
            sp.dma_start(A[:, 0:5, :].rearrange("p a b -> p (a b)")[:, 0:C_END], a["consts"]).then_inc(G["consts_in"], 16)
            for dst, src in ((wqkv0[:, :], a["wqkv0"]), (wproj[:, :], a["wproj"]), (wfc1[:, :], a["wfc1"]),
                             (wfc2[:, :, :], a["wfc2"]), (wup[:, :, :], a["wup"]), (wdown[:, :, :], a["wdown"]),
                             (wrout[:, :], a["wrout"]), (wgate[:, :], a["wgate"]), (wo[:, :, :], a["wo"]),
                             (vecs[:, :], a["vecs"]),
                             (biasb[:, :, :], a["biases"].partition_broadcast(128))):
                sp.dma_start(dst, src).then_inc(G["weights_in"], 16)

            sp.wait_ge(G["mod_one"], 1)
            sp.dma_start(a["modrows"], A[0:B, 6:8, :].rearrange("p a b -> p (a b)")[:, 0:2 * MODS * D]).then_inc(G["mod_out"], 16)
            sp.wait_ge(G["mod_out"], 16)
            sp.sem_inc(G["x_out"], 16)

            load_mods(0)

            def meet(v):
                sp.wait_ge(G["batch_ended"], v)
                sp.sem_inc(G["passed"], 1)
                sp.sem_clear(range(first, last + 1))
                sp.drain().then_inc(G["batch_open"], 1)

            sp.wait_ge(G["modT_copied"], 7)
            sp.wait_ge(G["set_done"], NSET)
            sp.wait_ge(G["pool_set"], NPOOL)

            sp.wait_ge(S["next_in"], 16)
            sp.wait_ge(S["next_mod"], 16)
            meet(4)
            with sp.Fori(0, B) as b:
                v = sp.snap(b * 16 + 16)
                sp.wait_ge(G["x_out"], v)
                sp.sem_inc(G["passed"], 1)
                sp.dma_start(x[:, :, :], a["x"][b]).then_inc(S["x_in"], 16)
                sp.dma_start(modb[:, :, :], a["modrows"].rearrange("b (m d) -> b m d", d=D)[b].partition_broadcast(128)).then_inc(S["mod_in"], 16)

                def load_head(g, s):
                    sp.dma_start(whead[s][:, :], a["whead"][g]).then_inc(S[f"wh_in{s}"], 16)

                def load_aux(g, s):
                    sp.dma_start(auxin[64:96, :], a["aux"][g]).then_inc(S[f"aux_in{s}"], 16)

                load_head(0, 0)
                load_head(1, 1)
                load_aux(0, 0)
                for e in range(WBUF):
                    sp.dma_start(wex[e][:, :], a["wex"][e]).then_inc(S[f"w1_in{e}"], 16)
                with sp.Fori(0, PAIRS - 1) as p:
                    va, vb = sp.snap(2 * p + 1), sp.snap(2 * p + 2)
                    sp.wait_ge(S["k_aux"], va)
                    sp.sem_inc(G["passed"], 1)
                    load_aux(2 * p + 1, 1)
                    sp.wait_ge(S["qk_mm"], va)
                    sp.sem_inc(G["passed"], 1)
                    load_head(2 * p + 2, 0)
                    sp.wait_ge(S["k_aux"], vb)
                    sp.sem_inc(G["passed"], 1)
                    load_aux(2 * p + 2, 0)
                    sp.wait_ge(S["qk_mm"], vb)
                    sp.sem_inc(G["passed"], 1)
                    load_head(2 * p + 3, 1)
                sp.wait_ge(S["k_aux"], H1 - 1)
                load_aux(H1 - 1, 1)

                sp.wait_ge(S["o1_mm"], T)
                load_rows((b + 1) % B)
                load_mods((b + 1) % B)

                with sp.Fori(0, (EX1 - 1) // WBUF - 1) as r:
                    vs = [sp.snap(3 * (r * WBUF + i + 1)) for i in range(WBUF)]
                    for i in range(WBUF):
                        sp.wait_ge(S["w_low"], vs[i])
                        sp.sem_inc(G["passed"], 1)
                        sp.dma_start(wex[i][:, :], a["wex"][(r + 1) * WBUF + i]).then_inc(S[f"w1_in{i}"], 16)
                for e, src in ((EX1 - 1, EX1 - 1), (EX1, 0)):
                    sp.wait_ge(S["w_low"], 3 * (e - WBUF + 1))
                    sp.dma_start(wex[e % WBUF][:, :], a["wex"][src]).then_inc(S[f"w1_in{e % WBUF}"], 16)

                sp.wait_ge(S["xd_done"], 1)
                sp.dma_start(a["out"][b], x[:, :, :]).then_inc(G["x_out"], 16)
                v = sp.snap(b * 4 + 8)
                for i in range(WBUF):
                    sp.wait_ge(S[f"w1_in{i}"], 16 * (EX1 + 1) // WBUF)
                sp.wait_ge(S["next_in"], 16)
                sp.wait_ge(S["next_mod"], 16)
                meet(v)
            sp.wait_ge(G["x_out"], 16 * B + 16)

        @block.gpsimd
        def _(pool):
            pool.memset(halfneg[:, :], -0.5).then_inc(G["pool_set"], 1)
            pool.memset(zerob[:, :], 0.0).then_inc(G["pool_set"], 1)
            pool.memset(onecol[:, :], 1.0).then_inc(G["pool_set"], 1)
            pool.memset(grows[:, :], 0.0).then_inc(G["pool_set"], 1)
            pool.memset(prob[:, :, :, :], -1.0).then_inc(G["pool_set"], 1)
            for s in range(2):
                beside = slice(64 - 64 * s, 128 - 64 * s)
                pool.memset(Vh[s][:, :, beside].bitcast(F32), 1.0).then_inc(G["pool_set"], 1)
                pool.memset(Vl[s][:, :, beside].bitcast(F32), 0.0).then_inc(G["pool_set"], 1)
            pool.memset(gate[:, :, :, :], 0.0).then_inc(G["pool_set"], 1)
            pool.wait_ge(G["pool_set"], NPOOL)

            def front_root(r, nth):
                pool.wait_ge(S["f_eps"], 2 * r + nth)
                pool.tensor_tensor(rstd[:, 0:2], veps[:, 0:2], halfneg[:, 0:2], ALU.pow).then_inc(S["f_rstd"], 1)

            cst_ = A[:, 0:5, :].rearrange("p a b -> p (a b)")
            for nth in (1, 2):
                pool.wait_ge(S["f_eps"], nth)
                pool.tensor_tensor(rstd[:, :], veps[:, :], halfneg[:, :], ALU.pow).then_inc(S["f_rstd"], 1)
                if nth == 1:
                    pool.wait_ge(G["consts_in"], 16)
                    pool.tensor_tensor(diagb[:, :, :], over(cst_[:, C_IDENT:C_IDENT + 128], [128, 3 * H1, 128]),
                                      cst_[:, C_SLOPE:C_SLOPE + 3 * H1].unsqueeze(2).to_broadcast([128, 3 * H1, 128]), ALU.mult)
            end_batch(pool, -1)
            with pool.Fori(0, B) as b:
                def scale(out, w, m, sem):
                    pool.tensor_tensor(out, w, over(modb[:, m, :], list(w.shape)), ALU.mult).then_inc(S[sem], 1)

                pool.wait_ge(S["mod_in"], 16)
                scale(wfc2s, wfc2[:, :, :], 2, "wfc2_scaled")
                scale(wdowns, wdown[:, :, :], 5, "wdown_scaled")

                def inverse_root(tag):
                    for i in range(NHALF):
                        ts = slice(i * TPH, (i + 1) * TPH)
                        pool.wait_ge(S["ln_eps"], NHALF * LN_TAGS.index(tag) + i + 1)
                        pool.tensor_tensor(rstd[:, ts], veps[:, ts], halfneg[:, ts], ALU.pow).then_inc(S["ln_rstd"], 1)

                for tag in LN_TAGS[:-1]:
                    inverse_root(tag)

                pool.wait_ge(S["turned"], NHALF * (TR_TAGS.index("c1") + 1))
                scale(wos[:, :, :], wo[:, :, :], MODS + 2, "wo_scaled")

                pool.sem_inc(S["p_low"], PLOW_AT)
                def apply_inverse(p, c):
                    pool.wait_ge(S["o_copied"], 2 * p + 2 + COPIED_AT)
                    pool.wait_ge(S["s_inv"], p * NCHUNK + (c + 1) * NCHUNK // NSCALE)
                    cols = slice(c * N // NSCALE, (c + 1) * N // NSCALE)
                    pool.tensor_tensor(A[:, p, cols], opair[:, cols], spair[:, cols], ALU.mult).then_inc(S["o_norm"], 1)

                def low_parts(p, has_last):
                    for j in range(2 * T):
                        k = 2 * T * p + j
                        wait_high(pool, 2 * p + j // T, j % T)
                        pool.wait_ge(S["pv_done"], k - 1 + PV_AT)
                        pool.tensor_tensor(plow[j % 2], pfull[:, j % 2, :], phigh[j % RING].bitcast(F32), ALU.subtract).then_inc(S["p_low"], 1)
                        if has_last and J_SCALE <= j < J_SCALE + NSCALE:
                            apply_inverse(p - 1, j - J_SCALE)

                pool.sem_inc(S["o_norm"], NORM_AT)
                low_parts(0, False)
                with pool.Fori(1, PAIRS) as p:
                    low_parts(p, True)
                for c in range(NSCALE):
                    apply_inverse(PAIRS - 1, c)

                inverse_root("d0")

                def low_weights(n, q, m):
                    pool.wait_ge(S["w_high"], 3 * n + m + 1)
                    cols = slice(m * F1, (m + 1) * F1)
                    pool.tensor_tensor(wl[q][:, cols], wex[q][:, cols], wh[q][:, cols].bitcast(F32), ALU.subtract).then_inc(S["w_low"], 1)

                def expert(n, q, r=None):
                    for u in range(UNITS):
                        i = u % 2
                        if r is not None and u in (2, 6):
                            front_root(r, 1 if u == 2 else 2)
                        pool.wait_ge(S["silu_done"], n * UNITS + u + 1 + UNIT_AT)
                        if u == 0:
                            pool.wait_ge(S["gates_in"], n * NHALF + NHALF)
                        pool.wait_ge(S["gu_done"], n * UNITS + u - 1 + UNIT_AT)
                        pool.tensor_tensor(half(gsilu, i), half(silu, i), half(gatesb[q], i), ALU.mult).then_inc(S["silu_gated"], 1)
                        if NEXT < u <= NEXT + 3:
                            low_weights(n + 1, 1 - q, u - NEXT - 1)

                for m in range(3):
                    low_weights(0, 0, m)
                pool.sem_inc(S["silu_gated"], UNIT_AT)
                expert(0, 0)
                with pool.Fori(0, (EX1 - 1) // 2) as r:
                    expert(2 * r + 1, 1, r)
                    expert(2 * r + 2, 0)
                end_batch(pool, b)

        @block.vector
        def _(dve):
            tens = [128, T, D]
            cst = A[:, 0:5, :].rearrange("p a b -> p (a b)")

            def half_moments(tag, i, src):
                nth = NHALF * LN_TAGS.index(tag) + i
                for t in range(i * TPH, (i + 1) * TPH):
                    dve.bn_stats(stats[:, t, :], src[:, t, :]).then_inc(S["ln_moments"], 1)
                dve.wait_ge(S["ln_moments"], (2 * nth + 1) * TPH)
                for t in range(i * TPH, (i + 1) * TPH):
                    dve.bn_aggr(mv[:, t, :], stats[:, t, :]).then_inc(S["ln_moments"], 1)
                dve.wait_ge(S["ln_moments"], (2 * nth + 2) * TPH)
                ts = slice(i * TPH, (i + 1) * TPH)
                dve.tensor_scalar(veps[:, ts], mv[:, ts, 1], EPS_LN, None, ALU.add).then_inc(S["ln_eps"], 1)

            def half_norm(tag, i, src, dst):
                dve.wait_ge(S["ln_rstd"], NHALF * LN_TAGS.index(tag) + i + 1)
                for t in range(i * TPH, (i + 1) * TPH):
                    dve.tensor_scalar(dst[:, t, :], src[:, t, :], mv[:, t, 0:1], rstd[:, t:t + 1],
                                      ALU.subtract, ALU.mult).then_inc(S["ln_norm"], 1)

            def residual(dst, bank, src, i, sem):
                ts = slice(i * TPH, (i + 1) * TPH)
                dve.tensor_tensor(dst[:, ts, :], P[:, bank + i, :].rearrange("p (t d) -> p t d", d=D), src[:, ts, :], ALU.add).then_inc(S[sem], 1)
                dve.wait_ge(S[sem], i + 1)

            def hT_half(tag, bank, scale, bias):
                dve.wait_ge(S["turned"], NHALF * TR_TAGS.index(tag) + 1)
                dve.tensor_scalar(half(hT, 0), P[:, bank, :], scale, bias, ALU.mult, ALU.add).then_inc(S["hT_dve"], 1)

            def router(tag, n, k, bank, bank2, table, factor):
                logits = P[:, bank, 0:T * n].rearrange("p (t e) -> p t e", e=n)
                dve.wait_ge(S[f"{tag}_mm"], 1)
                dve.tensor_reduce(rmax[:, 0, :], logits, AX.X, ALU.max).then_inc(S[f"{tag}_steps"], 1)
                dve.wait_ge(S[f"{tag}_steps"], 1)
                dve.tensor_tensor(rlog[:, :, 0:n], logits, col(rmax[:, 0, :], n), ALU.subtract).then_inc(S[f"{tag}_sub"], 1)
                dve.wait_ge(S[f"{tag}_exp"], 1)
                dve.tensor_reduce(rmax[:, 1, :], rexp[:, :, 0:n], AX.X, ALU.add).then_inc(S[f"{tag}_steps"], 1)
                dve.wait_ge(S[f"{tag}_steps"], 2)
                dve.reciprocal(rmax[:, 2, :], rmax[:, 1, :]).then_inc(S[f"{tag}_steps"], 1)
                dve.wait_ge(S[f"{tag}_steps"], 3)
                pr = prob[:, table, :, 0:n + 8]
                dve.scalar_tensor_tensor(pr[:, :, 0:n], rexp[:, :, 0:n], factor, col(rmax[:, 2, :], n),
                                         ALU.mult, ALU.mult).then_inc(S[f"{tag}_steps"], 1)
                dve.wait_ge(S[f"{tag}_steps"], 4)
                for t in range(T):
                    dve.max(top8[:, t, :], pr[:, t, :]).then_inc(S[f"{tag}_steps"], 1)
                dve.wait_ge(S[f"{tag}_steps"], 4 + T)
                dve.memset(top8[:, :, k:8], -1.0).then_inc(S[f"{tag}_steps"], 1)
                dve.wait_ge(S[f"{tag}_steps"], 5 + T)
                for t in range(T):
                    dve.match_replace(hit[:, t, 0:n + 8], top8[:, t, :], pr[:, t, :], -5.0).then_inc(S[f"{tag}_steps"], 1)
                dve.wait_ge(S[f"{tag}_steps"], 5 + 2 * T)
                dve.scalar_tensor_tensor(gate[:, 0, :, 0:n], hit[:, :, 0:n], -2.0, pr[:, :, 0:n],
                                         ALU.is_lt, ALU.mult).then_inc(S[f"{tag}_steps"], 1)
                dve.wait_ge(S[f"{tag}_steps"], 6 + 2 * T)
                g, r1, r2 = (gate[:, i, :, :] for i in range(3))
                hi, mid, lo = (gparts[:, :, i * GW:(i + 1) * GW] for i in range(3))
                dve.tensor_copy(hi, g).then_inc(S[f"{tag}_steps"], 1)
                dve.wait_ge(S[f"{tag}_steps"], 7 + 2 * T)
                dve.tensor_tensor(r1, g, hi, ALU.subtract).then_inc(S[f"{tag}_steps"], 1)
                dve.wait_ge(S[f"{tag}_steps"], 8 + 2 * T)
                dve.tensor_copy(mid, r1).then_inc(S[f"{tag}_steps"], 1)
                dve.wait_ge(S[f"{tag}_steps"], 9 + 2 * T)
                dve.tensor_tensor(lo, r1, mid, ALU.subtract).then_inc(S[f"{tag}_lo"], 1)
                dve.wait_ge(S[f"{tag}_turned"], 1)
                dve.tensor_copy(grows[0:3 * GW, :], P[0:3 * GW, bank2, :].bitcast(BF16)).then_inc(S[f"{tag}_rows"], 1)

            def moments(src, r, nth):
                dve.sem_inc(G["passed"], 1)
                for i in range(2):
                    dve.bn_stats(stats[:, i, :], src[:, 2 * r + i, :]).then_inc(S["f_moments"], 1)
                dve.wait_ge(S["f_moments"], 8 * r + 4 * nth - 2)
                dve.sem_inc(G["passed"], 1)
                for i in range(2):
                    dve.bn_aggr(mv[:, i, :], stats[:, i, :]).then_inc(S["f_moments"], 1)
                dve.wait_ge(S["f_moments"], 8 * r + 4 * nth)
                dve.tensor_scalar(veps[:, 0:2], mv[:, 0:2, 1], EPS_LN, None, ALU.add).then_inc(S["f_eps"], 1)

            def scaled(dst, src, r, nth, sem):
                dve.wait_ge(S["f_rstd"], 2 * r + nth)
                for i in range(2):
                    dve.tensor_scalar(dst[:, 2 * r + i, :], src[:, 2 * r + i, :], mv[:, i, 0:1], rstd[:, i:i + 1],
                                      ALU.subtract, ALU.mult).then_inc(S[sem], 1)

            def front(r, part):
                if part == 0:
                    dve.wait_ge(S["next_in"], 16)
                    moments(xnext, r, 1)
                elif part == 1:
                    scaled(h, xnext, r, 1, "f_h")
                    dve.wait_ge(S["next_mod"], 16)
                    for step, (m, op) in enumerate(((1, ALU.mult), (0, ALU.add))):
                        dve.wait_ge(S["f_h"], 6 * r + 2 * step + 2)
                        for i in range(2):
                            hi_ = h[:, 2 * r + i, :]
                            dve.tensor_tensor(hi_, hi_, modnext[:, m, :], op).then_inc(S["f_h"], 1)
                elif part == 2:
                    dve.wait_ge(S["f_h"], 6 * r + 6)
                    moments(h, r, 2)
                else:
                    scaled(xn, h, r, 2, "f_xn")

            def first_moments(src, nth):
                for t in range(T):
                    dve.bn_stats(stats[:, t, :], src[:, t, :]).then_inc(S["f_moments"], 1)
                dve.wait_ge(S["f_moments"], (2 * nth - 1) * T)
                for t in range(T):
                    dve.bn_aggr(mv[:, t, :], stats[:, t, :]).then_inc(S["f_moments"], 1)
                dve.wait_ge(S["f_moments"], 2 * nth * T)
                dve.tensor_scalar(veps[:, :], mv[:, :, 1], EPS_LN, None, ALU.add).then_inc(S["f_eps"], 1)

            def first_norm(dst, src, nth, sem):
                dve.wait_ge(S["f_rstd"], nth)
                for t in range(T):
                    dve.tensor_scalar(dst[:, t, :], src[:, t, :], mv[:, t, 0:1], rstd[:, t:t + 1],
                                      ALU.subtract, ALU.mult).then_inc(S[sem], 1)

            dve.wait_ge(S["next_in"], 16)
            first_moments(xnext, 1)

            rows = A[0:B, 6:8, :].rearrange("p a b -> p (a b)")[:, 0:2 * MODS * D]
            dve.wait_ge(G["mod_mm"], 1)
            dve.tensor_copy(rows, P[0:B, 0:3, :].rearrange("p a b -> p (a b)")).then_inc(G["mod_abs"], 1)
            dve.wait_ge(G["mod_abs"], 1)
            r3 = rows.rearrange("p (m d) -> p m d", d=D)
            gs = r3[:, 2::3, :]
            tmp = h[0:B, 0:4, :]
            sg = xn[0:B, 0:4, :]
            dve.scalar_tensor_tensor(tmp, gs, -1.0, gs, ALU.mult, ALU.max).then_inc(G["mod_abs"], 1)
            dve.tensor_scalar(sg, gs, 0.0, 2.0, ALU.is_ge, ALU.mult).then_inc(G["mod_abs"], 1)
            dve.wait_ge(G["mod_abs"], 3)
            dve.tensor_scalar(tmp, tmp, 0.25, None, ALU.max).then_inc(G["mod_sgn"], 1)
            dve.tensor_scalar(sg, sg, -1.0, None, ALU.add).then_inc(G["mod_sgn"], 1)
            dve.wait_ge(G["mod_sgn"], 2)
            dve.tensor_tensor(gs, tmp, sg, ALU.mult)
            dve.tensor_scalar(r3[:, 1::3, :], r3[:, 1::3, :], 1.0, None, ALU.add).then_inc(G["mod_one"], 1)
            dve.wait_ge(G["consts_in"], 16)
            dve.tensor_copy(identf[:, :], cst[:, C_IDENT:C_IDENT + 128])
            dve.tensor_copy(identb[:, :], cst[:, C_IDENT:C_IDENT + 128])
            dve.tensor_copy(distb[:, :], cst[:, C_DIST:C_DIST + 128])
            dve.tensor_copy(mask[:, :], cst[:, C_MASK:C_MASK + 128])
            dve.tensor_copy(selb[:, :, :].rearrange("p a b -> p (a b)"), cst[:, C_SELB:C_SELD])
            dve.tensor_copy(seld[:, :, :].rearrange("p a b -> p (a b)"), cst[:, C_SELD:C_AUXQ])
            for s in range(2):
                dve.tensor_copy(Qa[s][64:96, :], cst[64:96, C_AUXQ:C_END])
                dve.tensor_scalar(Ka[s][96:128, :], cst[96:128, C_AUXQ:C_END], 0.0, 1.0, ALU.mult, ALU.add)\
                    .then_inc(G["set_done"], 1)

            dve.wait_ge(G["modT_mm"], 1)
            dve.tensor_copy(modT[:, :, :], P[:, 3, 0:2 * MODS * B].rearrange("p (m b) -> p m b", b=B)).then_inc(G["modT_copied"], 1)
            dve.wait_ge(G["modT_copied"], 1)
            gT = modT[:, 2::3, :]
            tmpT, sgT = rlog[:, 0:4, 0:B], rexp[:, 0:4, 0:B]
            dve.scalar_tensor_tensor(tmpT, gT, -1.0, gT, ALU.mult, ALU.max).then_inc(G["modT_copied"], 1)
            dve.tensor_scalar(sgT, gT, 0.0, 2.0, ALU.is_ge, ALU.mult).then_inc(G["modT_copied"], 1)
            dve.wait_ge(G["modT_copied"], 3)
            dve.tensor_scalar(tmpT, tmpT, 0.25, None, ALU.max).then_inc(G["modT_copied"], 1)
            dve.tensor_scalar(sgT, sgT, -1.0, None, ALU.add).then_inc(G["modT_copied"], 1)
            dve.wait_ge(G["modT_copied"], 5)
            dve.tensor_tensor(gT, tmpT, sgT, ALU.mult).then_inc(G["modT_copied"], 1)
            dve.tensor_scalar(modT[:, 1::3, :], modT[:, 1::3, :], 1.0, None, ALU.add).then_inc(G["modT_copied"], 1)
            dve.wait_ge(G["modT_copied"], 7)

            first_norm(h, xnext, 1, "f_h")
            dve.wait_ge(S["next_mod"], 16)
            for step, (m, op) in enumerate(((1, ALU.mult), (0, ALU.add))):
                dve.wait_ge(S["f_h"], T + step)
                dve.tensor_tensor(h[:, :, :], h[:, :, :], over(modnext[:, m, :], tens), op).then_inc(S["f_h"], 1)
            dve.wait_ge(S["f_h"], T + 2)
            first_moments(h, 2)
            first_norm(xn, h, 2, "f_xn")
            end_batch(dve, -1)
            with dve.Fori(0, B) as b:
                dve.tensor_copy(modv[:, :], modT[:, :, b]).then_inc(S["vec_copied"], 1)

                dve.wait_ge(S["vec_copied"], 1)
                hT_half("a1", 0, vecs[:, 0:1], vecs[:, 1:2])
                kpsum = P[:, 2:6, :].rearrange("p a (t c) -> p (a t) c", c=2 * D)
                dve.wait_ge(S["k0_mm"], T)
                dve.tensor_scalar(tok(A[:, 2, :]), kpsum[:, :, 0:D], 0.0, None, ALU.min).then_inc(S["k0_min"], 1)
                dve.tensor_copy(tok(A[:, 4, :]), kpsum[:, :, D:2 * D]).then_inc(S["v0_copied"], 1)
                dve.wait_ge(S["k0_exp"], 1)
                dve.scalar_tensor_tensor(tok(A[:, 2, :]), kpsum[:, :, 0:D], 0.0, tok(A[:, 3, :]), ALU.max, ALU.add).then_inc(S["k0_done"], 1)
                dve.wait_ge(S["q0_mm"], 2)
                dve.tensor_scalar(A[:, 0, :], banks(0), 0.0, None, ALU.min).then_inc(S["q0_min"], 1)
                dve.wait_ge(S["q0_exp"], 1)
                dve.scalar_tensor_tensor(A[:, 0, :], banks(0), 0.0, A[:, 1, :], ALU.max, ALU.add).then_inc(S["q0_done"], 1)
                dve.wait_ge(S["ks_mm"], 1)
                by_head = mask[:, :].rearrange("p (h e) -> p h e", e=DH0)[:, :, 0]
                dve.tensor_scalar(small[:, 1, 0:H0], by_head, P[:, 7, 0:1], None, ALU.mult).then_inc(S["ks_masked"], 1)
                dve.wait_ge(S["kv_mm"], 1)
                dve.tensor_tensor(small[:, 0, :], P[:, 6, 0:D], mask[:, :], ALU.mult).then_inc(S["kv_masked"], 1)
                dve.tensor_tensor(h[:, :, :], h[:, :, :], over(biasb[:, 0, :], tens), ALU.add).then_inc(S["h_bias"], 1)
                dve.wait_ge(S["den_mm"], 1)
                dve.tensor_scalar(A[:, 1, 0:T * H0], P[:, 2, 0:T * H0], EPS_ATTN, None, ALU.add).then_inc(S["den_eps"], 1)
                dve.wait_ge(S["den_eps"], 1)
                dve.reciprocal(A[:, 3, 0:T * H0], A[:, 1, 0:T * H0]).then_inc(S["den_inv"], 1)
                dve.wait_ge(S["den_inv"], 1)
                for i in range(NHALF):
                    dve.wait_ge(S["num_mm"], (i + 1) * TPH)
                    z = A[:, 3, i * TPH * H0:(i + 1) * TPH * H0].unsqueeze(2).to_broadcast([128, TPH * H0, DH0])
                    dve.tensor_tensor(half(A[:, 5, :], i).rearrange("p (h e) -> p h e", e=DH0),
                                      P[:, i, :].rearrange("p (h e) -> p h e", e=DH0), z, ALU.mult).then_inc(S["o0_tok"], 1)
                dve.wait_ge(S["o0_turned"], 1)
                dve.tensor_copy(half(A[:, 7, :], 0), P[:, 6, :]).then_inc(S["o0_done"], 1)
                x1 = tok(A[:, 6, :])
                dve.wait_ge(S["h_bias"], 1)
                for i in range(NHALF):
                    dve.wait_ge(S["proj_mm"], (i + 1) * TPH)
                    residual(x1, 4, h, i, "x1_done")
                    half_moments("a2", i, x1)
                for i in range(NHALF):
                    half_norm("a2", i, x1, xn)
                hT_half("a2", 0, vecs[:, 2:3], vecs[:, 3:4])
                dve.tensor_tensor(tok(A[:, 7, :]), tok(A[:, 6, :]), over(biasb[:, 1, :], tens), ALU.add).then_inc(S["x1_bias"], 1)
                dve.wait_ge(S["x1_bias"], 1)
                dve.wait_ge(S["mod_in"], 16)
                dve.tensor_tensor(tok(A[:, 7, :]), tok(A[:, 7, :]), over(modb[:, 2, :], tens), ALU.mult).then_inc(S["x1_scaled"], 1)
                dve.wait_ge(S["x1_scaled"], 1)
                dve.wait_ge(S["x_in"], 16)
                dve.tensor_tensor(x[:, :, :], x[:, :, :], tok(A[:, 7, :]), ALU.add).then_inc(S["x_ready"], 1)
                dve.wait_ge(S["x_ready"], 1)
                for i in range(NHALF):
                    dve.wait_ge(S["fc2_mm"], (i + 1) * TPH)
                    residual(x, 4, x, i, "xa_done")
                    half_moments("b0", i, x)

                for i in range(NHALF):
                    half_norm("b0", i, x, xn)
                hT_half("b0", 6, modv[:, 4:5], modv[:, 3:4])
                router("rb", E0, K0, 7, 7, 0, 1.0)
                for u in range(NHALF, CH0 * NHALF):
                    dve.wait_ge(S["up_act"], u + 1)
                    dve.wait_ge(S["bcb_mm"], u - NHALF + 1)
                    if u - NHALF >= 4:
                        dve.wait_ge(S["downb_mm"], u - 4 + 1)
                    ga_ = A[:, 2 + (u % 4) // 2, (u % 2) * HALF:(u % 2 + 1) * HALF]
                    ac_ = A[:, (u % 4) // 2, (u % 2) * HALF:(u % 2 + 1) * HALF]
                    dve.tensor_tensor(ga_, P[:, 5 + u % 2, :], ac_, ALU.mult).then_inc(S["up_gated"], 1)
                for i in range(NHALF):
                    dve.wait_ge(S["downb_end"], i + 1)
                    residual(x, 0, x, i, "xb_done")
                    half_moments("c0", i, x)

                for i in range(NHALF):
                    half_norm("c0", i, x, xn)
                    ts = slice(i * TPH, (i + 1) * TPH)
                    part = [128, TPH, D]
                    dve.wait_ge(S["ln_norm"], LN_TAGS.index("c0") * T + (i + 1) * TPH)
                    dve.tensor_tensor(h[:, ts, :], xn[:, ts, :], over(modb[:, MODS + 1, :], part), ALU.mult).then_inc(S["modulated"], 1)
                    dve.wait_ge(S["modulated"], 2 * i + 1)
                    dve.tensor_tensor(h[:, ts, :], h[:, ts, :], over(modb[:, MODS, :], part), ALU.add).then_inc(S["modulated"], 1)
                    dve.wait_ge(S["modulated"], 2 * i + 2)
                    half_moments("c1", i, h)
                for i in range(NHALF):
                    half_norm("c1", i, h, xn)
                hT_half("c1", 6, vecs[:, 4 + FC:5 + FC], vecs[:, 5 + FC:6 + FC])

                def invert(p, c):
                    if c == 0:
                        dve.wait_ge(S["s_copied"], 2 * p + 2 + COPIED_AT)
                    cols = slice(c * N // NCHUNK, (c + 1) * N // NCHUNK)
                    dve.reciprocal(spair[:, cols], spair[:, cols]).then_inc(S["s_inv"], 1)

                def prep(s, n, done=None):
                    def high(j):
                        if not (isinstance(n, int) and n == 0):
                            k = T * (n - 1) + j
                            dve.wait_ge(S["exp_done"], k + 1 + EXP_AT)
                            dve.wait_ge(S["pv_done"], k + 1 - RING + PV_AT)
                            dve.tensor_copy(phigh[j], pfull[:, j % 2, :]).then_inc(S["p_high_v"], 1)

                    high(0)
                    dve.wait_ge(S["pv_done"], PV_AT if isinstance(n, int) and n == 0 else T * (n - 1) + PV_AT)
                    dve.wait_ge(S["st_mm"], T * (n - 1) + ST_AT if not (isinstance(n, int) and n == 0) else ST_AT)
                    dve.wait_ge(S[f"aux_in{s}"], 8 * (n - s) + 16)
                    dve.tensor_copy(Ka[s][64:96, :], auxin[64:96, :]).then_inc(S["k_aux"], 1)
                    if done is not None:
                        invert(done, 0)
                    for j in range(1, DHIGH):
                        high(j)
                    dve.wait_ge(S["v_high"], n + 1)
                    dve.tensor_tensor(Vl[s][:, :, 64 * s:64 * s + 64], vpsum, Vh[s][:, :, 64 * s:64 * s + 64].bitcast(F32), ALU.subtract).then_inc(S["v_low"], 1)
                    if done is not None:
                        for c in range(1, 5):
                            invert(done, c)
                    dve.wait_ge(S["q_hi"], n + 1)
                    dve.tensor_tensor(Qb[s][0:64, :], banks(6, 2, slice(0, 64)), Qa[s][0:64, :].bitcast(F32), ALU.subtract).then_inc(S["q_lo"], 1)
                    dve.wait_ge(S["k_hi"], n + 1)
                    dve.tensor_tensor(Kb[s][64:128, :], banks(6, 2, slice(64, 128)), Ka[s][0:64, :].bitcast(F32), ALU.subtract).then_inc(S["k_lo"], 1)
                    dve.tensor_copy(Qb[s][64:128, :], Qa[s][0:64, :].bitcast(F32)).then_inc(S["q_dup"], 1)
                    dve.tensor_copy(Kb[s][0:64, :], Ka[s][0:64, :].bitcast(F32)).then_inc(S["k_dup"], 1)
                    for t in range(T):
                        for i in range(NHALF):
                            dve.wait_ge(S["max_mm"], (n * T + t) * NHALF + i + 1)
                            dve.tensor_reduce(mhalf[:, i, t:t + 1], P[:, 6 + i, :], AX.X, ALU.max, negate=True).then_inc(S["max_red"], 1)
                        if done is not None and t % 2 == 1 and t // 2 < NCHUNK - 5:
                            invert(done, 5 + t // 2)
                    dve.wait_ge(S["max_red"], (n + 1) * T * NHALF)
                    dve.tensor_tensor(mneg[:, :], mhalf[:, 0, :], mhalf[:, 1, :], ALU.min).then_inc(S["max_both"], 1)
                    dve.wait_ge(S["max_both"], n + 1)
                    dve.tensor_copy(mparts[:, :, 0], mneg[:, :]).then_inc(S["m_hi"], 1)
                    dve.wait_ge(S["m_hi"], n + 1)
                    dve.tensor_tensor(mparts[:, :, 1], mneg[:, :], mparts[:, :, 0], ALU.subtract).then_inc(S["m_mid"], 1)

                def sums(s, p):
                    dve.wait_ge(S["pv_done"], (2 * p + s + 1) * T + PV_AT)
                    dve.wait_ge(S["o_norm"], p * NSCALE + NORM_AT)
                    dve.tensor_copy(spair[64 * s:64 * s + 64, :], banks(4, 2, slice(64 - 64 * s, 128 - 64 * s))).then_inc(S["s_copied"], 1)

                dve.sem_inc(S["s_copied"], COPIED_AT)
                prep(0, 0)
                prep(1, 1)
                sums(0, 0)
                with dve.Fori(0, PAIRS - 1) as p:
                    prep(0, 2 * p + 2)
                    sums(1, p)
                    prep(1, 2 * p + 3, p)
                    sums(0, p + 1)
                for j in range(DHIGH):
                    k = T * (H1 - 1) + j
                    dve.wait_ge(S["exp_done"], k + 1 + EXP_AT)
                    dve.wait_ge(S["pv_done"], k + 1 - RING + PV_AT)
                    dve.tensor_copy(phigh[j], pfull[:, j % 2, :]).then_inc(S["p_high_v"], 1)
                sums(1, PAIRS - 1)
                for c in range(NCHUNK):
                    invert(PAIRS - 1, c)

                for i in range(NHALF):
                    dve.wait_ge(S["o1_mm"], (i + 1) * TPH)
                    residual(x, 0, x, i, "xc_done")
                    half_moments("d0", i, x)

                for i in range(NHALF):
                    half_norm("d0", i, x, xn)
                hT_half("d0", 6, modv[:, MODS + 4:MODS + 5], modv[:, MODS + 3:MODS + 4])
                dve.memset(gate[:, 0, :, E1:E1 + 1], 0.5 / E1)
                router("rd", E1, K1N, 2, 3, 1, 0.5)

                def low_unit(c, i):
                    dve.wait_ge(S["gu_high"], c + 1)
                    dve.wait_ge(S["downd_mm"], c - 1 + UNIT_AT)
                    dve.tensor_tensor(half(gul, i), half(gu, i), half(guh, i).bitcast(F32), ALU.subtract).then_inc(S["gu_low"], 1)

                def expert(n, r=None, parts=()):
                    for u in range(UNITS):
                        c, i = n * UNITS + u, u % 2
                        for at, part in parts:
                            if at == u:
                                front(r, part)
                        if not (isinstance(c, int) and c == 0):
                            low_unit(c - 1, 1 - i)
                        dve.wait_ge(S["w3_mm"], c + 1)
                        dve.wait_ge(S["silu_gated"], c + 1 + UNIT_AT)
                        dve.wait_ge(S["gu_low"], c - 1 + UNIT_AT)
                        dve.tensor_tensor(half(gu, i), P[:, 4 + i, :], half(gsilu, i), ALU.mult).then_inc(S["gu_done"], 1)

                dve.wait_ge(S["hT_high"], 1)
                dve.tensor_tensor(hTl[:, :], hT[:, :], hTh[:, :].bitcast(F32), ALU.subtract).then_inc(S["hT_low"], 1)
                dve.sem_inc(S["gu_done"], UNIT_AT)
                dve.sem_inc(S["gu_low"], UNIT_AT)
                expert(0)
                with dve.Fori(0, (EX1 - 1) // 2) as r:
                    expert(2 * r + 1, r, ((1, 0), (3, 1), (5, 2)))
                    expert(2 * r + 2, r, ((1, 3),))
                low_unit(EX1 * UNITS - 1, 1)
                dve.wait_ge(S["downd_end"], NHALF)
                dve.tensor_scalar(A[:, 3, :], banks(0), modv[:, MODS + 5:MODS + 6], None, ALU.mult).then_inc(S["ydT_copied"], 1)
                dve.wait_ge(S["yd_turned"], 1)
                dve.tensor_tensor(x[:, :, :], tiles(2), x[:, :, :], ALU.add).then_inc(S["xd_done"], 1)
                end_batch(dve, b)

        @block.scalar
        def _(act):
            act.wait_ge(G["modw_in"], 32)
            act.activation(cs[:, :, :], cT[:, :, :], ACT.Silu).then_inc(G["c_silu"], 1)
            act.wait_ge(G["weights_in"], 16 * NLOAD)

            def hT_half(tag, bank, scale, bias):
                act.wait_ge(S["vec_copied"], 1)
                act.wait_ge(S["turned"], NHALF * TR_TAGS.index(tag) + 2)
                act.activation(half(hT, 1), P[:, bank + 1, :], ACT.Identity, bias=bias, scale=scale).then_inc(S["hT_act"], 1)

            act.wait_ge(G["set_done"], NSET)
            act.wait_ge(G["pool_set"], NPOOL)
            end_batch(act, -1)
            with act.Fori(0, B) as b:
                hT_half("a1", 0, vecs[:, 0:1], vecs[:, 1:2])
                act.wait_ge(S["k0_min"], 1)
                act.activation(A[:, 3, :], A[:, 2, :], ACT.Exp).then_inc(S["k0_exp"], 1)
                act.wait_ge(S["q0_min"], 1)
                act.activation(A[:, 1, :], A[:, 0, :], ACT.Exp).then_inc(S["q0_exp"], 1)
                act.wait_ge(S["o0_turned"], 2)
                act.activation(half(A[:, 7, :], 1), P[:, 7, :], ACT.Copy).then_inc(S["o0_done_a"], 1)
                hT_half("a2", 0, vecs[:, 2:3], vecs[:, 3:4])
                for u in range(FC * NHALF):
                    c, i = u // NHALF, u % NHALF
                    act.wait_ge(S["fc1_mm"], u + 1)
                    act.activation(half(A[:, c, :], i), P[:, 2 + u % 2, :], ACT.Gelu, bias=vecs[:, 4 + c:5 + c]).then_inc(S["fc1_act"], 1)
                hT_half("b0", 6, modv[:, 4:5], modv[:, 3:4])
                act.wait_ge(S["rb_sub"], 1)
                act.activation(rexp[:, :, 0:E0], rlog[:, :, 0:E0], ACT.Exp).then_inc(S["rb_exp"], 1)
                for u in range(CH0 * NHALF):
                    act.wait_ge(S["up_mm"], u + 1)
                    if u >= 4:
                        if u - 4 < NHALF:
                            act.wait_ge(S["downb_mm"], u - 4 + 1)
                        else:
                            act.wait_ge(S["up_gated"], u - 4 - NHALF + 1)
                    act.activation(A[:, (u % 4) // 2, (u % 2) * HALF:(u % 2 + 1) * HALF], P[:, 2 + u % 3, :], ACT.Gelu).then_inc(S["up_act"], 1)
                hT_half("c1", 6, vecs[:, 4 + FC:5 + FC], vecs[:, 5 + FC:6 + FC])

                def values(s, n):
                    act.wait_ge(S["st_mm"], ST_AT if isinstance(n, int) and n == 0 else T * (n - 1) + ST_AT)
                    act.wait_ge(S["v_mm"], n + 1)
                    act.wait_ge(S["pv_done"], PV_AT if isinstance(n, int) and n == 0 else T * (n - 1) + PV_AT)
                    act.activation(Vh[s][:, :, 64 * s:64 * s + 64], vpsum, ACT.Copy).then_inc(S["v_high"], 1)

                def high_parts(s, n):
                    act.wait_ge(S["qk_mm"], n + 1)
                    act.activation(Qa[s][0:64, :], banks(6, 2, slice(0, 64)), ACT.Copy).then_inc(S["q_hi"], 1)
                    act.activation(Ka[s][0:64, :], banks(6, 2, slice(64, 128)), ACT.Copy).then_inc(S["k_hi"], 1)

                def maxima(s, n):
                    act.wait_ge(S["m_row"], n + 1)
                    act.activation(Qa[s][MROW:MROW + 2, :], banks(6, 2, slice(0, 2)), ACT.Copy).then_inc(S["m_in"], 1)

                def exps(k, j, between=None):
                    act.wait_ge(S["st_mm"], k + 1 + ST_AT)
                    act.wait_ge(S["p_low"], k - 1 + PLOW_AT if not (isinstance(k, int) and k == 0) else PLOW_AT)
                    act.activation(pfull[:, j % 2, :], banks(2 * (j % 2)), ACT.Exp, scale=DH1 ** -0.5).then_inc(S["exp_done"], 1)
                    if between:
                        between()
                    if j % T >= DHIGH:
                        act.wait_ge(S["pv_done"], k + 1 - RING + PV_AT)
                        act.wait_ge(S["exp_done"], k + 1 + EXP_AT)
                        act.activation(phigh[j % RING], pfull[:, j % 2, :], ACT.Copy).then_inc(S["p_high"], 1)

                def outputs(s, p):
                    act.wait_ge(S["pv_done"], (2 * p + s + 1) * T + PV_AT)
                    act.wait_ge(S["o_norm"], p * NSCALE + NORM_AT)
                    act.activation(opair[64 * s:64 * s + 64, :], banks(4, 2, slice(64 * s, 64 * s + 64)), ACT.Copy).then_inc(S["o_copied"], 1)

                def pair(p, is_last):
                    for j in range(2 * T):
                        s, n = j // T, 2 * p + 1 + j // T
                        ahead = not (is_last and s == 1)
                        if ahead and j % T == T - 1:
                            maxima(1 - s, n)
                        if is_last and j == 2 * T - 1:
                            outputs(s, p)
                        elif j % T == T - 1:
                            exps(2 * T * p + j + 1, j + 1, lambda s=s: outputs(s, p))
                        elif j % T == 0 and ahead:
                            exps(2 * T * p + j + 1, j + 1, lambda s=s, n=n: values(1 - s, n))
                        elif j % T == 1 and ahead:
                            exps(2 * T * p + j + 1, j + 1, lambda s=s, n=n: high_parts(1 - s, n))
                        else:
                            exps(2 * T * p + j + 1, j + 1)

                act.sem_inc(S["exp_done"], EXP_AT)
                act.sem_inc(S["o_copied"], COPIED_AT)
                act.wait_ge(S["hT_act"], TR_TAGS.index("c1") + 1)
                values(0, 0)
                high_parts(0, 0)
                maxima(0, 0)
                exps(0, 0)
                with act.Fori(0, PAIRS - 1) as p:
                    pair(p, False)
                pair(PAIRS - 1, True)

                hT_half("d0", 6, modv[:, MODS + 4:MODS + 5], modv[:, MODS + 3:MODS + 4])
                act.wait_ge(S["rd_sub"], 1)
                act.activation(rexp[:, :, 0:E1], rlog[:, :, 0:E1], ACT.Exp).then_inc(S["rd_exp"], 1)
                act.wait_ge(S["hT_dve"], len(TR_TAGS))
                act.wait_ge(S["hT_act"], len(TR_TAGS))
                act.activation(hTh[:, :], hT[:, :], ACT.Copy).then_inc(S["hT_high"], 1)

                def high_weights(n, q, m, loads):
                    act.wait_ge(S[f"w1_in{q}"], loads)
                    cols = slice(m * F1, (m + 1) * F1)
                    act.activation(wh[q][:, cols], wex[q][:, cols], ACT.Copy).then_inc(S["w_high"], 1)

                def gates(n, q):
                    for i in range(NHALF):
                        act.wait_ge(S["bcd_mm"], n * NHALF + i + 1)
                        act.activation(half(gatesb[q], i), P[:, 6 + i, :], ACT.Copy).then_inc(S["gates_in"], 1)

                def high_unit(c, i):
                    act.wait_ge(S["gu_done"], c + 1 + UNIT_AT)
                    act.wait_ge(S["downd_mm"], c - 1 + UNIT_AT)
                    act.activation(half(guh, i), half(gu, i), ACT.Copy).then_inc(S["gu_high"], 1)

                def expert(n, q, loads):
                    for u in range(UNITS):
                        c, i = n * UNITS + u, u % 2
                        act.wait_ge(S["w1_mm"], c + 1)
                        act.wait_ge(S["silu_gated"], c - 1 + UNIT_AT)
                        act.activation(half(silu, i), P[:, 2 + i, :], ACT.Silu).then_inc(S["silu_done"], 1)
                        if NEXT <= u < NEXT + 3:
                            high_weights(n + 1, 1 - q, u - NEXT, loads)
                        if not (isinstance(c, int) and c == 0):
                            high_unit(c - 1, 1 - i)
                        if u == UNITS - 2:
                            gates(n + 1, 1 - q)

                for m in range(3):
                    high_weights(0, 0, m, 16)
                gates(0, 0)
                act.sem_inc(S["silu_done"], UNIT_AT)
                expert(0, 0, 16)
                with act.Fori(0, (EX1 - 1) // 2) as r:
                    expert(2 * r + 1, 1, 16 * r + 32)
                    expert(2 * r + 2, 0, 16 * r + 32)
                high_unit(EX1 * UNITS - 1, 1)
                end_batch(act, b)

        @block.tensor
        def _(pe):
            pe.wait_ge(G["modw_in"], 32)
            wmod = modb[:, :, :].rearrange("p a b -> p (a b)")
            pe.wait_ge(G["c_silu"], 1)
            for i, l in ((0, 0), (1, 0), (1, 1), (2, 1)):
                lo, hi = max(i * HALF, l * MODS * D), min((i + 1) * HALF, (l + 1) * MODS * D)
                mm = pe.matmul(P[0:B, i, lo - i * HALF:hi - i * HALF], cs[:, l, :], wmod[:, lo:hi], start=True, stop=True)
            mm.then_inc(G["mod_mm"], 1)
            for m in range(2 * MODS):
                mm = pe.matmul(P[:, 3, m * B:(m + 1) * B], wmod[:, m * D:(m + 1) * D], cs[:, m // MODS, :], start=True, stop=True)
            mm.then_inc(G["modT_mm"], 1)
            pe.wait_ge(G["modT_copied"], 7)
            pe.wait_ge(G["mod_one"], 1)
            pe.wait_ge(G["set_done"], NSET)
            pe.wait_ge(G["pool_set"], NPOOL)

            def turn(tag, bank):
                for t in range(T):
                    if tag in LN_TAGS:
                        pe.wait_ge(S["ln_norm"], LN_TAGS.index(tag) * T + t + 1)
                    tr = pe.transpose(bank_t(bank, t), xn[:, t, :], identf[:, :])
                    if t % TPH == TPH - 1:
                        tr.then_inc(S["turned"], 1)
                pe.wait_ge(S["hT_dve"], TR_TAGS.index(tag) + 1)
                pe.wait_ge(S["hT_act"], TR_TAGS.index(tag) + 1)

            def tile(t_, t):
                return t_[:, t * 128:(t + 1) * 128]

            def route(tag, n, w, bank):
                for t in range(T):
                    mm = pe.matmul(P[:, bank, t * n:(t + 1) * n], tile(hT, t), w, start=True, stop=True)
                mm.then_inc(S[f"{tag}_mm"], 1)

            def turn_gates(tag, bank):
                pe.wait_ge(S[f"{tag}_lo"], 1)
                rows = P[0:3 * GW, bank, :].bitcast(BF16)
                for t in range(T):
                    tr = pe.transpose(rows[:, t * 128:(t + 1) * 128], gparts[:, t, :], identb[:, :])
                tr.then_inc(S[f"{tag}_turned"], 1)

            def zero(bank):
                pe.matmul(P[:, bank, :], zerob[:, 0:128], zerob[:, :], start=True, stop=False)

            def close(bank):
                return pe.matmul(P[:, bank, :], zerob[:, 0:128], zerob[:, :], start=False, stop=True)

            pe.wait_ge(G["weights_in"], 16 * NLOAD)
            end_batch(pe, -1)
            with pe.Fori(0, B) as b:
                turn("a1", 0)
                for t in range(T):
                    pe.matmul(P[:, 2 + t // 2, (t % 2) * 2 * D:(t % 2 + 1) * 2 * D], tile(hT, t), wqkv0[:, D:3 * D],
                              start=True, stop=True).then_inc(S["k0_mm"], 1)
                for i in range(NHALF):
                    pe.matmul(P[:, i, :], wqkv0[:, 0:D], half(hT, i), start=True, stop=True).then_inc(S["q0_mm"], 1)
                pe.wait_ge(S["v0_copied"], 1)
                pe.wait_ge(S["k0_done"], 1)
                for t in range(T):
                    mm = pe.matmul(P[:, 7, 0:1], tile(A[:, 2, :], t), onecol[:, :], start=(t == 0), stop=(t == T - 1))
                mm.then_inc(S["ks_mm"], 1)
                for t in range(T):
                    mm = pe.matmul(P[:, 6, 0:D], tile(A[:, 2, :], t), tile(A[:, 4, :], t), start=(t == 0), stop=(t == T - 1))
                mm.then_inc(S["kv_mm"], 1)
                pe.wait_ge(S["q0_done"], 1)
                pe.wait_ge(S["ks_masked"], 1)
                for t in range(T):
                    mm = pe.matmul(P[:, 2, t * H0:(t + 1) * H0], tile(A[:, 0, :], t), small[:, 1, 0:H0], start=True, stop=True)
                mm.then_inc(S["den_mm"], 1)
                pe.wait_ge(S["kv_masked"], 1)
                for t in range(T):
                    pe.matmul(bank_t(0, t), tile(A[:, 0, :], t), small[:, 0, :], start=True, stop=True).then_inc(S["num_mm"], 1)
                for i in range(NHALF):
                    pe.wait_ge(S["o0_tok"], i + 1)
                    for t in range(i * TPH, (i + 1) * TPH):
                        tr = pe.transpose(bank_t(6, t), tile(A[:, 5, :], t), identf[:, :])
                    tr.then_inc(S["o0_turned"], 1)
                for t in range(T):
                    pe.wait_ge(S["o0_done" if t < TPH else "o0_done_a"], 1)
                    pe.matmul(bank_t(4, t), tile(A[:, 7, :], t), wproj[:, :], start=True, stop=True).then_inc(S["proj_mm"], 1)
                turn("a2", 0)
                for u in range(FC * NHALF):
                    c, i = u // NHALF, u % NHALF
                    if u >= 2:
                        pe.wait_ge(S["fc1_act"], u - 1)
                    pe.matmul(P[:, 2 + u % 2, :], wfc1[:, c * 128:(c + 1) * 128], half(hT, i), start=True, stop=True).then_inc(S["fc1_mm"], 1)
                pe.wait_ge(S["fc1_act"], FC * NHALF)
                pe.wait_ge(S["wfc2_scaled"], 1)
                for t in range(T):
                    for c in range(FC):
                        mm = pe.matmul(bank_t(4, t), tile(A[:, c, :], t), wfc2s[:, c, :], start=(c == 0), stop=(c == FC - 1))
                    mm.then_inc(S["fc2_mm"], 1)

                turn("b0", 6)
                route("rb", E0, wrout[:, :], 7)
                zero(0)
                zero(1)
                pe.wait_ge(S["wdown_scaled"], 1)

                def up(u):
                    if u >= 3:
                        pe.wait_ge(S["up_act"], u - 2)
                    pe.matmul(P[:, 2 + u % 3, :], wup[:, u // NHALF, :], half(hT, u % 2), start=True, stop=True).then_inc(S["up_mm"], 1)

                def spread(u):
                    if u - NHALF >= 2:
                        pe.wait_ge(S["up_gated"], u - NHALF - 1)
                    pe.matmul(P[:, 5 + u % 2, :], selb[:, u // NHALF - 1, :], half(grows, u % 2), start=True, stop=True).then_inc(S["bcb_mm"], 1)

                def down(u):
                    if u < NHALF:
                        pe.wait_ge(S["up_act"], u + 1)
                    else:
                        pe.wait_ge(S["up_gated"], u - NHALF + 1)
                    f = A[:, (0 if u < NHALF else 2) + (u % 4) // 2, (u % 2) * HALF:(u % 2 + 1) * HALF]
                    for t in range(TPH):
                        mm = pe.matmul(bank_t(0, u % 2 * TPH + t), tile(f, t), wdowns[:, u // NHALF, :],
                                       start=False, stop=False)
                    mm.then_inc(S["downb_mm"], 1)

                up(0)
                up(1)
                down(0)
                up(2)
                down(1)
                turn_gates("rb", 7)
                pe.wait_ge(S["rb_rows"], 1)
                spread(2)
                for u in range(2, CH0 * NHALF):
                    if u + 1 < CH0 * NHALF:
                        up(u + 1)
                        spread(u + 1)
                    down(u)
                    if u == CH0 * NHALF - 2:
                        close(0).then_inc(S["downb_end"], 1)
                close(1).then_inc(S["downb_end"], 1)

                turn("c1", 6)

                def project_v(s, n):
                    pe.wait_ge(S[f"wh_in{s}"], 8 * (n - s) + 16)
                    if not isinstance(n, int) or n > 0:
                        pe.wait_ge(S["m_in"], n)
                    for t in range(T):
                        mm = pe.matmul(P[:, 6, t * DH1:(t + 1) * DH1], tile(hT, t), whead[s][:, 2 * DH1:3 * DH1], start=True, stop=True)
                    mm.then_inc(S["v_mm"], 1)

                def project_qk(s, n):
                    pe.wait_ge(S["v_low"], n + 1)
                    for i in range(NHALF):
                        mm = pe.matmul(P[:, 6 + i, :], whead[s][:, 0:2 * DH1], half(hT, i), start=True, stop=True)
                    mm.then_inc(S["qk_mm"], 1)

                def near(out, n, parts, stop):
                    for part in range(parts):
                        mm = pe.matmul(out, distb[:, :], diagb[:, 3 * n + part, :], start=False, stop=(stop and part == parts - 1))
                    return mm

                def max_tile(s, n, t):
                    if t == 0:
                        pe.wait_ge(S["k_aux"], n + 1)
                        pe.wait_ge(S["k_lo"], n + 1)
                    for i in range(NHALF):
                        if t > 0:
                            pe.wait_ge(S["max_red"], (n * T + t) * NHALF + i - 1)
                        mine = i == t // TPH
                        mm = pe.matmul(P[:, 6 + i, :], tile(Qa[s][0:MROW, :], t), half(Ka[s][0:MROW, :], i), start=True, stop=not mine)
                        if mine:
                            mm = near(P[:, 6 + i, (t % TPH) * 128:(t % TPH + 1) * 128], n, 1, True)
                        mm.then_inc(S["max_mm"], 1)

                def turn_max(n):
                    pe.wait_ge(S["m_mid"], n + 1)
                    for t in range(T):
                        mm = pe.matmul(P[0:2, 6 + t // TPH, (t % TPH) * 128:(t % TPH + 1) * 128], mparts[:, t, :], identb[:, :], start=True, stop=True)
                    mm.then_inc(S["m_row"], 1)

                def scores(k, j, s, n):
                    if j == 0:
                        pe.wait_ge(S["m_in"], n + 1)
                        pe.wait_ge(S["k_dup"], n + 1)
                    if not isinstance(k, int) or k > 0:
                        pe.wait_ge(S["exp_done"], k - 1 + EXP_AT)
                    bank = 2 * (j % 2)
                    for i in (1 - j // TPH, j // TPH):
                        pe.matmul(P[:, bank + i, :], tile(Ka[s][0:KEXACT, :], j), half(Qa[s][0:KEXACT, :], i), start=True, stop=False)
                        if i == j // TPH:
                            near(P[:, bank + i, (j % TPH) * 128:(j % TPH + 1) * 128], n, 3, False)
                        mm = pe.matmul(P[:, bank + i, :], tile(Kb[s], j), half(Qb[s], i), start=False, stop=True)
                    mm.then_inc(S["st_mm"], 1)

                def weigh_high(k, j, s, n):
                    wait_high(pe, n, j)
                    if j == 0:
                        pe.wait_ge(S["v_low"], n + 1)
                        pe.wait_ge(S["o_copied"], n + COPIED_AT)
                        pe.wait_ge(S["s_copied"], n + COPIED_AT)
                    for v, starts in ((Vh[s], j == 0), (Vl[s], False)):
                        for i in range(NHALF):
                            pe.matmul(P[:, 4 + i, :], v[:, j, :], half(phigh[j % RING], i), start=starts, stop=False)

                def weigh_low(k, j, s):
                    pe.wait_ge(S["p_low"], k + 1 + PLOW_AT)
                    for i in range(NHALF):
                        mm = pe.matmul(P[:, 4 + i, :], Vh[s][:, j, :], half(plow[j % 2], i), start=False, stop=(j == T - 1))
                    mm.then_inc(S["pv_done"], 1)

                def pair(p, is_last):
                    for j in range(2 * T):
                        k, s, jj = 2 * T * p + j, j // T, j % T
                        n = 2 * p + s
                        ahead = not (is_last and s == 1)
                        before, after = MAX_TILES[jj]
                        if ahead:
                            for t in before:
                                max_tile(1 - s, n + 1, t)
                        if jj < T - 1:
                            scores(k + 1, jj + 1, s, n)
                        if ahead and jj == 0:
                            project_v(1 - s, n + 1)
                        if ahead and jj == 1:
                            project_qk(1 - s, n + 1)
                        if ahead:
                            for t in after:
                                max_tile(1 - s, n + 1, t)
                        if ahead and jj == T - 1:
                            turn_max(n + 1)
                        weigh_high(k, jj, s, n)
                        if jj > 0:
                            weigh_low(k - 1, jj - 1, s)
                        if ahead and jj == T - 1:
                            scores(k + 1, 0, 1 - s, n + 1)
                        if jj == T - 1:
                            weigh_low(k, jj, s)

                pe.sem_inc(S["st_mm"], ST_AT)
                pe.sem_inc(S["pv_done"], PV_AT)
                project_v(0, 0)
                project_qk(0, 0)
                for t in range(T):
                    max_tile(0, 0, t)
                turn_max(0)
                scores(0, 0, 0, 0)
                with pe.Fori(0, PAIRS - 1) as p:
                    pair(p, False)
                pair(PAIRS - 1, True)

                pe.wait_ge(S["wo_scaled"], 1)
                for t in range(T):
                    pe.wait_ge(S["o_norm"], (PAIRS - 1) * NSCALE + t * NSCALE // T + 1 + NORM_AT)
                    for c in range(PAIRS):
                        mm = pe.matmul(bank_t(0, t), tile(A[:, c, :], t), wos[:, c, :], start=(c == 0), stop=(c == PAIRS - 1))
                    mm.then_inc(S["o1_mm"], 1)

                turn("d0", 6)
                route("rd", E1, wgate[:, :], 2)
                zero(0)
                zero(1)
                turn_gates("rd", 3)
                pe.wait_ge(S["rd_rows"], 1)

                def spread_gate(n):
                    for i in range(NHALF):
                        if not isinstance(n, int) or n > 0:
                            pe.wait_ge(S["gates_in"], n * NHALF - NHALF + i + 1)
                        pe.matmul(P[:, 6 + i, :], seld[:, n, :], half(grows, i), start=True, stop=True).then_inc(S["bcd_mm"], 1)

                def parts(out, q, lo, high, low, starts, stops):
                    cols = slice(lo, lo + 128)
                    pe.matmul(out, wh[q][:, cols], high, start=starts, stop=False)
                    pe.matmul(out, wl[q][:, cols], high, start=False, stop=False)
                    return pe.matmul(out, wh[q][:, cols], low, start=False, stop=stops)

                def down_unit(c, q, u):
                    i = u % 2
                    pe.wait_ge(S["gu_low"], c + 1 + UNIT_AT)
                    parts(P[:, i, :], q, 2 * F1 + u // NHALF * 128, half(guh, i), half(gul, i), False, False).then_inc(S["downd_mm"], 1)

                def expert(n, q):
                    pe.wait_ge(S["w_low"], 3 * n + 3)
                    for u in range(UNITS):
                        c, f, i = n * UNITS + u, u // NHALF * 128, u % 2
                        pe.wait_ge(S["silu_done"], c - 1 + UNIT_AT)
                        parts(P[:, 2 + i, :], q, f, half(hTh, i), half(hTl, i), True, True).then_inc(S["w1_mm"], 1)
                        pe.wait_ge(S["gu_done"], c - 1 + UNIT_AT)
                        parts(P[:, 4 + i, :], q, F1 + f, half(hTh, i), half(hTl, i), True, True).then_inc(S["w3_mm"], 1)
                        if u >= 2:
                            down_unit(c - 2, q, u - 2)
                        elif not isinstance(n, int):
                            down_unit(c - 2, 1 - q, UNITS - 2 + u)
                        if u == NEXT:
                            spread_gate(n + 1)

                pe.sem_inc(S["downd_mm"], UNIT_AT)
                spread_gate(0)
                pe.wait_ge(S["hT_low"], 1)
                expert(0, 0)
                with pe.Fori(0, (EX1 - 1) // 2) as r:
                    expert(2 * r + 1, 1)
                    expert(2 * r + 2, 0)
                down_unit(EX1 * UNITS - 2, 0, UNITS - 2)
                down_unit(EX1 * UNITS - 1, 0, UNITS - 1)
                close(0).then_inc(S["downd_end"], 1)
                close(1).then_inc(S["downd_end"], 1)
                pe.wait_ge(S["ydT_copied"], 1)
                for t in range(T):
                    tr = pe.transpose(bank_t(2, t), tile(A[:, 3, :], t), identf[:, :])
                tr.then_inc(S["yd_turned"], 1)
                end_batch(pe, b)


def kernel(**inputs):
    import concourse.bacc as bacc
    from concourse.bass_utils import run_bass_kernel_spmd as run

    g = {k: np.asarray(v) for k, v in inputs.items()}
    consts, aux = constants()
    flat = lambda w: np.ascontiguousarray(w)
    per_chunk = lambda w: flat(w.reshape(-1, 128, w.shape[-1]).transpose(1, 0, 2))

    def heads(w):
        return w.reshape(D, H1, DH1).transpose(1, 0, 2)

    shared_w1, shared_w3 = (g[n].transpose(1, 0, 2).reshape(D, F1) for n in ("L1_ffn_w1_s", "L1_ffn_w3_s"))
    w1 = np.concatenate([g["L1_ffn_w1_e"], shared_w1[None]])
    w3 = np.concatenate([g["L1_ffn_w3_e"], shared_w3[None]])
    w2 = np.concatenate([g["L1_ffn_w2_e"], g["L1_ffn_w2_s"].reshape(1, F1, D)])
    w2 = w2.reshape(EX1, FCH, 128, D).transpose(0, 2, 1, 3).reshape(EX1, 128, F1)
    up = np.concatenate([g["L0_ffn_shared_up"], g["L0_ffn_routed_up"]]).reshape(CH0, 128, D)
    down = np.concatenate([g["L0_ffn_shared_down"], g["L0_ffn_routed_down"]]).transpose(0, 2, 1).reshape(CH0, 128, D)
    arrays = {
        "x": flat(g["L0_attn_x"].reshape(B, T, 128, D).transpose(0, 2, 1, 3)),
        "consts": consts, "aux": aux,
        "wqkv0": flat(g["L0_attn_qkv_w"].T), "wproj": flat(g["L0_attn_proj_w"].T),
        "wfc1": flat(g["L0_attn_fc1_w"].T), "wfc2": per_chunk(g["L0_attn_fc2_w"].T),
        "wup": flat(up.transpose(2, 0, 1)), "wdown": flat(down.transpose(1, 0, 2)),
        "wrout": flat(g["L0_ffn_router_w"].T), "wgate": flat(g["L1_ffn_gate_W"].T),
        "wo": per_chunk(g["L1_attn_Wo"]),
        "vecs": flat(np.stack([g["L0_attn_norm1_g"], g["L0_attn_norm1_b"], g["L0_attn_norm2_g"], g["L0_attn_norm2_b"],
                               *g["L0_attn_fc1_b"].reshape(FC, 128), g["L1_attn_ln_gamma"], g["L1_attn_ln_beta"]], axis=1)),
        "biases": flat(np.stack([g["L0_attn_proj_b"], g["L0_attn_fc2_b"]])),
        "wmod": flat(np.concatenate([g["L0_wmod"], g["L1_wmod"]], axis=1)),
        "cT": flat(np.stack([g["L0_c"].T, g["L1_c"].T], axis=1)),
        "whead": flat(np.concatenate([heads(g["L1_attn_Wq"]), heads(g["L1_attn_Wk"]), heads(g["L1_attn_Wv"])], axis=2)),
        "wex": flat(np.concatenate([w1, w3, w2], axis=2)),
    }
    nc = bacc.Bacc("TRN2", target_bir_lowering=False, num_devices=1)
    a = {n: nc.dram_tensor(f"in_{n}", v.shape, F32, kind="ExternalInput").ap() for n, v in arrays.items()}
    a["out"] = nc.dram_tensor("out_x", [B, 128, T, D], F32, kind="ExternalOutput").ap()
    a["modrows"] = nc.dram_tensor("modrows", [B, 2 * MODS * D], F32).ap()
    network(nc, a)
    r = run(nc, [{f"in_{n}": v for n, v in arrays.items()}], core_ids=[0])
    return r.results[0]["out_x"].transpose(0, 2, 1, 3).reshape(B, N, D)
```
